# Optimizing a Trainium2 kernel written in Bass

```python
import numpy as np
import jax
import jax.numpy as jnp

def _softmax(x, axis=-1):
    return jax.nn.softmax(x, axis=axis)

def _gelu(x):
    return jax.nn.gelu(x, approximate=True)

def _silu(x):
    return jax.nn.silu(x)

def _sigmoid(x):
    return jax.nn.sigmoid(x)

def _layernorm(x, axis=-1, eps=1e-05):
    m = jnp.mean(x, axis=axis, keepdims=True)
    v = jnp.var(x, axis=axis, keepdims=True)
    return (x - m) / jnp.sqrt(v + eps)

def _scatter_add(tgt, idx, src, axis=0):
    return tgt.at[idx].add(src)

def _segment_sum(src, seg, n):
    return jax.ops.segment_sum(src, seg, n)
kernel_name = 'mk_gnn_preln_d4_gnn_r32_793d81'

def setup_inputs(seed: int=0):
    np.random.seed(seed)
    _w = jnp.asarray

    def _rec_inputs():
        import jax
        import jax.numpy as jnp
        _gk = jax.random.key(seed)
        x = -0.000202 + 1 * jax.random.normal(jax.random.fold_in(_gk, 1), (50000, 128), jnp.float32)
        src = jax.random.randint(jax.random.fold_in(_gk, 2), (25000,), 0, 50000, jnp.int32)
        dst = jax.random.randint(jax.random.fold_in(_gk, 3), (25000,), 0, 50000, jnp.int32)
        _o = jnp.argsort(dst, stable=True)
        src = src[_o]
        dst = dst[_o]
        edge_attr_4 = 0.000714719 + 1.00021 * jax.random.normal(jax.random.fold_in(_gk, 11), (25000, 4), jnp.float32)
        edge_weight = jax.random.uniform(jax.random.fold_in(_gk, 13), (25000,), jnp.float32, 0.0, 0.999999)
        return (x, src, dst, edge_attr_4, edge_weight)
    x, src, dst, edge_attr_4, edge_weight = _rec_inputs()

    def _L0_gnn_setup():
        import jax, jax.numpy as jnp
        import numpy as np
        N_NODES = 50000
        N_EDGES = 50000
        D = 128
        N_LAYERS = 2
        NEG_SLOPE = 0.2

        def _gcn_layer(x, src, dst, ew, Ws, bs, Wn, bn, bias):
            n = x.shape[0]
            msg = x[src] * ew[:, None]
            agg = jax.ops.segment_sum(msg, dst, num_segments=n)
            agg = agg + x
            cnt = jax.ops.segment_sum(jnp.ones_like(ew), dst, num_segments=n) + 1.0
            neigh = agg / cnt[:, None]
            out = x @ Ws.T + bs + neigh @ Wn.T + bn + bias
            return jnp.where(out > 0, out, NEG_SLOPE * out)
        key = jax.random.key(seed)
        ks = jax.random.split(key, 10)
        user_embeddings = jax.random.normal(ks[0], (N_NODES, D), dtype=jnp.float32)
        social_edge_index = jax.random.randint(ks[1], (2, N_EDGES), 0, N_NODES, dtype=jnp.int64)
        social_edge_weights = jax.random.uniform(ks[2], (N_EDGES,), dtype=jnp.float32)
        s = 1.0 / np.sqrt(D)
        W_self = jax.random.uniform(ks[3], (N_LAYERS, D, D), minval=-s, maxval=s, dtype=jnp.float32)
        b_self = jax.random.uniform(ks[4], (N_LAYERS, D), minval=-s, maxval=s, dtype=jnp.float32)
        W_neigh = jax.random.uniform(ks[5], (N_LAYERS, D, D), minval=-s, maxval=s, dtype=jnp.float32)
        b_neigh = jax.random.uniform(ks[6], (N_LAYERS, D), minval=-s, maxval=s, dtype=jnp.float32)
        layer_bias = jnp.zeros((N_LAYERS, D), dtype=jnp.float32)
        W_agg = jax.random.uniform(ks[7], (D, D), minval=-s, maxval=s, dtype=jnp.float32)
        b_agg = jax.random.uniform(ks[8], (D,), minval=-s, maxval=s, dtype=jnp.float32)
        return {'user_embeddings': user_embeddings, 'social_edge_index': social_edge_index, 'social_edge_weights': social_edge_weights, 'W_self': W_self, 'b_self': b_self, 'W_neigh': W_neigh, 'b_neigh': b_neigh, 'layer_bias': layer_bias, 'W_agg': W_agg, 'b_agg': b_agg}
    _L0_gnn_all = _L0_gnn_setup()
    _L0_gnn_in = {k: v for k, v in _L0_gnn_all.items() if k in ('W_self', 'b_self', 'W_neigh', 'b_neigh', 'layer_bias', 'W_agg', 'b_agg')}
    del _L0_gnn_all

    def _L1_gnn_setup():
        import jax, jax.numpy as jnp
        import numpy as np
        NUM_NODES = 1250
        NUM_EDGES = 20000
        DIM = 128
        key = jax.random.key(seed)
        k1, k2, k3, k4 = jax.random.split(key, 4)
        x = jax.random.normal(k1, (NUM_NODES, DIM), dtype=jnp.float32)
        edge_index = jax.random.randint(k2, (2, NUM_EDGES), 0, NUM_NODES, dtype=jnp.int64)
        W = jax.random.normal(k3, (DIM, DIM), dtype=jnp.float32) * (1.0 / np.sqrt(DIM))
        b = jax.random.normal(k4, (DIM,), dtype=jnp.float32) * (1.0 / np.sqrt(DIM))
        return {'x': x, 'edge_index': edge_index, 'W': W, 'b': b}
    _L1_gnn_all = _L1_gnn_setup()
    _L1_gnn_in = {k: v for k, v in _L1_gnn_all.items() if k in ('W', 'b')}
    del _L1_gnn_all

    def _L2_gnn_setup():
        import jax, jax.numpy as jnp
        import numpy as np
        N, H, E, DE = (50000, 128, 25000, 4)
        key = jax.random.key(seed)
        ks = jax.random.split(key, 16)

        def dense(k, din, dout):
            kw, kb = jax.random.split(k)
            W = jax.random.normal(kw, (din, dout), jnp.float32) / jnp.sqrt(jnp.float32(din))
            b = jnp.zeros((dout,), jnp.float32)
            return (W, b)
        node_feats = jax.random.normal(ks[0], (N, H), jnp.float32)
        edge_index = jax.random.randint(ks[1], (2, E), 0, N, jnp.int32)
        edge_feats = jax.random.normal(ks[2], (E, DE), jnp.float32)
        W_msg1, b_msg1 = dense(ks[3], 2 * H + DE, H)
        W_msg2, b_msg2 = dense(ks[4], H, H)
        W_z, b_z = dense(ks[5], 2 * H, H)
        W_r, b_r = dense(ks[6], 2 * H, H)
        W_h, b_h = dense(ks[7], 2 * H, H)
        return {'node_feats': node_feats, 'edge_index': edge_index, 'edge_feats': edge_feats, 'W_msg1': W_msg1, 'b_msg1': b_msg1, 'W_msg2': W_msg2, 'b_msg2': b_msg2, 'W_z': W_z, 'b_z': b_z, 'W_r': W_r, 'b_r': b_r, 'W_h': W_h, 'b_h': b_h}
    _L2_gnn_all = _L2_gnn_setup()
    _L2_gnn_in = {k: v for k, v in _L2_gnn_all.items() if k in ('W_msg1', 'b_msg1', 'W_msg2', 'b_msg2', 'W_z', 'b_z', 'W_r', 'b_r', 'W_h', 'b_h')}
    del _L2_gnn_all

    def _L3_gnn_setup():
        import jax, jax.numpy as jnp
        import numpy as np
        N_NODES = 50000
        N_EDGES = 18750
        D_IN = 128
        D_OUT = 128
        key = jax.random.key(seed)
        k1, k2, k3, k4 = jax.random.split(key, 4)
        x = jax.random.normal(k1, (N_NODES, D_IN), dtype=jnp.float32)
        edge_index = jax.random.randint(k2, (2, N_EDGES), 0, N_NODES, dtype=jnp.int64)
        W = jax.random.normal(k3, (D_IN, D_OUT), dtype=jnp.float32) * (1.0 / np.sqrt(D_IN))
        a = jax.random.normal(k4, (2 * D_OUT,), dtype=jnp.float32) * (1.0 / np.sqrt(2 * D_OUT))
        return {'x': x, 'edge_index': edge_index, 'W': W, 'a': a}
    _L3_gnn_all = _L3_gnn_setup()
    _L3_gnn_in = {k: v for k, v in _L3_gnn_all.items() if k in ('W', 'a')}
    del _L3_gnn_all
    return {'x': x, 'src': src, 'dst': dst, 'edge_attr_4': edge_attr_4, 'edge_weight': edge_weight, 'L0_gnn_W_self': _L0_gnn_in['W_self'], 'L0_gnn_b_self': _L0_gnn_in['b_self'], 'L0_gnn_W_neigh': _L0_gnn_in['W_neigh'], 'L0_gnn_b_neigh': _L0_gnn_in['b_neigh'], 'L0_gnn_layer_bias': _L0_gnn_in['layer_bias'], 'L0_gnn_W_agg': _L0_gnn_in['W_agg'], 'L0_gnn_b_agg': _L0_gnn_in['b_agg'], 'L1_gnn_W': _L1_gnn_in['W'], 'L1_gnn_b': _L1_gnn_in['b'], 'L2_gnn_W_msg1': _L2_gnn_in['W_msg1'], 'L2_gnn_b_msg1': _L2_gnn_in['b_msg1'], 'L2_gnn_W_msg2': _L2_gnn_in['W_msg2'], 'L2_gnn_b_msg2': _L2_gnn_in['b_msg2'], 'L2_gnn_W_z': _L2_gnn_in['W_z'], 'L2_gnn_b_z': _L2_gnn_in['b_z'], 'L2_gnn_W_r': _L2_gnn_in['W_r'], 'L2_gnn_b_r': _L2_gnn_in['b_r'], 'L2_gnn_W_h': _L2_gnn_in['W_h'], 'L2_gnn_b_h': _L2_gnn_in['b_h'], 'L3_gnn_W': _L3_gnn_in['W'], 'L3_gnn_a': _L3_gnn_in['a']}

def reference(x, src, dst, edge_attr_4, edge_weight, L0_gnn_W_self, L0_gnn_b_self, L0_gnn_W_neigh, L0_gnn_b_neigh, L0_gnn_layer_bias, L0_gnn_W_agg, L0_gnn_b_agg, L1_gnn_W, L1_gnn_b, L2_gnn_W_msg1, L2_gnn_b_msg1, L2_gnn_W_msg2, L2_gnn_b_msg2, L2_gnn_W_z, L2_gnn_b_z, L2_gnn_W_r, L2_gnn_b_r, L2_gnn_W_h, L2_gnn_b_h, L3_gnn_W, L3_gnn_a):
    import jax
    import jax.numpy as jnp

    def _L0_gnn_ref(user_embeddings, social_edge_index, social_edge_weights, W_self, b_self, W_neigh, b_neigh, layer_bias, W_agg, b_agg):
        import jax, jax.numpy as jnp
        import numpy as np
        N_NODES = 50000
        N_EDGES = 50000
        D = 128
        N_LAYERS = 2
        NEG_SLOPE = 0.2

        def _gcn_layer(x, src, dst, ew, Ws, bs, Wn, bn, bias):
            n = x.shape[0]
            msg = x[src] * ew[:, None]
            agg = jax.ops.segment_sum(msg, dst, num_segments=n)
            agg = agg + x
            cnt = jax.ops.segment_sum(jnp.ones_like(ew), dst, num_segments=n) + 1.0
            neigh = agg / cnt[:, None]
            out = x @ Ws.T + bs + neigh @ Wn.T + bn + bias
            return jnp.where(out > 0, out, NEG_SLOPE * out)
        src = social_edge_index[0]
        dst = social_edge_index[1]
        x = user_embeddings
        for l in range(N_LAYERS):
            x = _gcn_layer(x, src, dst, social_edge_weights, W_self[l], b_self[l], W_neigh[l], b_neigh[l], layer_bias[l])
        return x @ W_agg.T + b_agg

    def _L1_gnn_ref(x, edge_index, W, b):
        import jax, jax.numpy as jnp
        import numpy as np
        NUM_NODES = 1250
        NUM_EDGES = 20000
        DIM = 128
        src, dst = (edge_index[0], edge_index[1])
        num_nodes = x.shape[0]
        messages = x[src] @ W.T + b
        out = jax.ops.segment_sum(messages, dst, num_segments=num_nodes)
        deg = jax.ops.segment_sum(jnp.ones((dst.shape[0],), dtype=x.dtype), dst, num_segments=num_nodes)
        out = out / jnp.maximum(deg, 1.0)[:, None]
        return out

    def _L2_gnn_ref(node_feats, edge_index, edge_feats, W_msg1, b_msg1, W_msg2, b_msg2, W_z, b_z, W_r, b_r, W_h, b_h):
        import jax, jax.numpy as jnp
        import numpy as np
        N, H, E, DE = (50000, 128, 25000, 4)
        n = node_feats.shape[0]
        src_idx = edge_index[0]
        dst_idx = edge_index[1]
        h_src = node_feats[src_idx]
        h_dst = node_feats[dst_idx]
        msg_input = jnp.concatenate([h_src, h_dst, edge_feats], axis=-1)
        messages = jax.nn.relu(msg_input @ W_msg1 + b_msg1)
        messages = messages @ W_msg2 + b_msg2
        agg = jax.ops.segment_sum(messages, dst_idx, num_segments=n)
        hx = jnp.concatenate([node_feats, agg], axis=-1)
        z = jax.nn.sigmoid(hx @ W_z + b_z)
        r = jax.nn.sigmoid(hx @ W_r + b_r)
        h_tilde = jnp.tanh(jnp.concatenate([r * node_feats, agg], axis=-1) @ W_h + b_h)
        return (1.0 - z) * node_feats + z * h_tilde

    def _L3_gnn_ref(x, edge_index, W, a):
        import jax, jax.numpy as jnp
        import numpy as np
        N_NODES = 50000
        N_EDGES = 18750
        D_IN = 128
        D_OUT = 128
        n_nodes = x.shape[0]
        d_out = W.shape[1]
        h = x @ W
        src, dst = (edge_index[0], edge_index[1])
        h_src = h[src]
        h_dst = h[dst]
        edge_e = h_src @ a[:d_out] + h_dst @ a[d_out:]
        attention = jax.nn.softmax(edge_e, axis=0)
        msgs = attention[:, None] * h_dst
        out = jax.ops.segment_sum(msgs, src, num_segments=n_nodes)
        return out
    edge_index = jnp.stack([src, dst])
    h = jnp.maximum(_layernorm(x, axis=-1), 0.0)
    x = x + _L0_gnn_ref(h, edge_index, edge_weight, L0_gnn_W_self, L0_gnn_b_self, L0_gnn_W_neigh, L0_gnn_b_neigh, L0_gnn_layer_bias, L0_gnn_W_agg, L0_gnn_b_agg)
    h = jnp.maximum(_layernorm(x, axis=-1), 0.0)
    x = x + _L1_gnn_ref(h, edge_index, L1_gnn_W, L1_gnn_b)
    h = jnp.maximum(_layernorm(x, axis=-1), 0.0)
    x = x + _L2_gnn_ref(h, edge_index, edge_attr_4, L2_gnn_W_msg1, L2_gnn_b_msg1, L2_gnn_W_msg2, L2_gnn_b_msg2, L2_gnn_W_z, L2_gnn_b_z, L2_gnn_W_r, L2_gnn_b_r, L2_gnn_W_h, L2_gnn_b_h)
    h = jnp.maximum(_layernorm(x, axis=-1), 0.0)
    x = x + _L3_gnn_ref(h, edge_index, L3_gnn_W, L3_gnn_a)
    return x

_drawn_inputs = setup_inputs


def setup_inputs(seed=0):
    import zlib

    import numpy as np

    out = dict(_drawn_inputs(seed))
    spreads = {'L0_gnn_layer_bias': (0.0, 0.1),
     'L2_gnn_b_msg1': (0.0, 0.539),
     'L2_gnn_b_msg2': (0.0, 0.339),
     'L2_gnn_b_z': (0.0, 0.573),
     'L2_gnn_b_r': (0.0, 2.0),
     'L2_gnn_b_h': (0.0, 0.1)}
    factors = {'edge_attr_4': 3.974,
     'edge_weight': 5.697,
     'L3_gnn_W': 24.012,
     'L3_gnn_a': 23.249,
     'L2_gnn_W_r': 3.102}
    for name, (base, spread) in spreads.items():
        noise = np.random.default_rng([zlib.crc32(name.encode()), seed]).standard_normal(out[name].shape)
        drawn = base * np.exp(spread * noise) if base else spread * noise
        out[name] = jnp.asarray(drawn.astype(out[name].dtype))
    for name, factor in factors.items():
        out[name] = (out[name] * factor).astype(out[name].dtype)
    return out
```

```python
from contextlib import ExitStack

import concourse.bass as bass
from concourse import mybir

ALU = mybir.AluOpType
ACT = mybir.ActivationFunctionType
F32 = mybir.dt.float32
I32 = mybir.dt.int32
AX_X = mybir.AxisListType.X
RMAX = bass.bass_isa.ReduceOp.max
RADD = bass.bass_isa.ReduceOp.add

P = 128
D = 128
T = 4
R = 4
GW = P * T
N = 50000
E = 25000
EG = -(-E // GW)
NG = -(-N // GW)
PAD_ROW = N + GW
ZR = -(-(PAD_ROW + 1) // (P * EG))
ROWS = ZR * P * EG
CW = D + 4
ZW = 4096
EPS = 1e-5
SLOPE = 0.2
OUTSIDE = -3e38

SRC, DST, DST_KEY, SRC_KEY = 0, T, 2 * T, 3 * T


def over_groups(eng, n, *parts, last=0, ring=R):
    R = ring
    latest = max(delay for _, delay in parts)
    ahead = max(0, -min(delay for _, delay in parts))
    first, end = -(-(R + latest) // R) * R, (n - ahead - last) // R * R

    def peeled(i):
        for part, delay in parts:
            g = i - delay
            if 0 <= g < n:
                part(g, g % R, g // R, min(g, R))

    for i in range(-ahead, first):
        peeled(i)
    with eng.Fori(first // R, end // R) as k:
        for s in range(R):
            for part, delay in parts:
                g = s - delay
                part(k * R + g, g % R, k + g // R, R)
    for i in range(end, n + latest):
        peeled(i)


def wait_apart(eng, sem, value, passed):
    eng.wait_ge(sem, value)
    eng.sem_inc(passed, 1)


def await_overlapped(eng, stored, g):
    if isinstance(g, int) and g == NG - 1:
        before = g - 1
        eng.wait_ge(stored[before % len(stored)], 16 * (before // len(stored) + 1))


class Chain:

    def __init__(self, eng, sem, per_group, passed):
        self.passed = passed
        self.eng, self.sem, self.per_group, self.n = eng, sem, per_group, per_group

    def start(self, g):
        assert self.n == self.per_group
        self.base, self.n = g * self.per_group, 0

    def done(self, instruction, apart=False):
        instruction.then_inc(self.sem, 1)
        self.n += 1
        if apart:
            wait_apart(self.eng, self.sem, self.base + self.n, self.passed)
        else:
            self.eng.wait_ge(self.sem, self.base + self.n)


def tiled(ap):
    return ap.rearrange("p (j d) -> p j d", j=T)


def rows_of(table, g, w=D):
    first = N - GW if isinstance(g, int) and g == NG - 1 else g * GW
    return table[bass.ds(first, GW), 0:w].rearrange("(p j) d -> p (j d)", j=T)


class Shared:

    def __init__(self, nc, ctx):
        self.nc, self.ctx = nc, ctx
        self.ident = self.keep("ident", [P, P])
        self.before = self.keep("before", [P, GW])
        self.spare = self.keep("spare", [P, T])
        self.zeros = self.keep("zeros", [P, ZW])
        self.degree = self.keep("degree", [P, NG * T])
        self.mean = self.keep("mean", [P, NG * T])
        self.scale = self.keep("scale", [P, NG * T])
        self.eps = self.keep("eps", [P, 1])
        self.junk = self.keep("junk", [P, T, GW])

    def keep(self, name, shape, dt=F32):
        return self.ctx.enter_context(self.nc.sbuf_tensor(name, shape, dt))

    def sem(self, name):
        return self.ctx.enter_context(self.nc.semaphore(name))


class Phase:

    def __init__(self, sh, tag, ctx):
        self.nc, self.tag, self.ctx, self.sems = sh.nc, tag, ctx, []
        ctx.callback(self.end)

    def sb(self, name, shape, dt=F32):
        return self.ctx.enter_context(self.nc.sbuf_tensor(self.tag + name, shape, dt))

    def ps(self, name, shape):
        return self.ctx.enter_context(self.nc.psum_tensor(self.tag + name, shape, F32))

    def sem(self, name):
        self.sems.append(self.nc.alloc_semaphore(name=self.tag + name))
        return self.sems[-1]

    def end(self):
        if self.sems:
            self.nc.clear_and_free_semaphores(self.sems)
            self.nc.all_engine_barrier()


def load_constants(nc, sh, ident, before, spare):
    loaded, cleared = sh.sem("constants_loaded"), sh.sem("zeros_set")
    with nc.Block() as block:
        @block.sync
        def _(sp):
            sp.dma_start(sh.ident[:, :], ident).then_inc(loaded, 16)
            sp.dma_start(sh.before[:, :], before).then_inc(loaded, 16)
            sp.dma_start(sh.spare[:, :], spare).then_inc(loaded, 16)
            sp.wait_ge(loaded, 48)

        @block.vector
        def _(dve):
            nc.vector.memset(sh.eps[:, :], EPS).then_inc(cleared, 1)
            nc.vector.memset(sh.zeros[:, :], 0.0).then_inc(cleared, 1)
            dve.wait_ge(cleared, 2)


NORM_STEPS = 2


def normalise(nc, chain, x, stats, mv, rstd, measured, root_ready, g):
    n = x.shape[1]
    for j in range(n):
        last = nc.vector.bn_stats(stats[:, j, :], x[:, j, :])
    chain.done(last, apart=True)
    for j in range(n):
        last = nc.vector.bn_aggr(mv[:, j, :], stats[:, j, :])
    last.then_inc(measured, 1)
    chain.eng.wait_ge(root_ready, g + 1)
    chain.done(nc.vector.reciprocal(rstd[:, 0:n], rstd[:, 0:n]))
    for j in range(n):
        last = nc.vector.tensor_scalar(x[:, j, :], x[:, j, :], mv[:, j, 0:1], rstd[:, j:j + 1],
                                       ALU.subtract, ALU.mult)
    return last


UNITE_STEPS = 5


def block_at(batch, b, a=0):
    return (b * (b + 1) // 2 + a) * P


def unite(nc, sh, chain, batch, eq, row, key, keyf, count, way):
    size = block_at(batch, batch)
    chain.done(nc.vector.tensor_copy(keyf, key))
    for j in range(T):
        first, b = j // batch * batch, j % batch
        at = j // batch * size + block_at(batch, b)
        last = nc.vector.tensor_scalar(eq[:, at:at + (b + 1) * P], row[:, first * P:(j + 1) * P],
                                       keyf[:, j:j + 1], None, ALU.is_equal)
    chain.done(last)
    chain.done(nc.vector.tensor_tensor(way, sh.spare[:, :], keyf, ALU.subtract))
    for j in range(T):
        b = j % batch
        at = j // batch * size + block_at(batch, b)
        last = nc.vector.tensor_tensor_reduce(
            sh.junk[:, j, 0:(b + 1) * P], eq[:, at:at + (b + 1) * P], sh.before[:, (T - 1 - b) * P:GW],
            1.0, 0.0, ALU.mult, ALU.add, count[:, j:j + 1])
    chain.done(last)
    chain.done(nc.vector.scalar_tensor_tensor(way, count[:, :], 0.0, way, ALU.is_gt, ALU.mult))


def batch_sums(pe, batch, out, eq, msg, w):
    size = block_at(batch, batch)
    for j in range(T):
        first, a = j // batch * batch, j % batch
        for b in range(a, batch):
            at = j // batch * size + block_at(batch, b, a)
            last = pe.matmul(out(j), eq[:, at:at + P], msg[:, first + b, 0:w], start=(b == a), stop=(b == batch - 1))
    return last


def linear_edges(nc, sh, tag, table, acc, w, weight, ends, dst_rows, scale=None, norm=False, bias=None,
                 clear_first=False, clear_next=None):
    with ExitStack() as ctx:
        ph = Phase(sh, tag, ctx)
        W, B = ph.sb("weight", [P, D]), ph.sb("bias", [P, D])
        end, key = ph.sb("ends", [P, R, T], I32), ph.sb("keys", [P, R, T], I32)
        row = ph.sb("key_row", [P, R, GW], I32)
        factor = ph.sb("factor", [P, R, T])
        x = ph.sb("x", [P, R, T, D])
        hT = ph.sb("hT", [P, GW])
        msg = ph.sb("msg", [P, R, T, w])
        eq = ph.sb("eq", [P, R, block_at(T, T)])
        keyf, count, way = ph.sb("keyf", [P, R, T]), ph.sb("count", [P, T]), ph.sb("way", [P, R, T])
        stats, mv, rstd = ph.sb("stats", [P, T, 6]), ph.sb("mv", [P, T, 2]), ph.sb("rstd", [P, T])
        to = ph.sb("to", [P, R, T], I32)
        sums = ph.sb("sums", [P, R, T, w])
        psT, psM, psS = ph.ps("psT", [P, GW]), ph.ps("psM", [P, GW]), ph.ps("psS", [P, 2, GW])

        weights_in = ph.sem("weights_in")
        ends_in = [ph.sem(f"ends_in{s}") for s in range(R)]
        loaded = [ph.sem(f"keys_in{s}") for s in range(R)]
        gathered = [ph.sem(f"rows_gathered{s}") for s in range(R)]
        cleared, next_cleared = ph.sem("acc_cleared"), ph.sem("next_cleared")
        ones_set, own, united, normed = ph.sem("ones_set"), ph.sem("norm_steps"), ph.sem("unite_steps"), ph.sem("rows_normed")
        measured, root_ready = ph.sem("rows_measured"), ph.sem("root_ready")
        turned, hT_ready, product = ph.sem("rows_turned"), ph.sem("hT_ready"), ph.sem("product")
        msg_ready, summed, sums_ready = ph.sem("msg_ready"), ph.sem("summed"), ph.sem("sums_ready")
        landed = ph.sem("scatters_landed")
        per_load = 16 * (3 if scale is not None else 2)
        n_weights = 16 * (1 if bias is None else 2)
        clears = -(-ROWS * w // P // ZW)

        block = ctx.enter_context(nc.Block())

        @block.sync
        def _(sp):
            sp.dma_start(W[:, :], weight).then_inc(weights_in, 16)
            if bias is not None:
                sp.dma_start(B[:, :], bias.to_broadcast([P, D])).then_inc(weights_in, 16)

            def load(g, s, k, back):
                if back == R:
                    sp.wait_ge(gathered[s], k * 64)
                sp.dma_start(end[:, s, :], ends[g, :, SRC:SRC + T]).then_inc(ends_in[s], 16)
                if back == R:
                    sp.wait_ge(msg_ready, 2 * (g - R + 1))
                sp.dma_start(key[:, s, :], ends[g, :, DST_KEY:DST_KEY + T]).then_inc(loaded[s], 16)
                sp.dma_start(row[:, s, :], dst_rows[bass.ds(g, 1), :].to_broadcast([P, GW])).then_inc(loaded[s], 16)
                if scale is not None:
                    sp.dma_start(factor[:, s, :], scale[g, :, :]).then_inc(loaded[s], 16)
                if clear_next is not None:
                    part = clear_next[bass.ds(g * (P * ZR), P * ZR), :]
                    sp.dma_start(part.rearrange("(p r) d -> p (r d)", p=P), sh.zeros[:, 0:ZR * part.shape[1]]
                                 ).then_inc(next_cleared, 16)
            over_groups(sp, EG, (load, 0))
            if clear_next is not None:
                sp.wait_ge(next_cleared, 16 * EG)

        @block.gpsimd
        def _(pool):
            passed = ph.sem("pool_waits_passed")
            def gather(s, j):
                at = bass.IndirectOffsetOnAxis(ap=end[:, s, j:j + 1], axis=0)
                pool.indirect_dma_start(x[:, s, j, :], None, table, at).then_inc(gathered[s], 16)

            for s in range(R):
                pool.wait_ge(ends_in[s], 16)
                for j in range(T):
                    gather(s, j)
            if clear_first:
                pool.wait_ge(cleared, 16 * clears)

            def scatter(g, s, k, back):
                ahead = not isinstance(g, int) or g + R < EG
                pool.wait_ge(sums_ready, g + 1)
                wait_apart(pool, msg_ready, 2 * (g + 1), passed)
                if ahead:
                    pool.wait_ge(ends_in[s], (k + 2) * 16)
                    wait_apart(pool, turned, g + 1, passed)
                for j in range(T):
                    at = bass.IndirectOffsetOnAxis(ap=to[:, s, j:j + 1], axis=0)
                    pool.indirect_dma_start(acc, at, sums[:, s, j, :], None, compute_op=ALU.add).then_inc(landed, 16)
                if ahead:
                    for j in range(T):
                        gather(s, j)
                wait_apart(pool, landed, (g + 1) * 64, passed)
            over_groups(pool, EG, (scatter, 0), last=R)

        @block.vector
        def _(dve):
            passed = ph.sem("dve_waits_passed")
            norms = Chain(dve, own, NORM_STEPS, passed)
            unites = Chain(dve, united, UNITE_STEPS, passed)
            nc.vector.memset(msg[:, :, :, :], 1.0).then_inc(ones_set, 1)
            dve.wait_ge(ones_set, 1)
            dve.wait_ge(weights_in, n_weights)

            def norm_rows(g, s, k, back):
                norms.start(g)
                dve.wait_ge(gathered[s], (k + 1) * 64)
                normalise(nc, norms, x[:, s], stats, mv, rstd, measured, root_ready, g).then_inc(normed, 1)

            def unite_edges(g, s, k, back):
                unites.start(g)
                dve.wait_ge(loaded[s], (k + 1) * per_load)
                if back == R:
                    dve.wait_ge(summed, g - R + 1)
                unite(nc, sh, unites, T, eq[:, s], row[:, s], key[:, s], keyf[:, s], count, way[:, s])

            def messages(g, s, k, back):
                dve.wait_ge(product, g + 1)
                if back == R:
                    dve.wait_ge(landed, (g - R + 1) * 64)
                nc.vector.tensor_tensor(to[:, s, :], way[:, s, :], keyf[:, s, :], ALU.add).then_inc(msg_ready, 1)
                if scale is not None:
                    by = factor[:, s, :].unsqueeze(2).to_broadcast([P, T, D])
                    last = nc.vector.tensor_tensor(msg[:, s, :, 0:D], tiled(psM[:, :]), by, ALU.mult)
                else:
                    by = B[:, :].unsqueeze(1).to_broadcast([P, T, D])
                    last = nc.vector.tensor_tensor(msg[:, s, :, 0:D], tiled(psM[:, :]), by, ALU.add)
                last.then_inc(msg_ready, 1)
            over_groups(dve, EG, *([(norm_rows, 0)] if norm else []), (messages, 1), (unite_edges, -1))

        @block.tensor
        def _(pe):
            pe.wait_ge(weights_in, n_weights)

            def turn(g, s, k, back):
                if norm:
                    pe.wait_ge(normed, g + 1)
                else:
                    pe.wait_ge(gathered[s], (k + 1) * 64)
                if back:
                    pe.wait_ge(hT_ready, g)
                for j in range(T):
                    last = pe.transpose(psT[:, j * P:(j + 1) * P], x[:, s, j, :], sh.ident[:, :])
                last.then_inc(turned, 1)

            def multiply(g, s, k, back):
                pe.wait_ge(hT_ready, g + 1)
                if back:
                    pe.wait_ge(msg_ready, 2 * g)
                for j in range(T):
                    last = pe.matmul(psM[:, j * D:(j + 1) * D], hT[:, j * P:(j + 1) * P], W[:, :],
                                     start=True, stop=True)
                last.then_inc(product, 1)

            def add_up(g, s, k, back):
                pe.wait_ge(msg_ready, 2 * (g + 1))
                if back:
                    pe.wait_ge(sums_ready, g)
                batch_sums(pe, T, lambda j: psS[:, j // 2, j % 2 * w:(j % 2 + 1) * w], eq[:, s], msg[:, s], w
                           ).then_inc(summed, 1)
            over_groups(pe, EG, (turn, 0), (add_up, 1), (multiply, 0))

        @block.scalar
        def _(act):
            if clear_first:
                flat = acc.rearrange("(p r) d -> p (r d)", p=P)
                for c in range(clears):
                    m = min(ZW, flat.shape[1] - c * ZW)
                    act.dma_start(flat[:, c * ZW:c * ZW + m], sh.zeros[:, 0:m]).then_inc(cleared, 16)

            def transposed(g, s, k, back):
                if norm:
                    act.wait_ge(measured, g + 1)
                    nc.scalar.activation(rstd[:, :], mv[:, :, 1], ACT.Sqrt, bias=sh.eps[:, :]).then_inc(root_ready, 1)
                act.wait_ge(turned, g + 1)
                if back:
                    act.wait_ge(product, g)
                nc.scalar.activation(hT[:, :], psT[:, :], ACT.Relu if norm else ACT.Copy).then_inc(hT_ready, 1)

            def sums_out(g, s, k, back):
                act.wait_ge(summed, g + 1)
                if back == R:
                    act.wait_ge(landed, (g - R + 1) * 64)
                nc.scalar.activation(sums[:, s, :, :].rearrange("p (q j) d -> p q (j d)", q=2), psS[:, :, 0:2 * w],
                                     ACT.Copy).then_inc(sums_ready, 1)
            over_groups(act, EG, (transposed, 0), (sums_out, 1))


def mlp_edges(nc, sh, tag, table, acc, w1, b1, w2, b2, ends, dst_rows, attrT):
    with ExitStack() as ctx:
        ph = Phase(sh, tag, ctx)
        W1s, W1d, W2, B2 = (ph.sb(n, [P, D]) for n in ("w1_src", "w1_dst", "w2", "b2"))
        W1e, B1 = ph.sb("w1_attr", [T, D]), ph.sb("b1", [P, 1])
        end, key = ph.sb("ends", [P, R, 2 * T], I32), ph.sb("keys", [P, R, T], I32)
        row = ph.sb("key_row", [P, R, GW], I32)
        attr = ph.sb("attr", [4, R, GW])
        x = ph.sb("x", [P, R, 2 * T, D])
        hT, hidden = ph.sb("hT", [P, 2 * GW]), ph.sb("hidden", [P, GW])
        msg = ph.sb("msg", [P, R, T, D])
        eq = ph.sb("eq", [P, R, block_at(T, T)])
        keyf, count, way = ph.sb("keyf", [P, R, T]), ph.sb("count", [P, T]), ph.sb("way", [P, R, T])
        stats, mv, rstd = ph.sb("stats", [P, 2 * T, 6]), ph.sb("mv", [P, 2 * T, 2]), ph.sb("rstd", [P, 2 * T])
        to = ph.sb("to", [P, R, T], I32)
        sums = ph.sb("sums", [P, R, T, D])
        psT, psH, psM, psS = ph.ps("psT", [P, 2 * GW]), ph.ps("psH", [P, GW]), ph.ps("psM", [P, GW]), ph.ps("psS", [P, GW])

        weights_in = ph.sem("weights_in")
        ends_in = [ph.sem(f"ends_in{s}") for s in range(R)]
        loaded = [ph.sem(f"keys_in{s}") for s in range(R)]
        gathered = [ph.sem(f"rows_gathered{s}") for s in range(R)]
        own, united, normed = ph.sem("norm_steps"), ph.sem("unite_steps"), ph.sem("rows_normed")
        measured, root_ready = ph.sem("rows_measured"), ph.sem("root_ready")
        turned, hT_ready, preact = ph.sem("rows_turned"), ph.sem("hT_ready"), ph.sem("preactivation")
        hidden_ready, product, msg_ready = ph.sem("hidden_ready"), ph.sem("product"), ph.sem("msg_ready")
        summed, sums_ready, landed = ph.sem("summed"), ph.sem("sums_ready"), ph.sem("scatters_landed")

        block = ctx.enter_context(nc.Block())

        @block.sync
        def _(sp):
            for dst, src in ((W1s[:, :], w1[0:D, :]), (W1d[:, :], w1[D:2 * D, :]), (W1e[:, :], w1[2 * D:2 * D + 4, :]),
                             (W2[:, :], w2), (B1[:, :], b1), (B2[:, :], b2.to_broadcast([P, D]))):
                sp.dma_start(dst, src).then_inc(weights_in, 16)

            def load(g, s, k, back):
                if back == R:
                    sp.wait_ge(gathered[s], k * 128)
                sp.dma_start(end[:, s, :], ends[g, :, SRC:SRC + 2 * T]).then_inc(ends_in[s], 16)
                if back == R:
                    sp.wait_ge(msg_ready, 2 * (g - R + 1))
                sp.dma_start(key[:, s, :], ends[g, :, DST_KEY:DST_KEY + T]).then_inc(loaded[s], 16)
                sp.dma_start(row[:, s, :], dst_rows[bass.ds(g, 1), :].to_broadcast([P, GW])).then_inc(loaded[s], 16)
                sp.dma_start(attr[:, s, :], attrT[:, bass.ds(g * GW, GW)]).then_inc(loaded[s], 16)
            over_groups(sp, EG, (load, 0))

        @block.gpsimd
        def _(pool):
            passed = ph.sem("pool_waits_passed")
            def gather(s, j):
                at = bass.IndirectOffsetOnAxis(ap=end[:, s, j:j + 1], axis=0)
                pool.indirect_dma_start(x[:, s, j, :], None, table, at).then_inc(gathered[s], 16)

            for s in range(R):
                pool.wait_ge(ends_in[s], 16)
                for j in range(2 * T):
                    gather(s, j)

            def scatter(g, s, k, back):
                ahead = not isinstance(g, int) or g + R < EG
                pool.wait_ge(sums_ready, g + 1)
                wait_apart(pool, msg_ready, 2 * (g + 1), passed)
                if ahead:
                    pool.wait_ge(ends_in[s], (k + 2) * 16)
                    wait_apart(pool, turned, g + 1, passed)
                for j in range(T):
                    at = bass.IndirectOffsetOnAxis(ap=to[:, s, j:j + 1], axis=0)
                    pool.indirect_dma_start(acc, at, sums[:, s, j, :], None, compute_op=ALU.add).then_inc(landed, 16)
                if ahead:
                    for j in range(2 * T):
                        gather(s, j)
                wait_apart(pool, landed, (g + 1) * 64, passed)
            over_groups(pool, EG, (scatter, 0), last=R)

        @block.vector
        def _(dve):
            passed = ph.sem("dve_waits_passed")
            norms = Chain(dve, own, NORM_STEPS, passed)
            unites = Chain(dve, united, UNITE_STEPS, passed)
            dve.wait_ge(weights_in, 96)

            def norm_rows(g, s, k, back):
                norms.start(g)
                dve.wait_ge(gathered[s], (k + 1) * 128)
                normalise(nc, norms, x[:, s], stats, mv, rstd, measured, root_ready, g).then_inc(normed, 1)

            def unite_edges(g, s, k, back):
                unites.start(g)
                dve.wait_ge(loaded[s], (k + 1) * 48)
                if back == R:
                    dve.wait_ge(summed, g - R + 1)
                unite(nc, sh, unites, T, eq[:, s], row[:, s], key[:, s], keyf[:, s], count, way[:, s])

            def messages(g, s, k, back):
                dve.wait_ge(product, g + 1)
                if back == R:
                    dve.wait_ge(landed, (g - R + 1) * 64)
                nc.vector.tensor_tensor(to[:, s, :], way[:, s, :], keyf[:, s, :], ALU.add).then_inc(msg_ready, 1)
                by = B2[:, :].unsqueeze(1).to_broadcast([P, T, D])
                nc.vector.tensor_tensor(msg[:, s, :, :], tiled(psM[:, :]), by, ALU.add).then_inc(msg_ready, 1)
            over_groups(dve, EG, (norm_rows, 0), (messages, 1), (unite_edges, -1))

        @block.tensor
        def _(pe):
            pe.wait_ge(weights_in, 96)

            def turn(g, s, k, back):
                pe.wait_ge(normed, g + 1)
                if back:
                    pe.wait_ge(hT_ready, g)
                for j in range(2 * T):
                    last = pe.transpose(psT[:, j * P:(j + 1) * P], x[:, s, j, :], sh.ident[:, :])
                last.then_inc(turned, 1)

            def first_layer(g, s, k, back):
                pe.wait_ge(loaded[s], (k + 1) * 48)
                pe.wait_ge(hT_ready, g + 1)
                if back:
                    pe.wait_ge(hidden_ready, g)
                pe.matmul(psH[:, :], W1s[:, :], hT[:, 0:GW], start=True, stop=False)
                pe.matmul(psH[:, :], W1d[:, :], hT[:, GW:2 * GW], start=False, stop=False)
                pe.matmul(psH[:, :], W1e[:, :], attr[:, s, :], start=False, stop=True).then_inc(preact, 1)

            def second_layer(g, s, k, back):
                pe.wait_ge(hidden_ready, g + 1)
                if back:
                    pe.wait_ge(msg_ready, 2 * g)
                for j in range(T):
                    last = pe.matmul(psM[:, j * D:(j + 1) * D], hidden[:, j * P:(j + 1) * P], W2[:, :],
                                     start=True, stop=True)
                last.then_inc(product, 1)

            def add_up(g, s, k, back):
                pe.wait_ge(msg_ready, 2 * (g + 1))
                if back:
                    pe.wait_ge(sums_ready, g)
                batch_sums(pe, T, lambda j: psS[:, j * D:(j + 1) * D], eq[:, s], msg[:, s], D).then_inc(summed, 1)
            over_groups(pe, EG, (turn, 0), (add_up, 1), (first_layer, 0), (second_layer, 0))

        @block.scalar
        def _(act):
            act.wait_ge(weights_in, 96)

            def transposed(g, s, k, back):
                act.wait_ge(measured, g + 1)
                nc.scalar.activation(rstd[:, :], mv[:, :, 1], ACT.Sqrt, bias=sh.eps[:, :]).then_inc(root_ready, 1)
                act.wait_ge(turned, g + 1)
                if back:
                    act.wait_ge(preact, g)
                nc.scalar.activation(hT[:, :], psT[:, :], ACT.Relu).then_inc(hT_ready, 1)

            def hide(g, s, k, back):
                act.wait_ge(preact, g + 1)
                if back:
                    act.wait_ge(product, g)
                nc.scalar.activation(hidden[:, :], psH[:, :], ACT.Relu, bias=B1[:, :]).then_inc(hidden_ready, 1)

            def sums_out(g, s, k, back):
                act.wait_ge(summed, g + 1)
                if back == R:
                    act.wait_ge(landed, (g - R + 1) * 64)
                nc.scalar.activation(sums[:, s, :, :].rearrange("p j d -> p (j d)"), psS[:, :], ACT.Copy
                                     ).then_inc(sums_ready, 1)
            over_groups(act, EG, (transposed, 0), (sums_out, 1), (hide, 0))


def gcn_nodes(nc, sh, tag, table, acc, w, weights, biases, out, norm=False, last_layer=None):
    R, products = (4, 2) if last_layer else (6, 3)
    with ExitStack() as ctx:
        ph = Phase(sh, tag, ctx)
        n_bias = biases.shape[0]
        W, bias_rows, bias = ph.sb("weights", [P, 2 * D]), ph.sb("bias_rows", [P, n_bias, D]), ph.sb("bias", [P, D])
        x, sums = ph.sb("x", [P, R, T * D]), ph.sb("sums", [P, R, T, w])
        hT = ph.sb("hT", [P, R, GW])
        part = ph.sb("part", [P, R, T * D])
        h = ph.sb("h", [P, R, T * D])
        share = ph.sb("share", [P, R, T])
        stats, mv = ph.sb("stats", [P, T, 6]), ph.sb("mv", [P, R, T, 2])
        rstd, minus = ph.sb("rstd", [P, R, T]), ph.sb("minus_mean", [P, R, T])
        psT, psP = ph.ps("psT", [P, GW]), ph.ps("psP", [P, products, T, 2 * D])
        n_load = 2
        if last_layer:
            res_table, wa, ba = last_layer
            WA, BA = ph.sb("w_last", [P, D]), ph.sb("b_last", [P, D])
            res, new = ph.sb("res", [P, R, T * D]), ph.sb("new", [P, R, T * D])
            h2T = ph.sb("h2T", [P, R, GW])
            psT2, psO = ph.ps("psT2", [P, GW]), ph.ps("psO", [P, GW])
            res_in = [ph.sem(f"res_in{s}") for s in range(R)]
        weights_in = ph.sem("weights_in")
        loaded = [ph.sem(f"rows_in{s}") for s in range(R)]
        stored = [ph.sem(f"stored{s}") for s in range(R)]
        degree_set, totalled, share_ready, bias_set = ph.sem("degree_set"), ph.sem("totalled"), ph.sem("share_ready"), ph.sem("bias_set")
        counted, measured, root_ready = ph.sem("counted"), ph.sem("rows_measured"), ph.sem("root_ready")
        inverted, factors_ready, normed = ph.sem("inverted"), ph.sem("factors_ready"), ph.sem("rows_normed")
        neighbours, scaled = ph.sem("neighbours_added"), ph.sem("scaled")
        turned, hT_ready, product = ph.sem("rows_turned"), ph.sem("hT_ready"), ph.sem("product")
        combined, biased, leaked = ph.sem("combined"), ph.sem("biased"), ph.sem("leaked")
        turned2, h2T_ready, product2 = ph.sem("turned2"), ph.sem("h2T_ready"), ph.sem("product2")
        added, finished = ph.sem("added"), ph.sem("finished")
        n_weights = 32 + (32 if last_layer else 0)

        block = ctx.enter_context(nc.Block())

        @block.sync
        def _(sp):
            sp.dma_start(W[:, :], weights).then_inc(weights_in, 16)
            rows = biases.rearrange("(o b) d -> o b d", o=1)
            sp.dma_start(bias_rows[:, :, :], rows.to_broadcast([P, n_bias, D])).then_inc(weights_in, 16)
            if last_layer:
                sp.dma_start(WA[:, :], wa).then_inc(weights_in, 16)
                sp.dma_start(BA[:, :], ba.to_broadcast([P, D])).then_inc(weights_in, 16)

            def load(g, s, k, back):
                if back == R:
                    sp.wait_ge(turned, g - R + 1)
                    sp.wait_ge(neighbours, g - R + 1)
                    if norm:
                        sp.wait_ge(degree_set, g - R + 1)
                sp.dma_start(x[:, s, :], rows_of(table, g)).then_inc(loaded[s], 16)
                sp.dma_start(sums[:, s, :, :].rearrange("p j d -> p (j d)"), rows_of(acc, g, w)).then_inc(loaded[s], 16)

            def load_res(g, s, k, back):
                if back == R:
                    sp.wait_ge(finished, g - R + 1)
                sp.dma_start(res[:, s, :], rows_of(res_table, g)).then_inc(res_in[s], 16)
            over_groups(sp, NG, (load, 0), *([(load_res, 2)] if last_layer else []), ring=R)

        @block.vector
        def _(dve):
            passed = ph.sem("dve_waits_passed")
            dve.wait_ge(weights_in, n_weights)
            nc.vector.tensor_tensor(bias[:, :], bias_rows[:, 0, :], bias_rows[:, 1, :], ALU.add).then_inc(bias_set, 1)
            for b in range(2, n_bias):
                dve.wait_ge(bias_set, b - 1)
                nc.vector.tensor_tensor(bias[:, :], bias[:, :], bias_rows[:, b, :], ALU.add).then_inc(bias_set, 1)

            def count(g, s, k, back):
                dve.wait_ge(loaded[s], (k + 1) * 32)
                if back:
                    dve.wait_ge(measured, g)
                for j in range(T):
                    i = nc.vector.bn_stats(stats[:, j, :], x[:, s, j * D:(j + 1) * D])
                i.then_inc(counted, 1)

            def measure(g, s, k, back):
                wait_apart(dve, counted, g + 1, passed)
                for j in range(T):
                    i = nc.vector.bn_aggr(mv[:, s, j, :], stats[:, j, :])
                i.then_inc(measured, 1)

            def invert(g, s, k, back):
                dve.wait_ge(root_ready, g + 1)
                nc.vector.reciprocal(rstd[:, s, :], rstd[:, s, :]).then_inc(inverted, 1)

            def centre(g, s, k, back):
                dve.wait_ge(inverted, g + 1)
                nc.vector.scalar_tensor_tensor(minus[:, s, :], mv[:, s, :, 0], -1.0, rstd[:, s, :], ALU.mult, ALU.mult
                                               ).then_inc(factors_ready, 1)

            def degrees(g, s, k, back):
                dve.wait_ge(loaded[s], (k + 1) * 32)
                nc.vector.tensor_copy(sh.degree[:, bass.ds(g * T, T)], sums[:, s, :, D]).then_inc(degree_set, 1)

            def totals(g, s, k, back):
                if norm:
                    dve.wait_ge(degree_set, g + 1)
                if back == R:
                    dve.wait_ge(combined, g - R + 1)
                nc.vector.tensor_scalar(share[:, s, :], sh.degree[:, bass.ds(g * T, T)], 1.0, None, ALU.add
                                        ).then_inc(totalled, 1)

            def shares(g, s, k, back):
                dve.wait_ge(totalled, g + 1)
                nc.vector.reciprocal(share[:, s, :], share[:, s, :]).then_inc(share_ready, 1)

            def add_neighbours(g, s, k, back):
                dve.wait_ge(loaded[s], (k + 1) * 32)
                dve.wait_ge(product, g + 1)
                if back == R:
                    if last_layer:
                        dve.wait_ge(combined, g - R + 1)
                    else:
                        dve.wait_ge(leaked, g - R + 1)
                nc.vector.tensor_tensor(tiled(part[:, s, :]), psP[:, s % products, :, D:2 * D], sums[:, s, :, 0:D], ALU.add
                                        ).then_inc(neighbours, 1)

            def combine(g, s, k, back):
                dve.wait_ge(neighbours, g + 1)
                dve.wait_ge(share_ready, g + 1)
                if back == R:
                    dve.wait_ge(turned2 if last_layer else leaked, g - R + 1)
                    if not last_layer:
                        dve.wait_ge(stored[s], k * 16)
                for j in range(T):
                    c = slice(j * D, (j + 1) * D)
                    i = nc.vector.scalar_tensor_tensor(h[:, s, c], part[:, s, c], share[:, s, j:j + 1],
                                                       psP[:, s % products, j, 0:D], ALU.mult, ALU.add)
                i.then_inc(combined, 1)

            def add_rest(g, s, k, back):
                dve.wait_ge(product2, g + 1)
                dve.wait_ge(res_in[s], (k + 1) * 16)
                if back == R:
                    dve.wait_ge(stored[s], k * 16)
                nc.vector.tensor_tensor(new[:, s, :], psO[:, :], res[:, s, :], ALU.add).then_inc(added, 1)

            def leak(g, s, k, back):
                dve.wait_ge(biased, g + 1)
                nc.vector.scalar_tensor_tensor(h[:, s, :], h[:, s, :], SLOPE, h[:, s, :], ALU.mult, ALU.max
                                               ).then_inc(leaked, 1)
            if norm:
                over_groups(dve, NG, (count, 0), (invert, 1), (degrees, 1), (measure, 0), (centre, 1), (totals, 1),
                            (add_neighbours, 3), (shares, 1), (combine, 3), ring=R)
            else:
                over_groups(dve, NG, (totals, 0), (add_neighbours, 1), (shares, 0), (combine, 1), (leak, 2), (add_rest, 4),
                            ring=R)

        @block.gpsimd
        def _(pool):
            passed = ph.sem("pool_waits_passed")
            pool.wait_ge(bias_set, n_bias - 1)

            def add_bias(g, s, k, back):
                pool.wait_ge(combined, g + 1)
                rows = tiled(h[:, s, :])
                nc.gpsimd.tensor_tensor(rows, rows, bias[:, :].unsqueeze(1).to_broadcast([P, T, D]), ALU.add
                                        ).then_inc(biased, 1)

            def finish(g, s, k, back):
                pool.wait_ge(added, g + 1)
                rows = tiled(new[:, s, :])
                nc.gpsimd.tensor_tensor(rows, rows, BA[:, :].unsqueeze(1).to_broadcast([P, T, D]), ALU.add
                                        ).then_inc(finished, 1)


            def leak(g, s, k, back):
                pool.wait_ge(scaled, g + 1)
                nc.gpsimd.tensor_tensor(h[:, s, :], h[:, s, :], part[:, s, :], ALU.add).then_inc(leaked, 1)
            if last_layer:
                over_groups(pool, NG, (add_bias, 1), (finish, 4), ring=R)
            else:
                over_groups(pool, NG, (add_bias, 0), (leak, 1), ring=R)

        @block.tensor
        def _(pe):
            pe.wait_ge(weights_in, n_weights)

            def turn(g, s, k, back):
                if norm:
                    pe.wait_ge(normed, g + 1)
                else:
                    pe.wait_ge(loaded[s], (k + 1) * 32)
                if back:
                    pe.wait_ge(hT_ready, g)
                for j in range(T):
                    i = pe.transpose(psT[:, j * P:(j + 1) * P], x[:, s, j * D:(j + 1) * D], sh.ident[:, :])
                i.then_inc(turned, 1)

            def multiply(g, s, k, back):
                pe.wait_ge(hT_ready, g + 1)
                if back >= products:
                    pe.wait_ge(combined, g - products + 1)
                for j in range(T):
                    i = pe.matmul(psP[:, s % products, j, :], hT[:, s, j * P:(j + 1) * P], W[:, :], start=True, stop=True)
                i.then_inc(product, 1)

            def turn2(g, s, k, back):
                pe.wait_ge(leaked, g + 1)
                if back:
                    pe.wait_ge(h2T_ready, g)
                for j in range(T):
                    i = pe.transpose(psT2[:, j * P:(j + 1) * P], h[:, s, j * D:(j + 1) * D], sh.ident[:, :])
                i.then_inc(turned2, 1)

            def multiply2(g, s, k, back):
                pe.wait_ge(h2T_ready, g + 1)
                if back:
                    pe.wait_ge(added, g)
                for j in range(T):
                    i = pe.matmul(psO[:, j * D:(j + 1) * D], h2T[:, s, j * P:(j + 1) * P], WA[:, :],
                                  start=True, stop=True)
                i.then_inc(product2, 1)
            over_groups(pe, NG, (multiply, 1), (turn, 0),
                        *([(multiply2, 4), (turn2, 3)] if last_layer else []), ring=R)

        @block.scalar
        def _(act):
            def take_root(g, s, k, back):
                act.wait_ge(measured, g + 1)
                nc.scalar.activation(rstd[:, s, :], mv[:, s, :, 1], ACT.Sqrt, bias=sh.eps[:, :]).then_inc(root_ready, 1)

            def normalise(g, s, k, back):
                act.wait_ge(factors_ready, g + 1)
                for j in range(T):
                    c = slice(j * D, (j + 1) * D)
                    i = nc.scalar.activation(x[:, s, c], x[:, s, c], ACT.Relu, scale=rstd[:, s, j:j + 1],
                                             bias=minus[:, s, j:j + 1])
                i.then_inc(normed, 1)

            def transposed(g, s, k, back):
                act.wait_ge(turned, g + 1)
                if back == R:
                    act.wait_ge(product, g - R + 1)
                nc.scalar.activation(hT[:, s, :], psT[:, :], ACT.Copy).then_inc(hT_ready, 1)

            def split_leaky(g, s, k, back):
                act.wait_ge(biased, g + 1)
                nc.scalar.activation(part[:, s, :], h[:, s, :], ACT.Relu, scale=1 - SLOPE)
                nc.scalar.activation(h[:, s, :], h[:, s, :], ACT.Copy, scale=SLOPE).then_inc(scaled, 1)

            def transposed2(g, s, k, back):
                act.wait_ge(turned2, g + 1)
                if back == R:
                    act.wait_ge(product2, g - R + 1)
                nc.scalar.activation(h2T[:, s, :], psT2[:, :], ACT.Copy).then_inc(h2T_ready, 1)

            def store(g, s, k, back):
                await_overlapped(act, stored, g)
                if last_layer:
                    act.wait_ge(finished, g + 1)
                    act.dma_start(rows_of(out, g), new[:, s, :]).then_inc(stored[s], 16)
                else:
                    act.wait_ge(leaked, g + 1)
                    act.dma_start(rows_of(out, g), h[:, s, :]).then_inc(stored[s], 16)
            if last_layer:
                over_groups(act, NG, (transposed, 0), (transposed2, 3), (store, 5), ring=R)
            else:
                over_groups(act, NG, (normalise, 1), (take_root, 0), (transposed, 1), (split_leaky, 4), (store, 6), ring=R)
            for s in range(R):
                act.wait_ge(stored[s], 16 * -(-(NG - s) // R))


def mean_nodes(nc, sh, tag, table, acc, out):
    with ExitStack() as ctx:
        ph = Phase(sh, tag, ctx)
        x, sums, new = (ph.sb(n, [P, R, T * D]) for n in ("x", "sums", "new"))
        share = ph.sb("share", [P, R, T])
        loaded = [ph.sem(f"rows_in{s}") for s in range(R)]
        stored = [ph.sem(f"stored{s}") for s in range(R)]
        stats, mv, root = ph.sb("stats", [P, T, 6]), ph.sb("mv", [P, R, T, 2]), ph.sb("root", [P, R, T])
        own, added = ph.sem("share_steps"), ph.sem("added")
        counted, measured, rooted, kept = (ph.sem(n) for n in ("counted", "measured", "rooted", "kept"))
        block = ctx.enter_context(nc.Block())

        @block.sync
        def _(sp):
            def load(g, s, k, back):
                if back == R:
                    sp.wait_ge(added, g - R + 1)
                sp.dma_start(x[:, s, :], rows_of(table, g)).then_inc(loaded[s], 16)
                sp.dma_start(sums[:, s, :], rows_of(acc, g)).then_inc(loaded[s], 16)
            over_groups(sp, NG, (load, 0))

        @block.vector
        def _(dve):
            passed = ph.sem("dve_waits_passed")
            steps = Chain(dve, own, 2, passed)

            def shares(g, s, k, back):
                steps.start(g)
                degree = sh.degree[:, bass.ds(g * T, T)]
                steps.done(nc.vector.tensor_scalar(share[:, s, :], degree, 1.0, None, ALU.max))
                steps.done(nc.vector.reciprocal(share[:, s, :], share[:, s, :]))

            def add(g, s, k, back):
                dve.wait_ge(loaded[s], (k + 1) * 32)
                if back == R:
                    dve.wait_ge(stored[s], k * 16)
                for j in range(T):
                    c = slice(j * D, (j + 1) * D)
                    i = nc.vector.scalar_tensor_tensor(new[:, s, c], sums[:, s, c], share[:, s, j:j + 1], x[:, s, c],
                                                       ALU.mult, ALU.add)
                i.then_inc(added, 1)

            def count(g, s, k, back):
                dve.wait_ge(added, g + 1)
                if back:
                    dve.wait_ge(measured, g)
                for j in range(T):
                    i = nc.vector.bn_stats(stats[:, j, :], new[:, s, j * D:(j + 1) * D])
                i.then_inc(counted, 1)

            def measure(g, s, k, back):
                wait_apart(dve, counted, g + 1, passed)
                for j in range(T):
                    i = nc.vector.bn_aggr(mv[:, s, j, :], stats[:, j, :])
                i.then_inc(measured, 1)

            def keep(g, s, k, back):
                dve.wait_ge(measured, g + 1)
                dve.wait_ge(rooted, g + 1)
                nc.vector.tensor_copy(sh.mean[:, bass.ds(g * T, T)], mv[:, s, :, 0]).then_inc(kept, 1)
                nc.vector.reciprocal(sh.scale[:, bass.ds(g * T, T)], root[:, s, :]).then_inc(kept, 1)
            over_groups(dve, NG, (count, 1), (add, 0), (measure, 1), (shares, -1), (keep, 2))
            dve.wait_ge(kept, 2 * NG)

        @block.scalar
        def _(act):
            def store(g, s, k, back):
                await_overlapped(act, stored, g)
                act.wait_ge(added, g + 1)
                act.dma_start(rows_of(out, g), new[:, s, :]).then_inc(stored[s], 16)

            def take_root(g, s, k, back):
                act.wait_ge(measured, g + 1)
                if back == R:
                    act.wait_ge(kept, 2 * (g - R + 1))
                nc.scalar.activation(root[:, s, :], mv[:, s, :, 1], ACT.Sqrt, bias=sh.eps[:, :]).then_inc(rooted, 1)
            over_groups(act, NG, (store, 0), (take_root, 0))
            for s in range(R):
                act.wait_ge(stored[s], 16 * -(-(NG - s) // R))


def gated_nodes(nc, sh, tag, table, acc, wz, wr, wh, bz, br, bh, out):
    R = 6
    with ExitStack() as ctx:
        ph = Phase(sh, tag, ctx)
        W = {n: ph.sb("w" + n, [P, 2, D]) for n in "zrh"}
        B = {n: ph.sb("b" + n, [P, 1]) for n in "zrh"}
        x, sums, xn = (ph.sb(n, [P, R, T * D]) for n in ("x", "sums", "xn"))
        hT, aT, z, r, t, new = (ph.sb(n, [P, R, GW]) for n in ("hT", "aT", "z", "r", "t", "new"))
        psH, psA, psZ, psR, psC, psO = (ph.ps(n, [P, GW]) for n in ("psH", "psA", "psZ", "psR", "psC", "psO"))
        weights_in, spare_cleared = ph.sem("weights_in"), ph.sem("spare_cleared")
        loaded = [ph.sem(f"rows_in{s}") for s in range(R)]
        stored = [ph.sem(f"stored{s}") for s in range(R)]
        normed = ph.sem("rows_normed")
        turned, acc_turned, hT_ready, aT_ready = (ph.sem(n) for n in ("turned", "acc_turned", "hT_ready", "aT_ready"))
        z_in, r_in, z_ready, r_ready = (ph.sem(n) for n in ("z_in", "r_in", "z_ready", "r_ready"))
        reset, cand, cand_ready = (ph.sem(n) for n in ("reset", "candidate", "candidate_ready"))
        mixing, back_turned, added = ph.sem("mixing"), ph.sem("back_turned"), ph.sem("added")

        block = ctx.enter_context(nc.Block())

        @block.sync
        def _(sp):
            for n, w, b in (("z", wz, bz), ("r", wr, br), ("h", wh, bh)):
                sp.dma_start(W[n][:, :, :], w.rearrange("(c p) d -> p c d", p=P)).then_inc(weights_in, 16)
                sp.dma_start(B[n][:, :], b).then_inc(weights_in, 16)
            sp.dma_start(out[N:PAD_ROW, :].rearrange("(p r) d -> p (r d)", p=P), sh.zeros[:, 0:T * D]
                         ).then_inc(spare_cleared, 16)
            sp.dma_start(out[PAD_ROW:PAD_ROW + 1, :], sh.zeros[0:1, 0:D]).then_inc(spare_cleared, 16)

            def load(g, s, k, back):
                if back == R:
                    sp.wait_ge(added, g - R + 1)
                    sp.wait_ge(acc_turned, g - R + 1)
                sp.dma_start(x[:, s, :], rows_of(table, g)).then_inc(loaded[s], 16)
                sp.dma_start(sums[:, s, :], rows_of(acc, g)).then_inc(loaded[s], 16)
            over_groups(sp, NG, (load, 0), ring=R)
            sp.wait_ge(spare_cleared, 32)

        @block.vector
        def _(dve):
            passed = ph.sem("dve_waits_passed")
            def norm_rows(g, s, k, back):
                dve.wait_ge(loaded[s], (k + 1) * 32)
                if back == R:
                    dve.wait_ge(turned, g - R + 1)
                for j in range(T):
                    c, at = slice(j * D, (j + 1) * D), bass.ds(g * T + j, 1)
                    i = nc.vector.tensor_scalar(xn[:, s, c], x[:, s, c], sh.mean[:, at], sh.scale[:, at],
                                                ALU.subtract, ALU.mult)
                i.then_inc(normed, 1)

            def reset_h(g, s, k, back):
                dve.wait_ge(r_ready, g + 1)
                nc.vector.tensor_tensor(r[:, s, :], r[:, s, :], hT[:, s, :], ALU.mult).then_inc(reset, 1)

            def add(g, s, k, back):
                dve.wait_ge(back_turned, g + 1)
                if back == R:
                    dve.wait_ge(stored[s], k * 16)
                nc.vector.tensor_tensor(new[:, s, :], psO[:, :], x[:, s, :], ALU.add).then_inc(added, 1)
            over_groups(dve, NG, (norm_rows, 0), (reset_h, 1), (add, 4), ring=R)

        @block.gpsimd
        def _(pool):
            passed = ph.sem("pool_waits_passed")
            def mix(g, s, k, back):
                pool.wait_ge(cand_ready, g + 1)
                pool.wait_ge(z_ready, g + 1)
                nc.gpsimd.tensor_tensor(t[:, s, :], t[:, s, :], hT[:, s, :], ALU.subtract).then_inc(mixing, 1)
                pool.wait_ge(mixing, g * 3 + 1)
                nc.gpsimd.tensor_tensor(t[:, s, :], t[:, s, :], z[:, s, :], ALU.mult).then_inc(mixing, 1)
                pool.wait_ge(mixing, g * 3 + 2)
                nc.gpsimd.tensor_tensor(t[:, s, :], t[:, s, :], hT[:, s, :], ALU.add).then_inc(mixing, 1)
            over_groups(pool, NG, (mix, 0), ring=R)

        @block.tensor
        def _(pe):
            pe.wait_ge(weights_in, 96)

            def turn(g, s, k, back):
                pe.wait_ge(loaded[s], (k + 1) * 32)
                if back:
                    pe.wait_ge(aT_ready, g)
                for j in range(T):
                    i = pe.transpose(psA[:, j * P:(j + 1) * P], sums[:, s, j * D:(j + 1) * D], sh.ident[:, :])
                i.then_inc(acc_turned, 1)
                pe.wait_ge(normed, g + 1)
                if back:
                    pe.wait_ge(hT_ready, g)
                for j in range(T):
                    i = pe.transpose(psH[:, j * P:(j + 1) * P], xn[:, s, j * D:(j + 1) * D], sh.ident[:, :])
                i.then_inc(turned, 1)

            def gates(g, s, k, back):
                pe.wait_ge(hT_ready, g + 1)
                pe.wait_ge(aT_ready, g + 1)
                for n, ps, read, done in (("r", psR, r_ready, r_in), ("z", psZ, z_ready, z_in)):
                    if back:
                        pe.wait_ge(read, g)
                    pe.matmul(ps[:, :], W[n][:, 0, :], hT[:, s, :], start=True, stop=False)
                    pe.matmul(ps[:, :], W[n][:, 1, :], aT[:, s, :], start=False, stop=True).then_inc(done, 1)

            def candidate(g, s, k, back):
                pe.wait_ge(reset, g + 1)
                if back:
                    pe.wait_ge(cand_ready, g)
                pe.matmul(psC[:, :], W["h"][:, 1, :], aT[:, s, :], start=True, stop=False)
                pe.matmul(psC[:, :], W["h"][:, 0, :], r[:, s, :], start=False, stop=True).then_inc(cand, 1)

            def turn_back(g, s, k, back):
                pe.wait_ge(mixing, (g + 1) * 3)
                if back:
                    pe.wait_ge(added, g)
                for j in range(T):
                    i = pe.transpose(psO[:, j * D:(j + 1) * D], t[:, s, j * P:(j + 1) * P], sh.ident[:, :])
                i.then_inc(back_turned, 1)
            over_groups(pe, NG, (gates, 1), (turn, 0), (candidate, 2), (turn_back, 4), ring=R)

        @block.scalar
        def _(act):
            act.wait_ge(weights_in, 96)

            def transposed(g, s, k, back):
                act.wait_ge(acc_turned, g + 1)
                if back == R:
                    act.wait_ge(cand, g - R + 1)
                    act.wait_ge(mixing, (g - R + 1) * 3)
                nc.scalar.activation(aT[:, s, :], psA[:, :], ACT.Copy).then_inc(aT_ready, 1)
                act.wait_ge(turned, g + 1)
                nc.scalar.activation(hT[:, s, :], psH[:, :], ACT.Relu).then_inc(hT_ready, 1)

            def squash(g, s, k, back):
                act.wait_ge(r_in, g + 1)
                if back == R:
                    act.wait_ge(cand, g - R + 1)
                    act.wait_ge(mixing, (g - R + 1) * 3)
                nc.scalar.activation(r[:, s, :], psR[:, :], ACT.Sigmoid, bias=B["r"][:, :]).then_inc(r_ready, 1)
                act.wait_ge(z_in, g + 1)
                nc.scalar.activation(z[:, s, :], psZ[:, :], ACT.Sigmoid, bias=B["z"][:, :]).then_inc(z_ready, 1)

            def bend(g, s, k, back):
                act.wait_ge(cand, g + 1)
                if back == R:
                    act.wait_ge(back_turned, g - R + 1)
                nc.scalar.activation(t[:, s, :], psC[:, :], ACT.Tanh, bias=B["h"][:, :]).then_inc(cand_ready, 1)

            def store(g, s, k, back):
                await_overlapped(act, stored, g)
                act.wait_ge(added, g + 1)
                act.dma_start(rows_of(out, g), new[:, s, :]).then_inc(stored[s], 16)
            over_groups(act, NG, (transposed, 0), (squash, 1), (bend, 2), (store, 5), ring=R)
            for s in range(R):
                act.wait_ge(stored[s], 16 * -(-(NG - s) // R))


def attend(nc, sh, tag, table, w, wT, a_cols, ends, src_rows, outside):
    with ExitStack() as ctx:
        keep = Phase(sh, tag, ctx)
        values = keep.sb("values", [P, EG, T * D])
        logit = keep.sb("logit", [P, EG * T])
        weight = keep.sb("weight", [P, EG * T])

        with ExitStack() as inner:
            ph = Phase(sh, tag, inner)
            W, WT, A = ph.sb("w", [P, D]), ph.sb("wT", [P, D]), ph.sb("a", [P, 2])
            spread, U = ph.sb("spread", [P, 2, D]), ph.sb("u", [P, 2, D])
            end = ph.sb("ends", [P, R, 2 * T], I32)
            x = ph.sb("x", [P, R, 2 * T, D])
            hT, product_junk = ph.sb("hT", [P, GW]), ph.sb("dots", [P, R, 2 * T, D])
            score = ph.sb("score", [P, R, 2 * T])
            stats, mv, rstd = ph.sb("stats", [P, 2 * T, 6]), ph.sb("mv", [P, 2 * T, 2]), ph.sb("rstd", [P, 2 * T])
            psT, psM, psU = ph.ps("psT", [P, GW]), ph.ps("psM", [P, GW]), ph.ps("psU", [P, 2, D])
            weights_in, spread_set, u_in, u_set = (ph.sem(n) for n in ("weights_in", "spread_set", "u_in", "u_set"))
            ends_in = [ph.sem(f"ends_in{s}") for s in range(R)]
            gathered = [ph.sem(f"rows_gathered{s}") for s in range(R)]
            own, measured, root_ready = ph.sem("norm_steps"), ph.sem("rows_measured"), ph.sem("root_ready")
            normed, turned, hT_ready = ph.sem("rows_normed"), ph.sem("rows_turned"), ph.sem("hT_ready")
            product, values_ready = ph.sem("product"), ph.sem("values_ready")
            scored, logits_set = ph.sem("scored"), ph.sem("logits_set")

            block = inner.enter_context(nc.Block())

            @block.sync
            def _(sp):
                sp.dma_start(W[:, :], w).then_inc(weights_in, 16)
                sp.dma_start(WT[:, :], wT).then_inc(weights_in, 16)
                sp.dma_start(A[:, :], a_cols).then_inc(weights_in, 16)

                def load(g, s, k, back):
                    if back == R:
                        sp.wait_ge(gathered[s], k * 128)
                    sp.dma_start(end[:, s, :], ends[g, :, SRC:SRC + 2 * T]).then_inc(ends_in[s], 16)
                over_groups(sp, EG, (load, 0))

            @block.gpsimd
            def _(pool):
                passed = ph.sem("pool_waits_passed")
                def gather(g, s, k, back):
                    pool.wait_ge(ends_in[s], (k + 1) * 16)
                    if back == R:
                        pool.wait_ge(turned, g - R + 1)
                        wait_apart(pool, scored, g - R + 1, passed)
                    for j in range(2 * T):
                        at = bass.IndirectOffsetOnAxis(ap=end[:, s, j:j + 1], axis=0)
                        pool.indirect_dma_start(x[:, s, j, :], None, table, at).then_inc(gathered[s], 16)
                over_groups(pool, EG, (gather, 0))

            @block.vector
            def _(dve):
                passed = ph.sem("dve_waits_passed")
                dve.wait_ge(weights_in, 48)
                for c in range(2):
                    i = nc.vector.tensor_copy(spread[:, c, :], A[:, c:c + 1].to_broadcast([P, D]))
                i.then_inc(spread_set, 1)
                dve.wait_ge(u_in, 1)
                nc.vector.tensor_copy(U[:, :, :], psU[:, :, :]).then_inc(u_set, 1)
                dve.wait_ge(u_set, 1)
                norms = Chain(dve, own, NORM_STEPS, passed)

                def norm_rows(g, s, k, back):
                    norms.start(g)
                    dve.wait_ge(gathered[s], (k + 1) * 128)
                    normalise(nc, norms, x[:, s], stats, mv, rstd, measured, root_ready, g).then_inc(normed, 1)
                    dve.wait_ge(normed, g + 1)
                    if back == R:
                        dve.wait_ge(logits_set, g - R + 1)
                    for j in range(2 * T):
                        i = nc.vector.scalar_tensor_tensor(product_junk[:, s, j, :], x[:, s, j, :], 0.0, U[:, j // T, :],
                                                           ALU.max, ALU.mult, accum_out=score[:, s, j:j + 1])
                    i.then_inc(scored, 1)

                def logits(g, s, k, back):
                    dve.wait_ge(scored, g + 1)
                    nc.vector.tensor_tensor(logit[:, bass.ds(g * T, T)], score[:, s, 0:T], score[:, s, T:2 * T], ALU.add
                                            ).then_inc(logits_set, 1)
                over_groups(dve, EG, (norm_rows, 0), (logits, 1))

            @block.tensor
            def _(pe):
                pe.wait_ge(weights_in, 48)
                pe.wait_ge(spread_set, 1)
                for c in range(2):
                    i = pe.matmul(psU[:, c, :], spread[:, c, :], WT[:, :], start=True, stop=True)
                i.then_inc(u_in, 1)

                def turn(g, s, k, back):
                    pe.wait_ge(normed, g + 1)
                    if back:
                        pe.wait_ge(hT_ready, g)
                    for j in range(T):
                        i = pe.transpose(psT[:, j * P:(j + 1) * P], x[:, s, T + j, :], sh.ident[:, :])
                    i.then_inc(turned, 1)

                def multiply(g, s, k, back):
                    pe.wait_ge(hT_ready, g + 1)
                    if back:
                        pe.wait_ge(values_ready, g)
                    for j in range(T):
                        i = pe.matmul(psM[:, j * D:(j + 1) * D], hT[:, j * P:(j + 1) * P], W[:, :], start=True, stop=True)
                    i.then_inc(product, 1)
                over_groups(pe, EG, (turn, 0), (multiply, 0))

            @block.scalar
            def _(act):
                def transposed(g, s, k, back):
                    act.wait_ge(measured, g + 1)
                    nc.scalar.activation(rstd[:, :], mv[:, :, 1], ACT.Sqrt, bias=sh.eps[:, :]).then_inc(root_ready, 1)
                    act.wait_ge(turned, g + 1)
                    if back:
                        act.wait_ge(product, g)
                    nc.scalar.activation(hT[:, :], psT[:, :], ACT.Relu).then_inc(hT_ready, 1)

                def keep_values(g, s, k, back):
                    act.wait_ge(product, g + 1)
                    nc.scalar.activation(values[:, bass.ds(g, 1), :].rearrange("p o d -> p (o d)"), psM[:, :], ACT.Copy
                                         ).then_inc(values_ready, 1)
                over_groups(act, EG, (transposed, 0), (keep_values, 0))

        with ExitStack() as inner:
            ph = Phase(sh, tag + "softmax_", inner)
            pad = ph.sb("outside", [P, EG * T])
            top, all_top, minus, total, all_total, inverse = (ph.sb(n, [P, 1]) for n in (
                "top", "all_top", "minus_top", "total", "all_total", "inverse"))
            pad_in, steps = ph.sem("outside_in"), ph.sem("steps")
            block = inner.enter_context(nc.Block())

            @block.sync
            def _(sp):
                sp.dma_start(pad[:, :], outside).then_inc(pad_in, 16)

            @block.vector
            def _(dve):
                passed = ph.sem("dve_waits_passed")
                dve.wait_ge(pad_in, 16)
                nc.vector.tensor_tensor(logit[:, :], logit[:, :], pad[:, :], ALU.add).then_inc(steps, 1)
                dve.wait_ge(steps, 1)
                nc.vector.reduce_max(top[:, :], logit[:, :], AX_X).then_inc(steps, 1)
                dve.wait_ge(steps, 5)
                nc.vector.reciprocal(inverse[:, :], all_total[:, :]).then_inc(steps, 1)
                dve.wait_ge(steps, 6)
                nc.vector.tensor_scalar(weight[:, :], weight[:, :], inverse[:, 0:1], None, ALU.mult).then_inc(steps, 1)
                dve.wait_ge(steps, 7)

            @block.gpsimd
            def _(pool):
                passed = ph.sem("pool_waits_passed")
                pool.wait_ge(steps, 2)
                nc.gpsimd.partition_all_reduce(all_top[:, :], top[:, :], P, RMAX).then_inc(steps, 1)
                pool.wait_ge(steps, 4)
                nc.gpsimd.partition_all_reduce(all_total[:, :], total[:, :], P, RADD).then_inc(steps, 1)

            @block.scalar
            def _(act):
                minus_set = ph.sem("minus_set")
                act.wait_ge(steps, 3)
                nc.scalar.mul(minus[:, :], all_top[:, :], -1.0).then_inc(minus_set, 1)
                act.wait_ge(minus_set, 1)
                nc.scalar.activation(weight[:, :], logit[:, :], ACT.Exp, bias=minus[:, :], accum_out=total[:, :]
                                     ).then_inc(steps, 1)

        with ExitStack() as inner:
            ph = Phase(sh, tag + "sum_", inner)
            key, row = ph.sb("keys", [P, R, T], I32), ph.sb("key_row", [P, R, GW], I32)
            msg, sums = ph.sb("msg", [P, R, T, D]), ph.sb("sums", [P, R, T, D])
            eq = ph.sb("eq", [P, 2, block_at(T, T)])
            keyf, count, way = ph.sb("keyf", [P, R, T]), ph.sb("count", [P, T]), ph.sb("way", [P, R, T])
            to = ph.sb("to", [P, R, T], I32)
            psS = ph.ps("psS", [P, 2, GW])
            loaded = [ph.sem(f"keys_in{s}") for s in range(R)]
            united, msg_ready, summed = ph.sem("unite_steps"), ph.sem("msg_ready"), ph.sem("summed")
            sums_ready, landed = ph.sem("sums_ready"), ph.sem("scatters_landed")
            block = inner.enter_context(nc.Block())

            @block.sync
            def _(sp):
                def load(g, s, k, back):
                    if back == R:
                        sp.wait_ge(msg_ready, 2 * (g - R + 1))
                    sp.dma_start(key[:, s, :], ends[g, :, SRC_KEY:SRC_KEY + T]).then_inc(loaded[s], 16)
                    sp.dma_start(row[:, s, :], src_rows[bass.ds(g, 1), :].to_broadcast([P, GW])).then_inc(loaded[s], 16)
                over_groups(sp, EG, (load, 0))

            @block.vector
            def _(dve):
                passed = ph.sem("dve_waits_passed")
                unites = Chain(dve, united, UNITE_STEPS, passed)

                def unite_edges(g, s, k, back):
                    unites.start(g)
                    dve.wait_ge(loaded[s], (k + 1) * 32)
                    if back >= 2:
                        dve.wait_ge(summed, g - 1)
                    unite(nc, sh, unites, T, eq[:, s % 2], row[:, s], key[:, s], keyf[:, s], count, way[:, s])

                def messages(g, s, k, back):
                    if back == R:
                        dve.wait_ge(landed, (g - R + 1) * 64)
                    nc.vector.tensor_tensor(to[:, s, :], way[:, s, :], keyf[:, s, :], ALU.add).then_inc(msg_ready, 1)
                    for j in range(T):
                        i = nc.vector.tensor_scalar(msg[:, s, j, :], values[:, bass.ds(g, 1), j * D:(j + 1) * D].rearrange("p o d -> p (o d)"),
                                                    weight[:, bass.ds(g * T + j, 1)], None, ALU.mult)
                    i.then_inc(msg_ready, 1)
                over_groups(dve, EG, (unite_edges, 0), (messages, 0))

            @block.tensor
            def _(pe):
                def add_up(g, s, k, back):
                    pe.wait_ge(msg_ready, 2 * (g + 1))
                    if back >= 2:
                        pe.wait_ge(sums_ready, g - 1)
                    batch_sums(pe, T, lambda j: psS[:, s % 2, j * D:(j + 1) * D], eq[:, s % 2], msg[:, s], D
                               ).then_inc(summed, 1)
                over_groups(pe, EG, (add_up, 0))

            @block.scalar
            def _(act):
                def sums_out(g, s, k, back):
                    act.wait_ge(summed, g + 1)
                    if back == R:
                        act.wait_ge(landed, (g - R + 1) * 64)
                    nc.scalar.activation(sums[:, s, :, :].rearrange("p j d -> p (j d)"), psS[:, s % 2, :], ACT.Copy
                                         ).then_inc(sums_ready, 1)
                over_groups(act, EG, (sums_out, 0))

            @block.gpsimd
            def _(pool):
                passed = ph.sem("pool_waits_passed")
                def scatter(g, s, k, back):
                    pool.wait_ge(sums_ready, g + 1)
                    wait_apart(pool, msg_ready, 2 * (g + 1), passed)
                    if back:
                        wait_apart(pool, landed, g * 64, passed)
                    for j in range(T):
                        at = bass.IndirectOffsetOnAxis(ap=to[:, s, j:j + 1], axis=0)
                        pool.indirect_dma_start(table, at, sums[:, s, j, :], None, compute_op=ALU.add
                                                ).then_inc(landed, 16)
                over_groups(pool, EG, (scatter, 0))
                pool.wait_ge(landed, EG * 64)


def dram(nc, name, rows, w=D):
    return nc.dram_tensor(name, (rows, w), F32, kind="Internal").ap()


def gnn_stack(nc, a, out):
    h1, x1, x2 = (dram(nc, n, N) for n in ("h1", "x1", "x2"))
    acc1 = dram(nc, "acc1", ROWS, CW)
    acc2, acc3, acc4 = (dram(nc, n, ROWS) for n in ("acc2", "acc3", "acc4"))
    x, ends, dst_rows, ew = a["x"], a["ends"], a["dst_rows"], a["edge_factor"]
    with ExitStack() as ctx:
        sh = Shared(nc, ctx)
        load_constants(nc, sh, a["ident"], a["before"], a["spare"])
        linear_edges(nc, sh, "edges1_", x, acc1, CW, a["gcn_w"][0, :, D:2 * D], ends, dst_rows, scale=ew, norm=True,
                     clear_first=True, clear_next=acc2)
        gcn_nodes(nc, sh, "nodes1_", x, acc1, CW, a["gcn_w"][0], a["gcn_b"][0], h1, norm=True)
        linear_edges(nc, sh, "edges2_", h1, acc2, D, a["gcn_w"][1, :, D:2 * D], ends, dst_rows, scale=ew, clear_next=acc3)
        gcn_nodes(nc, sh, "nodes2_", h1, acc2, D, a["gcn_w"][1], a["gcn_b"][1], x1,
                  last_layer=(x, a["agg_wT"], a["agg_b"]))
        linear_edges(nc, sh, "edges3_", x1, acc3, D, a["mean_wT"], ends, dst_rows, norm=True, bias=a["mean_b"],
                     clear_next=acc4)
        mean_nodes(nc, sh, "nodes3_", x1, acc3, x2)
        mlp_edges(nc, sh, "edges4_", x2, acc4, a["w_msg1"], a["b_msg1"], a["w_msg2"], a["b_msg2"], ends, dst_rows,
                  a["attrT"])
        gated_nodes(nc, sh, "nodes4_", x2, acc4, a["w_z"], a["w_r"], a["w_h"], a["b_z"], a["b_r"], a["b_h"], out)
        attend(nc, sh, "attend_", out, a["att_w"], a["att_wT"], a["att_a"], ends, a["src_rows"], a["outside"])


def kernel(x, src, dst, edge_attr_4, edge_weight, L0_gnn_W_self, L0_gnn_b_self, L0_gnn_W_neigh, L0_gnn_b_neigh,
           L0_gnn_layer_bias, L0_gnn_W_agg, L0_gnn_b_agg, L1_gnn_W, L1_gnn_b, L2_gnn_W_msg1, L2_gnn_b_msg1,
           L2_gnn_W_msg2, L2_gnn_b_msg2, L2_gnn_W_z, L2_gnn_b_z, L2_gnn_W_r, L2_gnn_b_r, L2_gnn_W_h, L2_gnn_b_h,
           L3_gnn_W, L3_gnn_a):
    import numpy as np
    import concourse.bacc as bacc
    from concourse.bass_utils import run_bass_kernel_spmd

    def padded(v, fill):
        return np.concatenate([np.asarray(v), np.full((EG * GW - E,) + v.shape[1:], fill, v.dtype)])

    def by_tile(v):
        return v.reshape(EG, T, P).transpose(0, 2, 1)

    src_key, dst_key = padded(src, PAD_ROW), padded(dst, PAD_ROW)
    position = np.arange(EG * GW).reshape(EG * T, P).T
    arrays = {
        "x": x,
        "ends": np.concatenate([by_tile(v) for v in (padded(src, 0), padded(dst, 0), dst_key, src_key)], 2),
        "dst_rows": dst_key.reshape(EG, GW),
        "src_rows": src_key.reshape(EG, GW),
        "edge_factor": by_tile(padded(edge_weight, 0)),
        "attrT": padded(edge_attr_4, 0).T,
        "ident": np.eye(P, dtype=np.float32),
        "before": np.concatenate([np.ones((P, 3 * P)), np.tril(np.ones((P, P)), -1)], 1).astype(np.float32),
        "spare": (N + np.arange(GW).reshape(T, P).T).astype(np.float32),
        "outside": np.where(position < E, 0.0, OUTSIDE).astype(np.float32),
        "gcn_w": np.concatenate([np.transpose(L0_gnn_W_self, (0, 2, 1)), np.transpose(L0_gnn_W_neigh, (0, 2, 1))], 2),
        "gcn_b": np.stack([L0_gnn_b_self, L0_gnn_b_neigh, L0_gnn_layer_bias], 1),
        "agg_wT": np.transpose(L0_gnn_W_agg), "agg_b": np.reshape(L0_gnn_b_agg, (1, D)),
        "mean_wT": np.transpose(L1_gnn_W), "mean_b": np.reshape(L1_gnn_b, (1, D)),
        "w_msg1": L2_gnn_W_msg1, "b_msg1": np.reshape(L2_gnn_b_msg1, (D, 1)),
        "w_msg2": L2_gnn_W_msg2, "b_msg2": np.reshape(L2_gnn_b_msg2, (1, D)),
        "w_z": L2_gnn_W_z, "b_z": np.reshape(L2_gnn_b_z, (D, 1)),
        "w_r": L2_gnn_W_r, "b_r": np.reshape(L2_gnn_b_r, (D, 1)),
        "w_h": L2_gnn_W_h, "b_h": np.reshape(L2_gnn_b_h, (D, 1)),
        "att_w": L3_gnn_W, "att_wT": np.transpose(L3_gnn_W), "att_a": np.reshape(L3_gnn_a, (2, D)).T,
    }
    nc = bacc.Bacc("TRN2", target_bir_lowering=False, num_devices=1)
    given, aps = {}, {}
    for name, v in arrays.items():
        v = np.ascontiguousarray(v)
        given[f"in_{name}"] = v
        aps[name] = nc.dram_tensor(f"in_{name}", v.shape, mybir.dt.from_np(v.dtype), kind="ExternalInput").ap()
    out = nc.dram_tensor("out", (PAD_ROW + 1, D), F32, kind="ExternalOutput").ap()
    gnn_stack(nc, aps, out)
    result = run_bass_kernel_spmd(nc, [given], core_ids=[0])
    return result.results[0]["out"][0:N]
```

```python
from contextlib import ExitStack

import concourse.bass as bass
from concourse import mybir

ALU = mybir.AluOpType
ACT = mybir.ActivationFunctionType
F32 = mybir.dt.float32
I32 = mybir.dt.int32
AX_X = mybir.AxisListType.X
RMAX = bass.bass_isa.ReduceOp.max
RADD = bass.bass_isa.ReduceOp.add

P = 128
D = 128
T = 4
R = 4
GW = P * T
N = 50000
E = 25000
EG = -(-E // GW)
NG = -(-N // GW)
PAD_ROW = N + GW
ZR = -(-(PAD_ROW + 1) // (P * EG))
ROWS = ZR * P * EG
CW = D + 4
ZW = 4096
EPS = 1e-5
SLOPE = 0.2
OUTSIDE = -3e38

SRC, DST, DST_KEY, SRC_KEY = 0, T, 2 * T, 3 * T


def over_groups(eng, n, *parts, last=0, ring=R):
    R = ring
    latest = max(delay for _, delay in parts)
    ahead = max(0, -min(delay for _, delay in parts))
    first, end = -(-(R + latest) // R) * R, (n - ahead - last) // R * R

    def peeled(i):
        for part, delay in parts:
            g = i - delay
            if 0 <= g < n:
                part(g, g % R, g // R, min(g, R))

    for i in range(-ahead, first):
        peeled(i)
    with eng.Fori(first // R, end // R) as k:
        for s in range(R):
            for part, delay in parts:
                g = s - delay
                part(k * R + g, g % R, k + g // R, R)
    for i in range(end, n + latest):
        peeled(i)


def wait_apart(eng, sem, value, passed):
    eng.wait_ge(sem, value)
    eng.sem_inc(passed, 1)


def await_overlapped(eng, stored, g, per_store=16):
    if isinstance(g, int) and g == NG - 1:
        before = g - 1
        eng.wait_ge(stored[before % len(stored)], per_store * (before // len(stored) + 1))


class Chain:

    def __init__(self, eng, sem, per_group, passed):
        self.passed = passed
        self.eng, self.sem, self.per_group, self.n = eng, sem, per_group, per_group

    def start(self, g):
        assert self.n == self.per_group
        self.base, self.n = g * self.per_group, 0

    def done(self, instruction, apart=False):
        instruction.then_inc(self.sem, 1)
        self.n += 1
        if apart:
            wait_apart(self.eng, self.sem, self.base + self.n, self.passed)
        else:
            self.eng.wait_ge(self.sem, self.base + self.n)


def tiled(ap):
    return ap.rearrange("p (j d) -> p j d", j=T)


def rows_of(table, g, w=D):
    first = N - GW if isinstance(g, int) and g == NG - 1 else g * GW
    return table[bass.ds(first, GW), 0:w].rearrange("(p j) d -> p (j d)", j=T)


class Shared:

    def __init__(self, nc, ctx):
        self.nc, self.ctx = nc, ctx
        self.ident = self.keep("ident", [P, P])
        self.before = self.keep("before", [P, GW])
        self.spare = self.keep("spare", [P, T])
        self.zeros = self.keep("zeros", [P, ZW])
        self.degree = self.keep("degree", [P, NG * T])
        self.share = self.keep("share", [P, EG * T])
        self.lanes = self.keep("lanes", [P, P])
        self.columns = self.keep("columns", [P, NG * T])
        self.mean = self.keep("mean", [P, NG * T])
        self.scale = self.keep("scale", [P, NG * T])
        self.eps = self.keep("eps", [P, 1])
        self.junk = self.keep("junk", [P, T, GW])

    def keep(self, name, shape, dt=F32):
        return self.ctx.enter_context(self.nc.sbuf_tensor(name, shape, dt))

    def sem(self, name):
        return self.ctx.enter_context(self.nc.semaphore(name))


class Phase:

    def __init__(self, sh, tag, ctx):
        self.nc, self.tag, self.ctx, self.sems = sh.nc, tag, ctx, []
        ctx.callback(self.end)

    def sb(self, name, shape, dt=F32):
        return self.ctx.enter_context(self.nc.sbuf_tensor(self.tag + name, shape, dt))

    def ps(self, name, shape):
        return self.ctx.enter_context(self.nc.psum_tensor(self.tag + name, shape, F32))

    def sem(self, name):
        self.sems.append(self.nc.alloc_semaphore(name=self.tag + name))
        return self.sems[-1]

    def end(self):
        if self.sems:
            self.nc.clear_and_free_semaphores(self.sems)
            self.nc.all_engine_barrier()


def load_constants(nc, sh, ident, before, spare, counting):
    loaded, cleared = sh.sem("constants_loaded"), sh.sem("zeros_set")
    with nc.Block() as block:
        @block.sync
        def _(sp):
            sp.dma_start(sh.ident[:, :], ident).then_inc(loaded, 16)
            sp.dma_start(sh.before[:, :], before).then_inc(loaded, 16)
            sp.dma_start(sh.spare[:, :], spare).then_inc(loaded, 16)
            sp.dma_start(sh.lanes[:, :], counting[:, 0:P].to_broadcast([P, P])).then_inc(loaded, 16)
            sp.dma_start(sh.columns[:, :], counting[:, 0:NG * T].to_broadcast([P, NG * T])).then_inc(loaded, 16)
            sp.wait_ge(loaded, 80)

        @block.vector
        def _(dve):
            nc.vector.memset(sh.eps[:, :], EPS).then_inc(cleared, 1)
            nc.vector.memset(sh.zeros[:, :], 0.0).then_inc(cleared, 1)
            dve.wait_ge(cleared, 2)


NORM_STEPS = 2


def normalise(nc, chain, x, stats, mv, rstd, measured, root_ready, g):
    n = x.shape[1]
    for j in range(n):
        last = nc.vector.bn_stats(stats[:, j, :], x[:, j, :])
    chain.done(last, apart=True)
    for j in range(n):
        last = nc.vector.bn_aggr(mv[:, j, :], stats[:, j, :])
    last.then_inc(measured, 1)
    chain.eng.wait_ge(root_ready, g + 1)
    chain.done(nc.vector.reciprocal(rstd[:, 0:n], rstd[:, 0:n]))
    for j in range(n):
        last = nc.vector.tensor_scalar(x[:, j, :], x[:, j, :], mv[:, j, 0:1], rstd[:, j:j + 1],
                                       ALU.subtract, ALU.mult)
    return last


UNITE_STEPS = 5


def block_at(batch, b, a=0):
    return (b * (b + 1) // 2 + a) * P


def unite(nc, sh, chain, batch, eq, row, key, keyf, count, way):
    size = block_at(batch, batch)
    chain.done(nc.vector.tensor_copy(keyf, key))
    for j in range(T):
        first, b = j // batch * batch, j % batch
        at = j // batch * size + block_at(batch, b)
        last = nc.vector.tensor_scalar(eq[:, at:at + (b + 1) * P], row[:, first * P:(j + 1) * P],
                                       keyf[:, j:j + 1], None, ALU.is_equal)
    chain.done(last)
    chain.done(nc.vector.tensor_tensor(way, sh.spare[:, :], keyf, ALU.subtract))
    for j in range(T):
        b = j % batch
        at = j // batch * size + block_at(batch, b)
        last = nc.vector.tensor_tensor_reduce(
            sh.junk[:, j, 0:(b + 1) * P], eq[:, at:at + (b + 1) * P], sh.before[:, (T - 1 - b) * P:GW],
            1.0, 0.0, ALU.mult, ALU.add, count[:, j:j + 1])
    chain.done(last)
    chain.done(nc.vector.scalar_tensor_tensor(way, count[:, :], 0.0, way, ALU.is_gt, ALU.mult))


def batch_sums(pe, batch, out, eq, msg, w):
    size = block_at(batch, batch)
    for j in range(T):
        first, a = j // batch * batch, j % batch
        for b in range(a, batch):
            at = j // batch * size + block_at(batch, b, a)
            last = pe.matmul(out(j), eq[:, at:at + P], msg[:, first + b, 0:w], start=(b == a), stop=(b == batch - 1))
    return last


class Lookup:

    def __init__(self, ph, sh, table, nodes):
        self.sh, self.table, self.nodes = sh, table, nodes
        self.keys, self.places = ph.sb("all_keys", [P, EG * T], I32), ph.sb("places", [P, EG * T], I32)
        self.lane, self.column = ph.sb("lane", [P, EG * T]), ph.sb("column", [P, EG * T])
        self.mark, self.markT = ph.sb("mark", [P, R, GW]), ph.sb("markT", [P, R, GW])
        self.chosen, self.value = ph.sb("chosen", [P, T, NG * T]), ph.sb("value", [P, R, T])
        self.result = ph.sb("result", [P, EG * T])
        self.psE, self.psL = ph.ps("psE", [P, GW]), ph.ps("psL", [P, T, GW])
        self.keys_in, self.placed = ph.sem("all_keys_in"), ph.sem("placed")
        self.marked, self.turned, self.markT_ready = ph.sem("marked"), ph.sem("marks_turned"), ph.sem("markT_ready")
        self.looked, self.found, self.noted = ph.sem("looked"), ph.sem("found"), ph.sem("noted")

    def load(self, sp):
        sp.dma_start(self.keys[:, :], self.nodes).then_inc(self.keys_in, 16)

    def place(self, nc, dve):
        keys, places, placed = self.keys[:, :], self.places[:, :], self.placed
        last_group = (NG - 1) * GW
        dve.wait_ge(self.keys_in, 16)
        nc.vector.tensor_scalar(places, keys, last_group, last_group - (N - GW), ALU.is_ge, ALU.mult).then_inc(placed, 1)
        dve.wait_ge(placed, 1)
        nc.vector.tensor_tensor(keys, keys, places, ALU.add).then_inc(placed, 1)
        dve.wait_ge(placed, 2)
        nc.vector.tensor_scalar(places, keys, 2, P - 1, ALU.logical_shift_right, ALU.bitwise_and).then_inc(placed, 1)
        dve.wait_ge(placed, 3)
        nc.vector.tensor_copy(self.lane[:, :], places).then_inc(placed, 1)
        dve.wait_ge(placed, 4)
        nc.vector.tensor_scalar(places, keys, 9, 2, ALU.logical_shift_right, ALU.logical_shift_left).then_inc(placed, 1)
        nc.vector.tensor_scalar(keys, keys, T - 1, None, ALU.bitwise_and).then_inc(placed, 1)
        dve.wait_ge(placed, 6)
        nc.vector.tensor_tensor(self.column[:, :], places, keys, ALU.add).then_inc(placed, 1)
        dve.wait_ge(placed, 7)

    def vector_parts(self, nc, dve):
        def mark(g, s, k, back):
            if back == R:
                dve.wait_ge(self.turned, g - R + 1)
            for j in range(T):
                i = nc.vector.tensor_scalar(self.mark[:, s, j * P:(j + 1) * P], self.sh.lanes[:, :],
                                            self.lane[:, bass.ds(g * T + j, 1)], None, ALU.is_equal)
            i.then_inc(self.marked, 1)

        def choose(g, s, k, back):
            dve.wait_ge(self.looked, g + 1)
            if back == R:
                dve.wait_ge(self.noted, g - R + 1)
            for j in range(T):
                i = nc.vector.scalar_tensor_tensor(
                    self.chosen[:, j, :], self.sh.columns[:, :], self.column[:, bass.ds(g * T + j, 1)],
                    self.psL[:, j, 0:NG * T], ALU.is_equal, ALU.mult, accum_out=self.value[:, s, j:j + 1])
            i.then_inc(self.found, 1)

        def note(g, s, k, back):
            dve.wait_ge(self.found, g + 1)
            nc.vector.tensor_copy(self.result[:, bass.ds(g * T, T)], self.value[:, s, :]).then_inc(self.noted, 1)
        return (mark, 0), (choose, 3), (note, 4)

    def tensor_parts(self, pe):
        def turn_marks(g, s, k, back):
            pe.wait_ge(self.marked, g + 1)
            if back:
                pe.wait_ge(self.markT_ready, g)
            for j in range(T):
                i = pe.transpose(self.psE[:, j * P:(j + 1) * P], self.mark[:, s, j * P:(j + 1) * P], self.sh.ident[:, :])
            i.then_inc(self.turned, 1)

        def look(g, s, k, back):
            pe.wait_ge(self.markT_ready, g + 1)
            if back:
                pe.wait_ge(self.found, g)
            for j in range(T):
                i = pe.matmul(self.psL[:, j, 0:NG * T], self.markT[:, s, j * P:(j + 1) * P], self.table[:, :],
                              start=True, stop=True)
            i.then_inc(self.looked, 1)
        return (look, 2), (turn_marks, 1)

    def scalar_parts(self, nc, act):
        def turned_marks(g, s, k, back):
            act.wait_ge(self.turned, g + 1)
            if back == R:
                act.wait_ge(self.looked, g - R + 1)
            nc.scalar.activation(self.markT[:, s, :], self.psE[:, :], ACT.Copy).then_inc(self.markT_ready, 1)
        return ((turned_marks, 1),)


def linear_edges(nc, sh, tag, table, acc, w, weight, ends, dst_rows, scale=None, norm=False, bias=None,
                 clear_first=False, clear_next=None,
                 find_share=None, share=False):
    with ExitStack() as ctx:
        ph = Phase(sh, tag, ctx)
        W, B = ph.sb("weight", [P, D]), ph.sb("bias", [P, D])
        end, key = ph.sb("ends", [P, R, T], I32), ph.sb("keys", [P, R, T], I32)
        row = ph.sb("key_row", [P, R, GW], I32)
        factor = ph.sb("factor", [P, R, T])
        x = ph.sb("x", [P, R, T, D])
        hT = ph.sb("hT", [P, GW])
        msg = ph.sb("msg", [P, R, T, w])
        eq = ph.sb("eq", [P, R, block_at(T, T)])
        keyf, count, way = ph.sb("keyf", [P, R, T]), ph.sb("count", [P, T]), ph.sb("way", [P, R, T])
        stats, mv, rstd = ph.sb("stats", [P, T, 6]), ph.sb("mv", [P, T, 2]), ph.sb("rstd", [P, T])
        to = ph.sb("to", [P, R, T], I32)
        sums = ph.sb("sums", [P, R, T, w])
        halves = -(-T * w // GW)
        psT, psM, psS = ph.ps("psT", [P, GW]), ph.ps("psM", [P, GW]), ph.ps("psS", [P, halves, GW])
        if find_share is not None:
            find = Lookup(ph, sh, sh.degree, find_share)

        weights_in = ph.sem("weights_in")
        ends_in = [ph.sem(f"ends_in{s}") for s in range(R)]
        loaded = [ph.sem(f"keys_in{s}") for s in range(R)]
        gathered = [ph.sem(f"rows_gathered{s}") for s in range(R)]
        cleared, next_cleared = ph.sem("acc_cleared"), ph.sem("next_cleared")
        ones_set, own, united, normed = ph.sem("ones_set"), ph.sem("norm_steps"), ph.sem("unite_steps"), ph.sem("rows_normed")
        measured, root_ready = ph.sem("rows_measured"), ph.sem("root_ready")
        turned, hT_ready, product = ph.sem("rows_turned"), ph.sem("hT_ready"), ph.sem("product")
        msg_ready, summed, sums_ready = ph.sem("msg_ready"), ph.sem("summed"), ph.sem("sums_ready")
        landed, shared = ph.sem("scatters_landed"), ph.sem("shared")
        per_load = 16 * (3 if scale is not None else 2)
        n_weights = 16 * (1 if bias is None else 2)
        clears = -(-ROWS * w // P // ZW)

        block = ctx.enter_context(nc.Block())

        @block.sync
        def _(sp):
            sp.dma_start(W[:, :], weight).then_inc(weights_in, 16)
            if find_share is not None:
                find.load(sp)
            if bias is not None:
                sp.dma_start(B[:, :], bias.to_broadcast([P, D])).then_inc(weights_in, 16)

            def load(g, s, k, back):
                if back == R:
                    sp.wait_ge(gathered[s], k * 64)
                sp.dma_start(end[:, s, :], ends[g, :, SRC:SRC + T]).then_inc(ends_in[s], 16)
                if back == R:
                    sp.wait_ge(msg_ready, 2 * (g - R + 1))
                sp.dma_start(key[:, s, :], ends[g, :, DST_KEY:DST_KEY + T]).then_inc(loaded[s], 16)
                sp.dma_start(row[:, s, :], dst_rows[bass.ds(g, 1), :].to_broadcast([P, GW])).then_inc(loaded[s], 16)
                if scale is not None:
                    sp.dma_start(factor[:, s, :], scale[g, :, :]).then_inc(loaded[s], 16)
                if clear_next is not None:
                    part = clear_next[bass.ds(g * (P * ZR), P * ZR), :]
                    sp.dma_start(part.rearrange("(p r) d -> p (r d)", p=P), sh.zeros[:, 0:ZR * part.shape[1]]
                                 ).then_inc(next_cleared, 16)
            over_groups(sp, EG, (load, 0))
            if clear_next is not None:
                sp.wait_ge(next_cleared, 16 * EG)

        @block.gpsimd
        def _(pool):
            passed = ph.sem("pool_waits_passed")
            def gather(s, j):
                at = bass.IndirectOffsetOnAxis(ap=end[:, s, j:j + 1], axis=0)
                pool.indirect_dma_start(x[:, s, j, :], None, table, at).then_inc(gathered[s], 16)

            for s in range(R):
                pool.wait_ge(ends_in[s], 16)
                for j in range(T):
                    gather(s, j)
            if clear_first:
                pool.wait_ge(cleared, 16 * clears)

            def scatter(g, s, k, back):
                ahead = not isinstance(g, int) or g + R < EG
                pool.wait_ge(sums_ready, g + 1)
                wait_apart(pool, msg_ready, 2 * (g + 1), passed)
                if ahead:
                    pool.wait_ge(ends_in[s], (k + 2) * 16)
                    wait_apart(pool, turned, g + 1, passed)
                for j in range(T):
                    at = bass.IndirectOffsetOnAxis(ap=to[:, s, j:j + 1], axis=0)
                    pool.indirect_dma_start(acc, at, sums[:, s, j, :], None, compute_op=ALU.add).then_inc(landed, 16)
                if ahead:
                    for j in range(T):
                        gather(s, j)
                wait_apart(pool, landed, (g + 1) * 64, passed)
            over_groups(pool, EG, (scatter, 0), last=R)

        @block.vector
        def _(dve):
            passed = ph.sem("dve_waits_passed")
            norms = Chain(dve, own, NORM_STEPS, passed)
            unites = Chain(dve, united, UNITE_STEPS, passed)
            nc.vector.memset(msg[:, :, :, :], 1.0).then_inc(ones_set, 1)
            dve.wait_ge(ones_set, 1)
            dve.wait_ge(weights_in, n_weights)

            def norm_rows(g, s, k, back):
                norms.start(g)
                dve.wait_ge(gathered[s], (k + 1) * 64)
                normalise(nc, norms, x[:, s], stats, mv, rstd, measured, root_ready, g).then_inc(normed, 1)

            def unite_edges(g, s, k, back):
                unites.start(g)
                dve.wait_ge(loaded[s], (k + 1) * per_load)
                if back == R:
                    dve.wait_ge(summed, g - R + 1)
                unite(nc, sh, unites, T, eq[:, s], row[:, s], key[:, s], keyf[:, s], count, way[:, s])

            def messages(g, s, k, back):
                dve.wait_ge(product, g + 1)
                if back == R:
                    dve.wait_ge(landed, (g - R + 1) * 64)
                nc.vector.tensor_tensor(to[:, s, :], way[:, s, :], keyf[:, s, :], ALU.add).then_inc(msg_ready, 1)
                if scale is not None:
                    by = factor[:, s, :].unsqueeze(2).to_broadcast([P, T, D])
                    last = nc.vector.tensor_tensor(msg[:, s, :, 0:D], tiled(psM[:, :]), by, ALU.mult)
                else:
                    by = B[:, :].unsqueeze(1).to_broadcast([P, T, D])
                    last = nc.vector.tensor_tensor(msg[:, s, :, 0:D], tiled(psM[:, :]), by, ALU.add)
                last.then_inc(msg_ready, 1)
            if find_share is not None:
                find.place(nc, dve)
            over_groups(dve, EG, *([(norm_rows, 0)] if norm else []), (messages, 1), (unite_edges, -1),
                        *(find.vector_parts(nc, dve) if find_share is not None else []))
            if find_share is not None:
                edge_share = find.result
                dve.wait_ge(find.noted, EG)
                nc.vector.tensor_scalar(edge_share[:, :], edge_share[:, :], 1.0, None, ALU.max).then_inc(shared, 1)
                dve.wait_ge(shared, 1)
                nc.vector.reciprocal(sh.share[:, :], edge_share[:, :]).then_inc(shared, 1)
                dve.wait_ge(shared, 2)

        @block.tensor
        def _(pe):
            pe.wait_ge(weights_in, n_weights)

            def turn(g, s, k, back):
                if norm:
                    pe.wait_ge(normed, g + 1)
                else:
                    pe.wait_ge(gathered[s], (k + 1) * 64)
                if back:
                    pe.wait_ge(hT_ready, g)
                for j in range(T):
                    last = pe.transpose(psT[:, j * P:(j + 1) * P], x[:, s, j, :], sh.ident[:, :])
                last.then_inc(turned, 1)

            def multiply(g, s, k, back):
                pe.wait_ge(hT_ready, g + 1)
                if back:
                    pe.wait_ge(msg_ready, 2 * g)
                for j in range(T):
                    last = pe.matmul(psM[:, j * D:(j + 1) * D], hT[:, j * P:(j + 1) * P], W[:, :],
                                     start=True, stop=True)
                last.then_inc(product, 1)

            def add_up(g, s, k, back):
                pe.wait_ge(msg_ready, 2 * (g + 1))
                if back:
                    pe.wait_ge(sums_ready, g)
                per = T // halves
                batch_sums(pe, T, lambda j: psS[:, j // per, j % per * w:(j % per + 1) * w], eq[:, s], msg[:, s], w
                           ).then_inc(summed, 1)
            over_groups(pe, EG, (turn, 0), (add_up, 1), (multiply, 0), *(find.tensor_parts(pe) if find_share is not None else []))

        @block.scalar
        def _(act):
            if clear_first:
                flat = acc.rearrange("(p r) d -> p (r d)", p=P)
                for c in range(clears):
                    m = min(ZW, flat.shape[1] - c * ZW)
                    act.dma_start(flat[:, c * ZW:c * ZW + m], sh.zeros[:, 0:m]).then_inc(cleared, 16)

            def transposed(g, s, k, back):
                if norm:
                    act.wait_ge(measured, g + 1)
                    nc.scalar.activation(rstd[:, :], mv[:, :, 1], ACT.Sqrt, bias=sh.eps[:, :]).then_inc(root_ready, 1)
                act.wait_ge(turned, g + 1)
                if back:
                    act.wait_ge(product, g)
                nc.scalar.activation(hT[:, :], psT[:, :], ACT.Relu if norm else ACT.Copy).then_inc(hT_ready, 1)

            def sums_out(g, s, k, back):
                act.wait_ge(summed, g + 1)
                if back == R:
                    act.wait_ge(landed, (g - R + 1) * 64)
                if share:
                    for j in range(T):
                        i = nc.scalar.activation(sums[:, s, j, :], psS[:, 0, j * D:(j + 1) * D], ACT.Copy,
                                                 scale=sh.share[:, bass.ds(g * T + j, 1)])
                else:
                    i = nc.scalar.activation(sums[:, s, :, :].rearrange("p (q j) d -> p q (j d)", q=halves),
                                             psS[:, :, 0:T // halves * w], ACT.Copy)
                i.then_inc(sums_ready, 1)
            over_groups(act, EG, (transposed, 0), (sums_out, 1), *(find.scalar_parts(nc, act) if find_share is not None else []))


class Measure:

    def __init__(self, ph, sh, table):
        assert NG == 2 * EG
        self.sh, self.table = sh, table
        self.x, self.stats = ph.sb("all_x", [P, R, 2 * T, D]), ph.sb("all_stats", [P, R, 2 * T, 6])
        self.mv, self.root = ph.sb("all_mv", [P, R, 2 * T, 2]), ph.sb("all_root", [P, R, 2 * T])
        self.loaded = [ph.sem(f"all_rows_in{s}") for s in range(R)]
        self.counted, self.measured, self.rooted, self.kept = (ph.sem(n) for n in (
            "all_counted", "all_measured", "all_rooted", "all_kept"))

    def load(self, sp, g, s, back):
        if back == R:
            sp.wait_ge(self.counted, g - R + 1)
        for half in range(2):
            rows = self.x[:, s, half * T:(half + 1) * T, :].rearrange("p j d -> p (j d)")
            sp.dma_start(rows, rows_of(self.table, g * 2 + half)).then_inc(self.loaded[s], 16)

    def vector_parts(self, nc, dve, passed):
        def count(g, s, k, back):
            dve.wait_ge(self.loaded[s], (k + 1) * 32)
            if back == R:
                dve.wait_ge(self.measured, g - R + 1)
            for j in range(2 * T):
                i = nc.vector.bn_stats(self.stats[:, s, j, :], self.x[:, s, j, :])
            i.then_inc(self.counted, 1)

        def measure(g, s, k, back):
            wait_apart(dve, self.counted, g + 1, passed)
            for j in range(2 * T):
                i = nc.vector.bn_aggr(self.mv[:, s, j, :], self.stats[:, s, j, :])
            i.then_inc(self.measured, 1)

        def keep(g, s, k, back):
            at = bass.ds(g * (2 * T), 2 * T)
            dve.wait_ge(self.measured, g + 1)
            dve.wait_ge(self.rooted, g + 1)
            nc.vector.tensor_copy(self.sh.mean[:, at], self.mv[:, s, :, 0]).then_inc(self.kept, 1)
            nc.vector.reciprocal(self.sh.scale[:, at], self.root[:, s, :]).then_inc(self.kept, 1)
        return count, measure, keep

    def take_root(self, nc, act):
        def take_root(g, s, k, back):
            act.wait_ge(self.measured, g + 1)
            if back == R:
                act.wait_ge(self.kept, 2 * (g - R + 1))
            nc.scalar.activation(self.root[:, s, :], self.mv[:, s, :, 1], ACT.Sqrt, bias=self.sh.eps[:, :]
                                 ).then_inc(self.rooted, 1)
        return take_root


def mlp_edges(nc, sh, tag, table, acc, w1, b1, w2, b2, ends, dst_rows, attrT):
    with ExitStack() as ctx:
        ph = Phase(sh, tag, ctx)
        W1s, W1d, W2, B2 = (ph.sb(n, [P, D]) for n in ("w1_src", "w1_dst", "w2", "b2"))
        W1e, B1 = ph.sb("w1_attr", [T, D]), ph.sb("b1", [P, 1])
        end, key = ph.sb("ends", [P, R, 2 * T], I32), ph.sb("keys", [P, R, T], I32)
        row = ph.sb("key_row", [P, R, GW], I32)
        attr = ph.sb("attr", [4, R, GW])
        x = ph.sb("x", [P, R, 2 * T, D])
        hT, hidden = ph.sb("hT", [P, 2 * GW]), ph.sb("hidden", [P, GW])
        msg = ph.sb("msg", [P, R, T, D])
        eq = ph.sb("eq", [P, R, block_at(T, T)])
        keyf, count, way = ph.sb("keyf", [P, R, T]), ph.sb("count", [P, T]), ph.sb("way", [P, R, T])
        stats, mv, rstd = ph.sb("stats", [P, 2 * T, 6]), ph.sb("mv", [P, 2 * T, 2]), ph.sb("rstd", [P, 2 * T])
        to = ph.sb("to", [P, R, T], I32)
        sums = ph.sb("sums", [P, R, T, D])
        psT, psH, psM, psS = ph.ps("psT", [P, 2 * GW]), ph.ps("psH", [P, GW]), ph.ps("psM", [P, GW]), ph.ps("psS", [P, GW])

        weights_in = ph.sem("weights_in")
        ends_in = [ph.sem(f"ends_in{s}") for s in range(R)]
        loaded = [ph.sem(f"keys_in{s}") for s in range(R)]
        gathered = [ph.sem(f"rows_gathered{s}") for s in range(R)]
        own, united, normed = ph.sem("norm_steps"), ph.sem("unite_steps"), ph.sem("rows_normed")
        measured, root_ready = ph.sem("rows_measured"), ph.sem("root_ready")
        turned, hT_ready, preact = ph.sem("rows_turned"), ph.sem("hT_ready"), ph.sem("preactivation")
        hidden_ready, product, msg_ready = ph.sem("hidden_ready"), ph.sem("product"), ph.sem("msg_ready")
        summed, sums_ready, landed = ph.sem("summed"), ph.sem("sums_ready"), ph.sem("scatters_landed")

        every = Measure(ph, sh, table)

        block = ctx.enter_context(nc.Block())

        @block.sync
        def _(sp):
            for dst, src in ((W1s[:, :], w1[0:D, :]), (W1d[:, :], w1[D:2 * D, :]), (W1e[:, :], w1[2 * D:2 * D + 4, :]),
                             (W2[:, :], w2), (B1[:, :], b1), (B2[:, :], b2.to_broadcast([P, D]))):
                sp.dma_start(dst, src).then_inc(weights_in, 16)

            def load(g, s, k, back):
                if back == R:
                    sp.wait_ge(gathered[s], k * 128)
                sp.dma_start(end[:, s, :], ends[g, :, SRC:SRC + 2 * T]).then_inc(ends_in[s], 16)
                if back == R:
                    sp.wait_ge(msg_ready, 2 * (g - R + 1))
                sp.dma_start(key[:, s, :], ends[g, :, DST_KEY:DST_KEY + T]).then_inc(loaded[s], 16)
                sp.dma_start(row[:, s, :], dst_rows[bass.ds(g, 1), :].to_broadcast([P, GW])).then_inc(loaded[s], 16)
                sp.dma_start(attr[:, s, :], attrT[:, bass.ds(g * GW, GW)]).then_inc(loaded[s], 16)
                every.load(sp, g, s, back)
            over_groups(sp, EG, (load, 0))

        @block.gpsimd
        def _(pool):
            passed = ph.sem("pool_waits_passed")
            def gather(s, j):
                at = bass.IndirectOffsetOnAxis(ap=end[:, s, j:j + 1], axis=0)
                pool.indirect_dma_start(x[:, s, j, :], None, table, at).then_inc(gathered[s], 16)

            for s in range(R):
                pool.wait_ge(ends_in[s], 16)
                for j in range(2 * T):
                    gather(s, j)

            def scatter(g, s, k, back):
                ahead = not isinstance(g, int) or g + R < EG
                pool.wait_ge(sums_ready, g + 1)
                wait_apart(pool, msg_ready, 2 * (g + 1), passed)
                if ahead:
                    pool.wait_ge(ends_in[s], (k + 2) * 16)
                    wait_apart(pool, turned, g + 1, passed)
                for j in range(T):
                    at = bass.IndirectOffsetOnAxis(ap=to[:, s, j:j + 1], axis=0)
                    pool.indirect_dma_start(acc, at, sums[:, s, j, :], None, compute_op=ALU.add).then_inc(landed, 16)
                if ahead:
                    for j in range(2 * T):
                        gather(s, j)
                wait_apart(pool, landed, (g + 1) * 64, passed)
            over_groups(pool, EG, (scatter, 0), last=R)

        @block.vector
        def _(dve):
            passed = ph.sem("dve_waits_passed")
            norms = Chain(dve, own, NORM_STEPS, passed)
            unites = Chain(dve, united, UNITE_STEPS, passed)
            dve.wait_ge(weights_in, 96)

            def norm_rows(g, s, k, back):
                norms.start(g)
                dve.wait_ge(gathered[s], (k + 1) * 128)
                normalise(nc, norms, x[:, s], stats, mv, rstd, measured, root_ready, g).then_inc(normed, 1)

            def unite_edges(g, s, k, back):
                unites.start(g)
                dve.wait_ge(loaded[s], (k + 1) * 48)
                if back == R:
                    dve.wait_ge(summed, g - R + 1)
                unite(nc, sh, unites, T, eq[:, s], row[:, s], key[:, s], keyf[:, s], count, way[:, s])

            def messages(g, s, k, back):
                dve.wait_ge(product, g + 1)
                if back == R:
                    dve.wait_ge(landed, (g - R + 1) * 64)
                nc.vector.tensor_tensor(to[:, s, :], way[:, s, :], keyf[:, s, :], ALU.add).then_inc(msg_ready, 1)
                by = B2[:, :].unsqueeze(1).to_broadcast([P, T, D])
                nc.vector.tensor_tensor(msg[:, s, :, :], tiled(psM[:, :]), by, ALU.add).then_inc(msg_ready, 1)
            count_all, measure_all, keep_all = every.vector_parts(nc, dve, passed)
            over_groups(dve, EG, (norm_rows, 0), (messages, 1), (count_all, 0), (unite_edges, -1), (measure_all, 0), (keep_all, 1))
            dve.wait_ge(every.kept, 2 * EG)

        @block.tensor
        def _(pe):
            pe.wait_ge(weights_in, 96)

            def turn(g, s, k, back):
                pe.wait_ge(normed, g + 1)
                if back:
                    pe.wait_ge(hT_ready, g)
                for j in range(2 * T):
                    last = pe.transpose(psT[:, j * P:(j + 1) * P], x[:, s, j, :], sh.ident[:, :])
                last.then_inc(turned, 1)

            def first_layer(g, s, k, back):
                pe.wait_ge(loaded[s], (k + 1) * 48)
                pe.wait_ge(hT_ready, g + 1)
                if back:
                    pe.wait_ge(hidden_ready, g)
                pe.matmul(psH[:, :], W1s[:, :], hT[:, 0:GW], start=True, stop=False)
                pe.matmul(psH[:, :], W1d[:, :], hT[:, GW:2 * GW], start=False, stop=False)
                pe.matmul(psH[:, :], W1e[:, :], attr[:, s, :], start=False, stop=True).then_inc(preact, 1)

            def second_layer(g, s, k, back):
                pe.wait_ge(hidden_ready, g + 1)
                if back:
                    pe.wait_ge(msg_ready, 2 * g)
                for j in range(T):
                    last = pe.matmul(psM[:, j * D:(j + 1) * D], hidden[:, j * P:(j + 1) * P], W2[:, :],
                                     start=True, stop=True)
                last.then_inc(product, 1)

            def add_up(g, s, k, back):
                pe.wait_ge(msg_ready, 2 * (g + 1))
                if back:
                    pe.wait_ge(sums_ready, g)
                batch_sums(pe, T, lambda j: psS[:, j * D:(j + 1) * D], eq[:, s], msg[:, s], D).then_inc(summed, 1)
            over_groups(pe, EG, (turn, 0), (add_up, 1), (first_layer, 0), (second_layer, 0))

        @block.scalar
        def _(act):
            act.wait_ge(weights_in, 96)

            def transposed(g, s, k, back):
                act.wait_ge(measured, g + 1)
                nc.scalar.activation(rstd[:, :], mv[:, :, 1], ACT.Sqrt, bias=sh.eps[:, :]).then_inc(root_ready, 1)
                act.wait_ge(turned, g + 1)
                if back:
                    act.wait_ge(preact, g)
                nc.scalar.activation(hT[:, :], psT[:, :], ACT.Relu).then_inc(hT_ready, 1)

            def hide(g, s, k, back):
                act.wait_ge(preact, g + 1)
                if back:
                    act.wait_ge(product, g)
                nc.scalar.activation(hidden[:, :], psH[:, :], ACT.Relu, bias=B1[:, :]).then_inc(hidden_ready, 1)

            def sums_out(g, s, k, back):
                act.wait_ge(summed, g + 1)
                if back == R:
                    act.wait_ge(landed, (g - R + 1) * 64)
                nc.scalar.activation(sums[:, s, :, :].rearrange("p j d -> p (j d)"), psS[:, :], ACT.Copy
                                     ).then_inc(sums_ready, 1)
            over_groups(act, EG, (transposed, 0), (sums_out, 1), (hide, 0), (every.take_root(nc, act), 0))


def gcn_nodes(nc, sh, tag, table, acc, w, weights, biases, out, norm=False, last_layer=None, copy=None):
    R, products = (4, 2) if last_layer else (8, 2)
    with ExitStack() as ctx:
        ph = Phase(sh, tag, ctx)
        n_bias = biases.shape[0]
        W, bias_rows, bias = ph.sb("weights", [P, 2 * D]), ph.sb("bias_rows", [P, n_bias, D]), ph.sb("bias", [P, D])
        x, sums = ph.sb("x", [P, R, T * D]), ph.sb("sums", [P, R, T, w])
        hT = ph.sb("hT", [P, R, GW])
        part = ph.sb("part", [P, R, T * D])
        h = ph.sb("h", [P, R, T * D])
        share = ph.sb("share", [P, R, T])
        stats, mv = ph.sb("stats", [P, T, 6]), ph.sb("mv", [P, R, T, 2])
        rstd, minus = ph.sb("rstd", [P, R, T]), ph.sb("minus_mean", [P, R, T])
        psT, psP = ph.ps("psT", [P, GW]), ph.ps("psP", [P, products, T, 2 * D])
        n_load = 2
        if last_layer:
            res_table, wa, ba = last_layer
            WA, BA = ph.sb("w_last", [P, D]), ph.sb("b_last", [P, D])
            res, new = ph.sb("res", [P, R, T * D]), ph.sb("new", [P, R, T * D])
            h2T = ph.sb("h2T", [P, R, GW])
            psT2, psO = ph.ps("psT2", [P, GW]), ph.ps("psO", [P, GW])
            res_in = [ph.sem(f"res_in{s}") for s in range(R)]
        weights_in, spare_cleared = ph.sem("weights_in"), ph.sem("spare_cleared")
        loaded = [ph.sem(f"rows_in{s}") for s in range(R)]
        stored = [ph.sem(f"stored{s}") for s in range(R)]
        degree_set, totalled, share_ready, bias_set = ph.sem("degree_set"), ph.sem("totalled"), ph.sem("share_ready"), ph.sem("bias_set")
        counted, measured, root_ready = ph.sem("counted"), ph.sem("rows_measured"), ph.sem("root_ready")
        inverted, factors_ready, normed = ph.sem("inverted"), ph.sem("factors_ready"), ph.sem("rows_normed")
        neighbours, scaled = ph.sem("neighbours_added"), ph.sem("scaled")
        turned, hT_ready, product = ph.sem("rows_turned"), ph.sem("hT_ready"), ph.sem("product")
        combined, biased, leaked = ph.sem("combined"), ph.sem("biased"), ph.sem("leaked")
        turned2, h2T_ready, product2 = ph.sem("turned2"), ph.sem("h2T_ready"), ph.sem("product2")
        added, finished = ph.sem("added"), ph.sem("finished")
        per_store = 16 if copy is None else 32
        n_weights = 32 + (32 if last_layer else 0)

        block = ctx.enter_context(nc.Block())

        @block.sync
        def _(sp):
            sp.dma_start(W[:, :], weights).then_inc(weights_in, 16)
            rows = biases.rearrange("(o b) d -> o b d", o=1)
            sp.dma_start(bias_rows[:, :, :], rows.to_broadcast([P, n_bias, D])).then_inc(weights_in, 16)
            if last_layer:
                sp.dma_start(WA[:, :], wa).then_inc(weights_in, 16)
                sp.dma_start(BA[:, :], ba.to_broadcast([P, D])).then_inc(weights_in, 16)

            if copy is not None:
                sp.dma_start(copy[N:PAD_ROW, :].rearrange("(p r) d -> p (r d)", p=P), sh.zeros[:, 0:T * D]
                             ).then_inc(spare_cleared, 16)
                sp.dma_start(copy[PAD_ROW:PAD_ROW + 1, :], sh.zeros[0:1, 0:D]).then_inc(spare_cleared, 16)

            def load(g, s, k, back):
                if back == R:
                    sp.wait_ge(turned, g - R + 1)
                    sp.wait_ge(neighbours, g - R + 1)
                    if norm:
                        sp.wait_ge(degree_set, g - R + 1)
                sp.dma_start(x[:, s, :], rows_of(table, g)).then_inc(loaded[s], 16)
                sp.dma_start(sums[:, s, :, :].rearrange("p j d -> p (j d)"), rows_of(acc, g, w)).then_inc(loaded[s], 16)

            def load_res(g, s, k, back):
                if back == R:
                    sp.wait_ge(finished, g - R + 1)
                sp.dma_start(res[:, s, :], rows_of(res_table, g)).then_inc(res_in[s], 16)
            over_groups(sp, NG, (load, 0), *([(load_res, 2)] if last_layer else []), ring=R)
            if copy is not None:
                sp.wait_ge(spare_cleared, 32)

        @block.vector
        def _(dve):
            passed = ph.sem("dve_waits_passed")
            dve.wait_ge(weights_in, n_weights)
            nc.vector.tensor_tensor(bias[:, :], bias_rows[:, 0, :], bias_rows[:, 1, :], ALU.add).then_inc(bias_set, 1)
            for b in range(2, n_bias):
                dve.wait_ge(bias_set, b - 1)
                nc.vector.tensor_tensor(bias[:, :], bias[:, :], bias_rows[:, b, :], ALU.add).then_inc(bias_set, 1)

            def count(g, s, k, back):
                dve.wait_ge(loaded[s], (k + 1) * 32)
                if back:
                    dve.wait_ge(measured, g)
                for j in range(T):
                    i = nc.vector.bn_stats(stats[:, j, :], x[:, s, j * D:(j + 1) * D])
                i.then_inc(counted, 1)

            def measure(g, s, k, back):
                wait_apart(dve, counted, g + 1, passed)
                for j in range(T):
                    i = nc.vector.bn_aggr(mv[:, s, j, :], stats[:, j, :])
                i.then_inc(measured, 1)

            def invert(g, s, k, back):
                dve.wait_ge(root_ready, g + 1)
                nc.vector.reciprocal(rstd[:, s, :], rstd[:, s, :]).then_inc(inverted, 1)

            def centre(g, s, k, back):
                dve.wait_ge(inverted, g + 1)
                nc.vector.scalar_tensor_tensor(minus[:, s, :], mv[:, s, :, 0], -1.0, rstd[:, s, :], ALU.mult, ALU.mult
                                               ).then_inc(factors_ready, 1)

            def degrees(g, s, k, back):
                dve.wait_ge(loaded[s], (k + 1) * 32)
                nc.vector.tensor_copy(sh.degree[:, bass.ds(g * T, T)], sums[:, s, :, D]).then_inc(degree_set, 1)

            def totals(g, s, k, back):
                if norm:
                    dve.wait_ge(degree_set, g + 1)
                if back == R:
                    dve.wait_ge(combined, g - R + 1)
                nc.vector.tensor_scalar(share[:, s, :], sh.degree[:, bass.ds(g * T, T)], 1.0, None, ALU.add
                                        ).then_inc(totalled, 1)

            def shares(g, s, k, back):
                dve.wait_ge(totalled, g + 1)
                nc.vector.reciprocal(share[:, s, :], share[:, s, :]).then_inc(share_ready, 1)

            def add_neighbours(g, s, k, back):
                dve.wait_ge(loaded[s], (k + 1) * 32)
                dve.wait_ge(product, g + 1)
                if back == R:
                    if last_layer:
                        dve.wait_ge(combined, g - R + 1)
                    else:
                        dve.wait_ge(leaked, g - R + 1)
                nc.vector.tensor_tensor(tiled(part[:, s, :]), psP[:, s % products, :, D:2 * D], sums[:, s, :, 0:D], ALU.add
                                        ).then_inc(neighbours, 1)

            def combine(g, s, k, back):
                dve.wait_ge(neighbours, g + 1)
                dve.wait_ge(share_ready, g + 1)
                if back == R:
                    dve.wait_ge(turned2 if last_layer else leaked, g - R + 1)
                    if not last_layer:
                        dve.wait_ge(stored[s], k * per_store)
                for j in range(T):
                    c = slice(j * D, (j + 1) * D)
                    i = nc.vector.scalar_tensor_tensor(h[:, s, c], part[:, s, c], share[:, s, j:j + 1],
                                                       psP[:, s % products, j, 0:D], ALU.mult, ALU.add)
                i.then_inc(combined, 1)

            def add_rest(g, s, k, back):
                dve.wait_ge(product2, g + 1)
                dve.wait_ge(res_in[s], (k + 1) * 16)
                if back == R:
                    dve.wait_ge(stored[s], k * per_store)
                nc.vector.tensor_tensor(new[:, s, :], psO[:, :], res[:, s, :], ALU.add).then_inc(added, 1)

            def leak(g, s, k, back):
                dve.wait_ge(biased, g + 1)
                nc.vector.scalar_tensor_tensor(h[:, s, :], h[:, s, :], SLOPE, h[:, s, :], ALU.mult, ALU.max
                                               ).then_inc(leaked, 1)
            if norm:
                over_groups(dve, NG, (count, 0), (invert, 2), (degrees, 2), (measure, 0), (centre, 2), (totals, 2),
                            (add_neighbours, 5), (shares, 2), (combine, 5), ring=R)
            else:
                over_groups(dve, NG, (totals, 0), (add_neighbours, 1), (shares, 0), (combine, 1), (leak, 2), (add_rest, 4),
                            ring=R)

        @block.gpsimd
        def _(pool):
            passed = ph.sem("pool_waits_passed")
            pool.wait_ge(bias_set, n_bias - 1)

            def add_bias(g, s, k, back):
                pool.wait_ge(combined, g + 1)
                rows = tiled(h[:, s, :])
                nc.gpsimd.tensor_tensor(rows, rows, bias[:, :].unsqueeze(1).to_broadcast([P, T, D]), ALU.add
                                        ).then_inc(biased, 1)

            def finish(g, s, k, back):
                pool.wait_ge(added, g + 1)
                rows = tiled(new[:, s, :])
                nc.gpsimd.tensor_tensor(rows, rows, BA[:, :].unsqueeze(1).to_broadcast([P, T, D]), ALU.add
                                        ).then_inc(finished, 1)


            def leak(g, s, k, back):
                pool.wait_ge(scaled, g + 1)
                nc.gpsimd.tensor_tensor(h[:, s, :], h[:, s, :], part[:, s, :], ALU.add).then_inc(leaked, 1)
            if last_layer:
                over_groups(pool, NG, (add_bias, 1), (finish, 4), ring=R)
            else:
                over_groups(pool, NG, (add_bias, 0), (leak, 1), ring=R)

        @block.tensor
        def _(pe):
            pe.wait_ge(weights_in, n_weights)

            def turn(g, s, k, back):
                if norm:
                    pe.wait_ge(normed, g + 1)
                else:
                    pe.wait_ge(loaded[s], (k + 1) * 32)
                if back:
                    pe.wait_ge(hT_ready, g)
                for j in range(T):
                    i = pe.transpose(psT[:, j * P:(j + 1) * P], x[:, s, j * D:(j + 1) * D], sh.ident[:, :])
                i.then_inc(turned, 1)

            def multiply(g, s, k, back):
                pe.wait_ge(hT_ready, g + 1)
                if back >= products:
                    pe.wait_ge(combined, g - products + 1)
                for j in range(T):
                    i = pe.matmul(psP[:, s % products, j, :], hT[:, s, j * P:(j + 1) * P], W[:, :], start=True, stop=True)
                i.then_inc(product, 1)

            def turn2(g, s, k, back):
                pe.wait_ge(leaked, g + 1)
                if back:
                    pe.wait_ge(h2T_ready, g)
                for j in range(T):
                    i = pe.transpose(psT2[:, j * P:(j + 1) * P], h[:, s, j * D:(j + 1) * D], sh.ident[:, :])
                i.then_inc(turned2, 1)

            def multiply2(g, s, k, back):
                pe.wait_ge(h2T_ready, g + 1)
                if back:
                    pe.wait_ge(added, g)
                for j in range(T):
                    i = pe.matmul(psO[:, j * D:(j + 1) * D], h2T[:, s, j * P:(j + 1) * P], WA[:, :],
                                  start=True, stop=True)
                i.then_inc(product2, 1)
            over_groups(pe, NG, (multiply, 1), (turn, 0),
                        *([(multiply2, 4), (turn2, 3)] if last_layer else []), ring=R)

        @block.scalar
        def _(act):
            def take_root(g, s, k, back):
                act.wait_ge(measured, g + 1)
                nc.scalar.activation(rstd[:, s, :], mv[:, s, :, 1], ACT.Sqrt, bias=sh.eps[:, :]).then_inc(root_ready, 1)

            def normalise(g, s, k, back):
                act.wait_ge(factors_ready, g + 1)
                for j in range(T):
                    c = slice(j * D, (j + 1) * D)
                    i = nc.scalar.activation(x[:, s, c], x[:, s, c], ACT.Relu, scale=rstd[:, s, j:j + 1],
                                             bias=minus[:, s, j:j + 1])
                i.then_inc(normed, 1)

            def transposed(g, s, k, back):
                act.wait_ge(turned, g + 1)
                if back == R:
                    act.wait_ge(product, g - R + 1)
                nc.scalar.activation(hT[:, s, :], psT[:, :], ACT.Copy).then_inc(hT_ready, 1)

            def split_leaky(g, s, k, back):
                act.wait_ge(biased, g + 1)
                nc.scalar.activation(part[:, s, :], h[:, s, :], ACT.Relu, scale=1 - SLOPE)
                nc.scalar.activation(h[:, s, :], h[:, s, :], ACT.Copy, scale=SLOPE).then_inc(scaled, 1)

            def transposed2(g, s, k, back):
                act.wait_ge(turned2, g + 1)
                if back == R:
                    act.wait_ge(product2, g - R + 1)
                nc.scalar.activation(h2T[:, s, :], psT2[:, :], ACT.Copy).then_inc(h2T_ready, 1)

            def store(g, s, k, back):
                await_overlapped(act, stored, g, per_store)
                if last_layer:
                    act.wait_ge(finished, g + 1)
                    act.dma_start(rows_of(out, g), new[:, s, :]).then_inc(stored[s], 16)
                    act.dma_start(rows_of(copy, g), new[:, s, :]).then_inc(stored[s], 16)
                else:
                    act.wait_ge(leaked, g + 1)
                    act.dma_start(rows_of(out, g), h[:, s, :]).then_inc(stored[s], 16)
            if last_layer:
                over_groups(act, NG, (transposed, 0), (transposed2, 3), (store, 5), ring=R)
            else:
                over_groups(act, NG, (take_root, 0), (split_leaky, 6), (transposed, 3), (normalise, 2), (store, 8), ring=R)
            for s in range(R):
                act.wait_ge(stored[s], per_store * -(-(NG - s) // R))


def gated_nodes(nc, sh, tag, table, acc, wz, wr, wh, bz, br, bh, out):
    R = 6
    with ExitStack() as ctx:
        ph = Phase(sh, tag, ctx)
        W = {n: ph.sb("w" + n, [P, 2, D]) for n in "zrh"}
        B = {n: ph.sb("b" + n, [P, 1]) for n in "zrh"}
        x, sums, xn = (ph.sb(n, [P, R, T * D]) for n in ("x", "sums", "xn"))
        hT, aT, z, r, t, new = (ph.sb(n, [P, R, GW]) for n in ("hT", "aT", "z", "r", "t", "new"))
        psH, psA, psZ, psR, psC, psO = (ph.ps(n, [P, GW]) for n in ("psH", "psA", "psZ", "psR", "psC", "psO"))
        weights_in, spare_cleared = ph.sem("weights_in"), ph.sem("spare_cleared")
        loaded = [ph.sem(f"rows_in{s}") for s in range(R)]
        stored = [ph.sem(f"stored{s}") for s in range(R)]
        normed = ph.sem("rows_normed")
        turned, acc_turned, hT_ready, aT_ready = (ph.sem(n) for n in ("turned", "acc_turned", "hT_ready", "aT_ready"))
        z_in, r_in, z_ready, r_ready = (ph.sem(n) for n in ("z_in", "r_in", "z_ready", "r_ready"))
        reset, cand, cand_ready = (ph.sem(n) for n in ("reset", "candidate", "candidate_ready"))
        mixing, back_turned, added = ph.sem("mixing"), ph.sem("back_turned"), ph.sem("added")

        block = ctx.enter_context(nc.Block())

        @block.sync
        def _(sp):
            for n, w, b in (("z", wz, bz), ("r", wr, br), ("h", wh, bh)):
                sp.dma_start(W[n][:, :, :], w.rearrange("(c p) d -> p c d", p=P)).then_inc(weights_in, 16)
                sp.dma_start(B[n][:, :], b).then_inc(weights_in, 16)
            sp.dma_start(out[N:PAD_ROW, :].rearrange("(p r) d -> p (r d)", p=P), sh.zeros[:, 0:T * D]
                         ).then_inc(spare_cleared, 16)
            sp.dma_start(out[PAD_ROW:PAD_ROW + 1, :], sh.zeros[0:1, 0:D]).then_inc(spare_cleared, 16)

            def load(g, s, k, back):
                if back == R:
                    sp.wait_ge(added, g - R + 1)
                    sp.wait_ge(acc_turned, g - R + 1)
                sp.dma_start(x[:, s, :], rows_of(table, g)).then_inc(loaded[s], 16)
                sp.dma_start(sums[:, s, :], rows_of(acc, g)).then_inc(loaded[s], 16)
            over_groups(sp, NG, (load, 0), ring=R)
            sp.wait_ge(spare_cleared, 32)

        @block.vector
        def _(dve):
            passed = ph.sem("dve_waits_passed")
            def norm_rows(g, s, k, back):
                dve.wait_ge(loaded[s], (k + 1) * 32)
                if back == R:
                    dve.wait_ge(turned, g - R + 1)
                for j in range(T):
                    c, at = slice(j * D, (j + 1) * D), bass.ds(g * T + j, 1)
                    i = nc.vector.tensor_scalar(xn[:, s, c], x[:, s, c], sh.mean[:, at], sh.scale[:, at],
                                                ALU.subtract, ALU.mult)
                i.then_inc(normed, 1)

            def reset_h(g, s, k, back):
                dve.wait_ge(r_ready, g + 1)
                nc.vector.tensor_tensor(r[:, s, :], r[:, s, :], hT[:, s, :], ALU.mult).then_inc(reset, 1)

            def add(g, s, k, back):
                dve.wait_ge(back_turned, g + 1)
                if back == R:
                    dve.wait_ge(stored[s], k * 16)
                nc.vector.tensor_tensor(new[:, s, :], psO[:, :], x[:, s, :], ALU.add).then_inc(added, 1)
            over_groups(dve, NG, (norm_rows, 0), (reset_h, 1), (add, 4), ring=R)

        @block.gpsimd
        def _(pool):
            passed = ph.sem("pool_waits_passed")
            def mix(g, s, k, back):
                pool.wait_ge(cand_ready, g + 1)
                pool.wait_ge(z_ready, g + 1)
                nc.gpsimd.tensor_tensor(t[:, s, :], t[:, s, :], hT[:, s, :], ALU.subtract).then_inc(mixing, 1)
                pool.wait_ge(mixing, g * 3 + 1)
                nc.gpsimd.tensor_tensor(t[:, s, :], t[:, s, :], z[:, s, :], ALU.mult).then_inc(mixing, 1)
                pool.wait_ge(mixing, g * 3 + 2)
                nc.gpsimd.tensor_tensor(t[:, s, :], t[:, s, :], hT[:, s, :], ALU.add).then_inc(mixing, 1)
            over_groups(pool, NG, (mix, 0), ring=R)

        @block.tensor
        def _(pe):
            pe.wait_ge(weights_in, 96)

            def turn(g, s, k, back):
                pe.wait_ge(loaded[s], (k + 1) * 32)
                if back:
                    pe.wait_ge(aT_ready, g)
                for j in range(T):
                    i = pe.transpose(psA[:, j * P:(j + 1) * P], sums[:, s, j * D:(j + 1) * D], sh.ident[:, :])
                i.then_inc(acc_turned, 1)
                pe.wait_ge(normed, g + 1)
                if back:
                    pe.wait_ge(hT_ready, g)
                for j in range(T):
                    i = pe.transpose(psH[:, j * P:(j + 1) * P], xn[:, s, j * D:(j + 1) * D], sh.ident[:, :])
                i.then_inc(turned, 1)

            def gates(g, s, k, back):
                pe.wait_ge(hT_ready, g + 1)
                pe.wait_ge(aT_ready, g + 1)
                for n, ps, read, done in (("r", psR, r_ready, r_in), ("z", psZ, z_ready, z_in)):
                    if back:
                        pe.wait_ge(read, g)
                    pe.matmul(ps[:, :], W[n][:, 0, :], hT[:, s, :], start=True, stop=False)
                    pe.matmul(ps[:, :], W[n][:, 1, :], aT[:, s, :], start=False, stop=True).then_inc(done, 1)

            def candidate(g, s, k, back):
                pe.wait_ge(reset, g + 1)
                if back:
                    pe.wait_ge(cand_ready, g)
                pe.matmul(psC[:, :], W["h"][:, 1, :], aT[:, s, :], start=True, stop=False)
                pe.matmul(psC[:, :], W["h"][:, 0, :], r[:, s, :], start=False, stop=True).then_inc(cand, 1)

            def turn_back(g, s, k, back):
                pe.wait_ge(mixing, (g + 1) * 3)
                if back:
                    pe.wait_ge(added, g)
                for j in range(T):
                    i = pe.transpose(psO[:, j * D:(j + 1) * D], t[:, s, j * P:(j + 1) * P], sh.ident[:, :])
                i.then_inc(back_turned, 1)
            over_groups(pe, NG, (gates, 1), (turn, 0), (candidate, 2), (turn_back, 4), ring=R)

        @block.scalar
        def _(act):
            act.wait_ge(weights_in, 96)

            def transposed(g, s, k, back):
                act.wait_ge(acc_turned, g + 1)
                if back == R:
                    act.wait_ge(cand, g - R + 1)
                    act.wait_ge(mixing, (g - R + 1) * 3)
                nc.scalar.activation(aT[:, s, :], psA[:, :], ACT.Copy).then_inc(aT_ready, 1)
                act.wait_ge(turned, g + 1)
                nc.scalar.activation(hT[:, s, :], psH[:, :], ACT.Relu).then_inc(hT_ready, 1)

            def squash(g, s, k, back):
                act.wait_ge(r_in, g + 1)
                if back == R:
                    act.wait_ge(cand, g - R + 1)
                    act.wait_ge(mixing, (g - R + 1) * 3)
                nc.scalar.activation(r[:, s, :], psR[:, :], ACT.Sigmoid, bias=B["r"][:, :]).then_inc(r_ready, 1)
                act.wait_ge(z_in, g + 1)
                nc.scalar.activation(z[:, s, :], psZ[:, :], ACT.Sigmoid, bias=B["z"][:, :]).then_inc(z_ready, 1)

            def bend(g, s, k, back):
                act.wait_ge(cand, g + 1)
                if back == R:
                    act.wait_ge(back_turned, g - R + 1)
                nc.scalar.activation(t[:, s, :], psC[:, :], ACT.Tanh, bias=B["h"][:, :]).then_inc(cand_ready, 1)

            def store(g, s, k, back):
                await_overlapped(act, stored, g)
                act.wait_ge(added, g + 1)
                act.dma_start(rows_of(out, g), new[:, s, :]).then_inc(stored[s], 16)
            over_groups(act, NG, (transposed, 0), (squash, 1), (bend, 2), (store, 5), ring=R)
            for s in range(R):
                act.wait_ge(stored[s], 16 * -(-(NG - s) // R))


def attend(nc, sh, tag, table, w, wT, a_cols, ends, src_rows, outside):
    with ExitStack() as ctx:
        keep = Phase(sh, tag, ctx)
        values = keep.sb("values", [P, EG, T * D])
        logit = keep.sb("logit", [P, EG * T])
        weight = keep.sb("weight", [P, EG * T])

        with ExitStack() as inner:
            ph = Phase(sh, tag, inner)
            W, WT, A = ph.sb("w", [P, D]), ph.sb("wT", [P, D]), ph.sb("a", [P, 2])
            spread, U = ph.sb("spread", [P, 2, D]), ph.sb("u", [P, 2, D])
            end = ph.sb("ends", [P, R, 2 * T], I32)
            x = ph.sb("x", [P, R, 2 * T, D])
            hT, product_junk = ph.sb("hT", [P, GW]), ph.sb("dots", [P, R, 2 * T, D])
            score = ph.sb("score", [P, R, 2 * T])
            stats, mv, rstd = ph.sb("stats", [P, 2 * T, 6]), ph.sb("mv", [P, 2 * T, 2]), ph.sb("rstd", [P, 2 * T])
            psT, psM, psU = ph.ps("psT", [P, GW]), ph.ps("psM", [P, GW]), ph.ps("psU", [P, 2, D])
            weights_in, spread_set, u_in, u_set = (ph.sem(n) for n in ("weights_in", "spread_set", "u_in", "u_set"))
            ends_in = [ph.sem(f"ends_in{s}") for s in range(R)]
            gathered = [ph.sem(f"rows_gathered{s}") for s in range(R)]
            own, measured, root_ready = ph.sem("norm_steps"), ph.sem("rows_measured"), ph.sem("root_ready")
            normed, turned, hT_ready = ph.sem("rows_normed"), ph.sem("rows_turned"), ph.sem("hT_ready")
            product, values_ready = ph.sem("product"), ph.sem("values_ready")
            scored, logits_set = ph.sem("scored"), ph.sem("logits_set")

            block = inner.enter_context(nc.Block())

            @block.sync
            def _(sp):
                sp.dma_start(W[:, :], w).then_inc(weights_in, 16)
                sp.dma_start(WT[:, :], wT).then_inc(weights_in, 16)
                sp.dma_start(A[:, :], a_cols).then_inc(weights_in, 16)

                def load(g, s, k, back):
                    if back == R:
                        sp.wait_ge(gathered[s], k * 128)
                    sp.dma_start(end[:, s, :], ends[g, :, SRC:SRC + 2 * T]).then_inc(ends_in[s], 16)
                over_groups(sp, EG, (load, 0))

            @block.gpsimd
            def _(pool):
                passed = ph.sem("pool_waits_passed")
                def gather(g, s, k, back):
                    pool.wait_ge(ends_in[s], (k + 1) * 16)
                    if back == R:
                        pool.wait_ge(turned, g - R + 1)
                        wait_apart(pool, scored, g - R + 1, passed)
                    for j in range(2 * T):
                        at = bass.IndirectOffsetOnAxis(ap=end[:, s, j:j + 1], axis=0)
                        pool.indirect_dma_start(x[:, s, j, :], None, table, at).then_inc(gathered[s], 16)
                over_groups(pool, EG, (gather, 0))

            @block.vector
            def _(dve):
                passed = ph.sem("dve_waits_passed")
                dve.wait_ge(weights_in, 48)
                for c in range(2):
                    i = nc.vector.tensor_copy(spread[:, c, :], A[:, c:c + 1].to_broadcast([P, D]))
                i.then_inc(spread_set, 1)
                dve.wait_ge(u_in, 1)
                nc.vector.tensor_copy(U[:, :, :], psU[:, :, :]).then_inc(u_set, 1)
                dve.wait_ge(u_set, 1)
                norms = Chain(dve, own, NORM_STEPS, passed)

                def norm_rows(g, s, k, back):
                    norms.start(g)
                    dve.wait_ge(gathered[s], (k + 1) * 128)
                    normalise(nc, norms, x[:, s], stats, mv, rstd, measured, root_ready, g).then_inc(normed, 1)
                    dve.wait_ge(normed, g + 1)
                    if back == R:
                        dve.wait_ge(logits_set, g - R + 1)
                    for j in range(2 * T):
                        i = nc.vector.scalar_tensor_tensor(product_junk[:, s, j, :], x[:, s, j, :], 0.0, U[:, j // T, :],
                                                           ALU.max, ALU.mult, accum_out=score[:, s, j:j + 1])
                    i.then_inc(scored, 1)

                def logits(g, s, k, back):
                    dve.wait_ge(scored, g + 1)
                    nc.vector.tensor_tensor(logit[:, bass.ds(g * T, T)], score[:, s, 0:T], score[:, s, T:2 * T], ALU.add
                                            ).then_inc(logits_set, 1)
                over_groups(dve, EG, (norm_rows, 0), (logits, 1))

            @block.tensor
            def _(pe):
                pe.wait_ge(weights_in, 48)
                pe.wait_ge(spread_set, 1)
                for c in range(2):
                    i = pe.matmul(psU[:, c, :], spread[:, c, :], WT[:, :], start=True, stop=True)
                i.then_inc(u_in, 1)

                def turn(g, s, k, back):
                    pe.wait_ge(normed, g + 1)
                    if back:
                        pe.wait_ge(hT_ready, g)
                    for j in range(T):
                        i = pe.transpose(psT[:, j * P:(j + 1) * P], x[:, s, T + j, :], sh.ident[:, :])
                    i.then_inc(turned, 1)

                def multiply(g, s, k, back):
                    pe.wait_ge(hT_ready, g + 1)
                    if back:
                        pe.wait_ge(values_ready, g)
                    for j in range(T):
                        i = pe.matmul(psM[:, j * D:(j + 1) * D], hT[:, j * P:(j + 1) * P], W[:, :], start=True, stop=True)
                    i.then_inc(product, 1)
                over_groups(pe, EG, (turn, 0), (multiply, 0))

            @block.scalar
            def _(act):
                def transposed(g, s, k, back):
                    act.wait_ge(measured, g + 1)
                    nc.scalar.activation(rstd[:, :], mv[:, :, 1], ACT.Sqrt, bias=sh.eps[:, :]).then_inc(root_ready, 1)
                    act.wait_ge(turned, g + 1)
                    if back:
                        act.wait_ge(product, g)
                    nc.scalar.activation(hT[:, :], psT[:, :], ACT.Relu).then_inc(hT_ready, 1)

                def keep_values(g, s, k, back):
                    act.wait_ge(product, g + 1)
                    nc.scalar.activation(values[:, bass.ds(g, 1), :].rearrange("p o d -> p (o d)"), psM[:, :], ACT.Copy
                                         ).then_inc(values_ready, 1)
                over_groups(act, EG, (transposed, 0), (keep_values, 0))

        with ExitStack() as inner:
            ph = Phase(sh, tag + "softmax_", inner)
            pad = ph.sb("outside", [P, EG * T])
            top, all_top, minus, total, all_total, inverse = (ph.sb(n, [P, 1]) for n in (
                "top", "all_top", "minus_top", "total", "all_total", "inverse"))
            pad_in, steps = ph.sem("outside_in"), ph.sem("steps")
            block = inner.enter_context(nc.Block())

            @block.sync
            def _(sp):
                sp.dma_start(pad[:, :], outside).then_inc(pad_in, 16)

            @block.vector
            def _(dve):
                passed = ph.sem("dve_waits_passed")
                dve.wait_ge(pad_in, 16)
                nc.vector.tensor_tensor(logit[:, :], logit[:, :], pad[:, :], ALU.add).then_inc(steps, 1)
                dve.wait_ge(steps, 1)
                nc.vector.reduce_max(top[:, :], logit[:, :], AX_X).then_inc(steps, 1)
                dve.wait_ge(steps, 5)
                nc.vector.reciprocal(inverse[:, :], all_total[:, :]).then_inc(steps, 1)
                dve.wait_ge(steps, 6)
                nc.vector.tensor_scalar(weight[:, :], weight[:, :], inverse[:, 0:1], None, ALU.mult).then_inc(steps, 1)
                dve.wait_ge(steps, 7)

            @block.gpsimd
            def _(pool):
                passed = ph.sem("pool_waits_passed")
                pool.wait_ge(steps, 2)
                nc.gpsimd.partition_all_reduce(all_top[:, :], top[:, :], P, RMAX).then_inc(steps, 1)
                pool.wait_ge(steps, 4)
                nc.gpsimd.partition_all_reduce(all_total[:, :], total[:, :], P, RADD).then_inc(steps, 1)

            @block.scalar
            def _(act):
                minus_set = ph.sem("minus_set")
                act.wait_ge(steps, 3)
                nc.scalar.mul(minus[:, :], all_top[:, :], -1.0).then_inc(minus_set, 1)
                act.wait_ge(minus_set, 1)
                nc.scalar.activation(weight[:, :], logit[:, :], ACT.Exp, bias=minus[:, :], accum_out=total[:, :]
                                     ).then_inc(steps, 1)

        with ExitStack() as inner:
            ph = Phase(sh, tag + "sum_", inner)
            key, row = ph.sb("keys", [P, R, T], I32), ph.sb("key_row", [P, R, GW], I32)
            msg, sums = ph.sb("msg", [P, R, T, D]), ph.sb("sums", [P, R, T, D])
            eq = ph.sb("eq", [P, 2, block_at(T, T)])
            keyf, count, way = ph.sb("keyf", [P, R, T]), ph.sb("count", [P, T]), ph.sb("way", [P, R, T])
            to = ph.sb("to", [P, R, T], I32)
            psS = ph.ps("psS", [P, 2, GW])
            loaded = [ph.sem(f"keys_in{s}") for s in range(R)]
            united, msg_ready, summed = ph.sem("unite_steps"), ph.sem("msg_ready"), ph.sem("summed")
            sums_ready, landed = ph.sem("sums_ready"), ph.sem("scatters_landed")
            block = inner.enter_context(nc.Block())

            @block.sync
            def _(sp):
                def load(g, s, k, back):
                    if back == R:
                        sp.wait_ge(msg_ready, 2 * (g - R + 1))
                    sp.dma_start(key[:, s, :], ends[g, :, SRC_KEY:SRC_KEY + T]).then_inc(loaded[s], 16)
                    sp.dma_start(row[:, s, :], src_rows[bass.ds(g, 1), :].to_broadcast([P, GW])).then_inc(loaded[s], 16)
                over_groups(sp, EG, (load, 0))

            @block.vector
            def _(dve):
                passed = ph.sem("dve_waits_passed")
                unites = Chain(dve, united, UNITE_STEPS, passed)

                def unite_edges(g, s, k, back):
                    unites.start(g)
                    dve.wait_ge(loaded[s], (k + 1) * 32)
                    if back >= 2:
                        dve.wait_ge(summed, g - 1)
                    unite(nc, sh, unites, T, eq[:, s % 2], row[:, s], key[:, s], keyf[:, s], count, way[:, s])

                def messages(g, s, k, back):
                    if back == R:
                        dve.wait_ge(landed, (g - R + 1) * 64)
                    nc.vector.tensor_tensor(to[:, s, :], way[:, s, :], keyf[:, s, :], ALU.add).then_inc(msg_ready, 1)
                    for j in range(T):
                        i = nc.vector.tensor_scalar(msg[:, s, j, :], values[:, bass.ds(g, 1), j * D:(j + 1) * D].rearrange("p o d -> p (o d)"),
                                                    weight[:, bass.ds(g * T + j, 1)], None, ALU.mult)
                    i.then_inc(msg_ready, 1)
                over_groups(dve, EG, (unite_edges, 0), (messages, 0))

            @block.tensor
            def _(pe):
                def add_up(g, s, k, back):
                    pe.wait_ge(msg_ready, 2 * (g + 1))
                    if back >= 2:
                        pe.wait_ge(sums_ready, g - 1)
                    batch_sums(pe, T, lambda j: psS[:, s % 2, j * D:(j + 1) * D], eq[:, s % 2], msg[:, s], D
                               ).then_inc(summed, 1)
                over_groups(pe, EG, (add_up, 0))

            @block.scalar
            def _(act):
                def sums_out(g, s, k, back):
                    act.wait_ge(summed, g + 1)
                    if back == R:
                        act.wait_ge(landed, (g - R + 1) * 64)
                    nc.scalar.activation(sums[:, s, :, :].rearrange("p j d -> p (j d)"), psS[:, s % 2, :], ACT.Copy
                                         ).then_inc(sums_ready, 1)
                over_groups(act, EG, (sums_out, 0))

            @block.gpsimd
            def _(pool):
                passed = ph.sem("pool_waits_passed")
                def scatter(g, s, k, back):
                    pool.wait_ge(sums_ready, g + 1)
                    wait_apart(pool, msg_ready, 2 * (g + 1), passed)
                    if back:
                        wait_apart(pool, landed, g * 64, passed)
                    for j in range(T):
                        at = bass.IndirectOffsetOnAxis(ap=to[:, s, j:j + 1], axis=0)
                        pool.indirect_dma_start(table, at, sums[:, s, j, :], None, compute_op=ALU.add
                                                ).then_inc(landed, 16)
                over_groups(pool, EG, (scatter, 0))
                pool.wait_ge(landed, EG * 64)


def dram(nc, name, rows, w=D):
    return nc.dram_tensor(name, (rows, w), F32, kind="Internal").ap()


def gnn_stack(nc, a, out):
    h1, x1, x2 = dram(nc, "h1", N), dram(nc, "x1", N), dram(nc, "x2", PAD_ROW + 1)
    acc1 = dram(nc, "acc1", ROWS, CW)
    acc2, acc4 = dram(nc, "acc2", ROWS), dram(nc, "acc4", ROWS)
    x, ends, dst_rows, ew = a["x"], a["ends"], a["dst_rows"], a["edge_factor"]
    with ExitStack() as ctx:
        sh = Shared(nc, ctx)
        load_constants(nc, sh, a["ident"], a["before"], a["spare"], a["counting"])
        linear_edges(nc, sh, "edges1_", x, acc1, CW, a["gcn_w"][0, :, D:2 * D], ends, dst_rows, scale=ew, norm=True,
                     clear_first=True, clear_next=acc2)
        gcn_nodes(nc, sh, "nodes1_", x, acc1, CW, a["gcn_w"][0], a["gcn_b"][0], h1, norm=True)
        linear_edges(nc, sh, "edges2_", h1, acc2, D, a["gcn_w"][1, :, D:2 * D], ends, dst_rows, scale=ew, clear_next=acc4,
                     find_share=a["dst_by_tile"])
        gcn_nodes(nc, sh, "nodes2_", h1, acc2, D, a["gcn_w"][1], a["gcn_b"][1], x1,
                  last_layer=(x, a["agg_wT"], a["agg_b"]), copy=x2)
        linear_edges(nc, sh, "edges3_", x1, x2, D, a["mean_wT"], ends, dst_rows, norm=True, bias=a["mean_b"], share=True)
        mlp_edges(nc, sh, "edges4_", x2, acc4, a["w_msg1"], a["b_msg1"], a["w_msg2"], a["b_msg2"], ends, dst_rows,
                  a["attrT"])
        gated_nodes(nc, sh, "nodes4_", x2, acc4, a["w_z"], a["w_r"], a["w_h"], a["b_z"], a["b_r"], a["b_h"], out)
        attend(nc, sh, "attend_", out, a["att_w"], a["att_wT"], a["att_a"], ends, a["src_rows"], a["outside"])


def kernel(x, src, dst, edge_attr_4, edge_weight, L0_gnn_W_self, L0_gnn_b_self, L0_gnn_W_neigh, L0_gnn_b_neigh,
           L0_gnn_layer_bias, L0_gnn_W_agg, L0_gnn_b_agg, L1_gnn_W, L1_gnn_b, L2_gnn_W_msg1, L2_gnn_b_msg1,
           L2_gnn_W_msg2, L2_gnn_b_msg2, L2_gnn_W_z, L2_gnn_b_z, L2_gnn_W_r, L2_gnn_b_r, L2_gnn_W_h, L2_gnn_b_h,
           L3_gnn_W, L3_gnn_a):
    import numpy as np
    import concourse.bacc as bacc
    from concourse.bass_utils import run_bass_kernel_spmd

    def padded(v, fill):
        return np.concatenate([np.asarray(v), np.full((EG * GW - E,) + v.shape[1:], fill, v.dtype)])

    def by_tile(v):
        return v.reshape(EG, T, P).transpose(0, 2, 1)

    src_key, dst_key = padded(src, PAD_ROW), padded(dst, PAD_ROW)
    position = np.arange(EG * GW).reshape(EG * T, P).T
    arrays = {
        "x": x,
        "ends": np.concatenate([by_tile(v) for v in (padded(src, 0), padded(dst, 0), dst_key, src_key)], 2),
        "dst_rows": dst_key.reshape(EG, GW),
        "src_rows": src_key.reshape(EG, GW),
        "edge_factor": by_tile(padded(edge_weight, 0)),
        "attrT": padded(edge_attr_4, 0).T,
        "ident": np.eye(P, dtype=np.float32),
        "before": np.concatenate([np.ones((P, 3 * P)), np.tril(np.ones((P, P)), -1)], 1).astype(np.float32),
        "spare": (N + np.arange(GW).reshape(T, P).T).astype(np.float32),
        "dst_by_tile": dst_key.reshape(EG * T, P).T, "src_by_tile": src_key.reshape(EG * T, P).T,
        "counting": np.arange(NG * T, dtype=np.float32).reshape(1, NG * T),
        "outside": np.where(position < E, 0.0, OUTSIDE).astype(np.float32),
        "gcn_w": np.concatenate([np.transpose(L0_gnn_W_self, (0, 2, 1)), np.transpose(L0_gnn_W_neigh, (0, 2, 1))], 2),
        "gcn_b": np.stack([L0_gnn_b_self, L0_gnn_b_neigh, L0_gnn_layer_bias], 1),
        "agg_wT": np.transpose(L0_gnn_W_agg), "agg_b": np.reshape(L0_gnn_b_agg, (1, D)),
        "mean_wT": np.transpose(L1_gnn_W), "mean_b": np.reshape(L1_gnn_b, (1, D)),
        "w_msg1": L2_gnn_W_msg1, "b_msg1": np.reshape(L2_gnn_b_msg1, (D, 1)),
        "w_msg2": L2_gnn_W_msg2, "b_msg2": np.reshape(L2_gnn_b_msg2, (1, D)),
        "w_z": L2_gnn_W_z, "b_z": np.reshape(L2_gnn_b_z, (D, 1)),
        "w_r": L2_gnn_W_r, "b_r": np.reshape(L2_gnn_b_r, (D, 1)),
        "w_h": L2_gnn_W_h, "b_h": np.reshape(L2_gnn_b_h, (D, 1)),
        "att_w": L3_gnn_W, "att_wT": np.transpose(L3_gnn_W), "att_a": np.reshape(L3_gnn_a, (2, D)).T,
    }
    nc = bacc.Bacc("TRN2", target_bir_lowering=False, num_devices=1)
    given, aps = {}, {}
    for name, v in arrays.items():
        v = np.ascontiguousarray(v)
        given[f"in_{name}"] = v
        aps[name] = nc.dram_tensor(f"in_{name}", v.shape, mybir.dt.from_np(v.dtype), kind="ExternalInput").ap()
    out = nc.dram_tensor("out", (PAD_ROW + 1, D), F32, kind="ExternalOutput").ap()
    gnn_stack(nc, aps, out)
    result = run_bass_kernel_spmd(nc, [given], core_ids=[0])
    return result.results[0]["out"][0:N]
```

```python
from contextlib import ExitStack

import concourse.bass as bass
from concourse import mybir

ALU = mybir.AluOpType
ACT = mybir.ActivationFunctionType
F32 = mybir.dt.float32
I32 = mybir.dt.int32
AX_X = mybir.AxisListType.X
RMAX = bass.bass_isa.ReduceOp.max
RADD = bass.bass_isa.ReduceOp.add

P = 128
D = 128
T = 4
R = 4
GW = P * T
N = 50000
E = 25000
EG = -(-E // GW)
NG = -(-N // GW)
PAD_ROW = N + GW
ZR = -(-(PAD_ROW + 1) // (P * EG))
ROWS = ZR * P * EG
CW = D + 4
ZW = 4096
EPS = 1e-5
SLOPE = 0.2
OUTSIDE = -3e38

SRC, DST, DST_KEY, SRC_KEY = 0, T, 2 * T, 3 * T


def over_groups(eng, n, *parts, last=0, ring=R):
    R = ring
    latest = max(delay for _, delay in parts)
    ahead = max(0, -min(delay for _, delay in parts))
    first, end = -(-(R + latest) // R) * R, (n - ahead - last) // R * R

    def peeled(i):
        for part, delay in parts:
            g = i - delay
            if 0 <= g < n:
                part(g, g % R, g // R, min(g, R))

    for i in range(-ahead, first):
        peeled(i)
    with eng.Fori(first // R, end // R) as k:
        for s in range(R):
            for part, delay in parts:
                g = s - delay
                part(k * R + g, g % R, k + g // R, R)
    for i in range(end, n + latest):
        peeled(i)


def wait_apart(eng, sem, value, passed):
    eng.wait_ge(sem, value)
    eng.sem_inc(passed, 1)


def await_overlapped(eng, stored, g, per_store=16):
    if isinstance(g, int) and g == NG - 1:
        before = g - 1
        eng.wait_ge(stored[before % len(stored)], per_store * (before // len(stored) + 1))


class Chain:

    def __init__(self, eng, sem, per_group, passed):
        self.passed = passed
        self.eng, self.sem, self.per_group, self.n = eng, sem, per_group, per_group

    def start(self, g):
        assert self.n == self.per_group
        self.base, self.n = g * self.per_group, 0

    def done(self, instruction, apart=False):
        instruction.then_inc(self.sem, 1)
        self.n += 1
        if apart:
            wait_apart(self.eng, self.sem, self.base + self.n, self.passed)
        else:
            self.eng.wait_ge(self.sem, self.base + self.n)


def tiled(ap):
    return ap.rearrange("p (j d) -> p j d", j=T)


def rows_of(table, g, w=D):
    first = N - GW if isinstance(g, int) and g == NG - 1 else g * GW
    return table[bass.ds(first, GW), 0:w].rearrange("(p j) d -> p (j d)", j=T)


class Shared:

    def __init__(self, nc, ctx):
        self.nc, self.ctx = nc, ctx
        self.ident = self.keep("ident", [P, P])
        self.before = self.keep("before", [P, GW])
        self.spare = self.keep("spare", [P, T])
        self.zeros = self.keep("zeros", [P, ZW])
        self.degree = self.keep("degree", [P, NG * T])
        self.share = self.keep("share", [P, EG * T])
        self.score = self.keep("score", [P, NG * T])
        self.lanes = self.keep("lanes", [P, P])
        self.columns = self.keep("columns", [P, NG * T])
        self.mean = self.keep("mean", [P, NG * T])
        self.scale = self.keep("scale", [P, NG * T])
        self.eps = self.keep("eps", [P, 1])
        self.junk = self.keep("junk", [P, T, GW])

    def keep(self, name, shape, dt=F32):
        return self.ctx.enter_context(self.nc.sbuf_tensor(name, shape, dt))

    def sem(self, name):
        return self.ctx.enter_context(self.nc.semaphore(name))


class Phase:

    def __init__(self, sh, tag, ctx):
        self.nc, self.tag, self.ctx, self.sems = sh.nc, tag, ctx, []
        ctx.callback(self.end)

    def sb(self, name, shape, dt=F32):
        return self.ctx.enter_context(self.nc.sbuf_tensor(self.tag + name, shape, dt))

    def ps(self, name, shape):
        return self.ctx.enter_context(self.nc.psum_tensor(self.tag + name, shape, F32))

    def sem(self, name):
        self.sems.append(self.nc.alloc_semaphore(name=self.tag + name))
        return self.sems[-1]

    def end(self):
        if self.sems:
            self.nc.clear_and_free_semaphores(self.sems)
            self.nc.all_engine_barrier()


def load_constants(nc, sh, ident, before, spare, counting):
    loaded, cleared = sh.sem("constants_loaded"), sh.sem("zeros_set")
    with nc.Block() as block:
        @block.sync
        def _(sp):
            sp.dma_start(sh.ident[:, :], ident).then_inc(loaded, 16)
            sp.dma_start(sh.before[:, :], before).then_inc(loaded, 16)
            sp.dma_start(sh.spare[:, :], spare).then_inc(loaded, 16)
            sp.dma_start(sh.lanes[:, :], counting[:, 0:P].to_broadcast([P, P])).then_inc(loaded, 16)
            sp.dma_start(sh.columns[:, :], counting[:, 0:NG * T].to_broadcast([P, NG * T])).then_inc(loaded, 16)
            sp.wait_ge(loaded, 80)

        @block.vector
        def _(dve):
            nc.vector.memset(sh.eps[:, :], EPS).then_inc(cleared, 1)
            nc.vector.memset(sh.zeros[:, :], 0.0).then_inc(cleared, 1)
            dve.wait_ge(cleared, 2)


NORM_STEPS = 2


def normalise(nc, chain, x, stats, mv, rstd, measured, root_ready, g):
    n = x.shape[1]
    for j in range(n):
        last = nc.vector.bn_stats(stats[:, j, :], x[:, j, :])
    chain.done(last, apart=True)
    for j in range(n):
        last = nc.vector.bn_aggr(mv[:, j, :], stats[:, j, :])
    last.then_inc(measured, 1)
    chain.eng.wait_ge(root_ready, g + 1)
    chain.done(nc.vector.reciprocal(rstd[:, 0:n], rstd[:, 0:n]))
    for j in range(n):
        last = nc.vector.tensor_scalar(x[:, j, :], x[:, j, :], mv[:, j, 0:1], rstd[:, j:j + 1],
                                       ALU.subtract, ALU.mult)
    return last


UNITE_STEPS = 5


def block_at(batch, b, a=0):
    return (b * (b + 1) // 2 + a) * P


def unite(nc, sh, chain, batch, eq, row, key, keyf, count, way):
    size = block_at(batch, batch)
    chain.done(nc.vector.tensor_copy(keyf, key))
    for j in range(T):
        first, b = j // batch * batch, j % batch
        at = j // batch * size + block_at(batch, b)
        last = nc.vector.tensor_scalar(eq[:, at:at + (b + 1) * P], row[:, first * P:(j + 1) * P],
                                       keyf[:, j:j + 1], None, ALU.is_equal)
    chain.done(last)
    chain.done(nc.vector.tensor_tensor(way, sh.spare[:, :], keyf, ALU.subtract))
    for j in range(T):
        b = j % batch
        at = j // batch * size + block_at(batch, b)
        last = nc.vector.tensor_tensor_reduce(
            sh.junk[:, j, 0:(b + 1) * P], eq[:, at:at + (b + 1) * P], sh.before[:, (T - 1 - b) * P:GW],
            1.0, 0.0, ALU.mult, ALU.add, count[:, j:j + 1])
    chain.done(last)
    chain.done(nc.vector.scalar_tensor_tensor(way, count[:, :], 0.0, way, ALU.is_gt, ALU.mult))


def batch_sums(pe, batch, out, eq, msg, w):
    size = block_at(batch, batch)
    for j in range(T):
        first, a = j // batch * batch, j % batch
        for b in range(a, batch):
            at = j // batch * size + block_at(batch, b, a)
            last = pe.matmul(out(j), eq[:, at:at + P], msg[:, first + b, 0:w], start=(b == a), stop=(b == batch - 1))
    return last


class Lookup:

    def __init__(self, ph, sh, table, nodes):
        self.sh, self.table, self.nodes = sh, table, nodes
        self.keys, self.places = ph.sb("all_keys", [P, EG * T], I32), ph.sb("places", [P, EG * T], I32)
        self.lane, self.column = ph.sb("lane", [P, EG * T]), ph.sb("column", [P, EG * T])
        self.mark, self.markT = ph.sb("mark", [P, R, GW]), ph.sb("markT", [P, R, GW])
        self.chosen, self.value = ph.sb("chosen", [P, T, NG * T]), ph.sb("value", [P, R, T])
        self.result = ph.sb("result", [P, EG * T])
        self.psE, self.psL = ph.ps("psE", [P, GW]), ph.ps("psL", [P, T, GW])
        self.keys_in, self.placed = ph.sem("all_keys_in"), ph.sem("placed")
        self.marked, self.turned, self.markT_ready = ph.sem("marked"), ph.sem("marks_turned"), ph.sem("markT_ready")
        self.looked, self.found, self.noted = ph.sem("looked"), ph.sem("found"), ph.sem("noted")

    def load(self, sp):
        sp.dma_start(self.keys[:, :], self.nodes).then_inc(self.keys_in, 16)

    def place(self, nc, dve):
        keys, places, placed = self.keys[:, :], self.places[:, :], self.placed
        last_group = (NG - 1) * GW
        dve.wait_ge(self.keys_in, 16)
        nc.vector.tensor_scalar(places, keys, last_group, last_group - (N - GW), ALU.is_ge, ALU.mult).then_inc(placed, 1)
        dve.wait_ge(placed, 1)
        nc.vector.tensor_tensor(keys, keys, places, ALU.add).then_inc(placed, 1)
        dve.wait_ge(placed, 2)
        nc.vector.tensor_scalar(places, keys, 2, P - 1, ALU.logical_shift_right, ALU.bitwise_and).then_inc(placed, 1)
        dve.wait_ge(placed, 3)
        nc.vector.tensor_copy(self.lane[:, :], places).then_inc(placed, 1)
        dve.wait_ge(placed, 4)
        nc.vector.tensor_scalar(places, keys, 9, 2, ALU.logical_shift_right, ALU.logical_shift_left).then_inc(placed, 1)
        nc.vector.tensor_scalar(keys, keys, T - 1, None, ALU.bitwise_and).then_inc(placed, 1)
        dve.wait_ge(placed, 6)
        nc.vector.tensor_tensor(self.column[:, :], places, keys, ALU.add).then_inc(placed, 1)
        dve.wait_ge(placed, 7)

    def vector_parts(self, nc, dve):
        def mark(g, s, k, back):
            if back == R:
                dve.wait_ge(self.turned, g - R + 1)
            for j in range(T):
                i = nc.vector.tensor_scalar(self.mark[:, s, j * P:(j + 1) * P], self.sh.lanes[:, :],
                                            self.lane[:, bass.ds(g * T + j, 1)], None, ALU.is_equal)
            i.then_inc(self.marked, 1)

        def choose(g, s, k, back):
            dve.wait_ge(self.looked, g + 1)
            if back == R:
                dve.wait_ge(self.noted, g - R + 1)
            for j in range(T):
                i = nc.vector.scalar_tensor_tensor(
                    self.chosen[:, j, :], self.sh.columns[:, :], self.column[:, bass.ds(g * T + j, 1)],
                    self.psL[:, j, 0:NG * T], ALU.is_equal, ALU.mult, accum_out=self.value[:, s, j:j + 1])
            i.then_inc(self.found, 1)

        def note(g, s, k, back):
            dve.wait_ge(self.found, g + 1)
            nc.vector.tensor_copy(self.result[:, bass.ds(g * T, T)], self.value[:, s, :]).then_inc(self.noted, 1)
        return (choose, 4), (mark, 0), (note, 5)

    def tensor_parts(self, pe):
        def turn_marks(g, s, k, back):
            pe.wait_ge(self.marked, g + 1)
            if back:
                pe.wait_ge(self.markT_ready, g)
            for j in range(T):
                i = pe.transpose(self.psE[:, j * P:(j + 1) * P], self.mark[:, s, j * P:(j + 1) * P], self.sh.ident[:, :])
            i.then_inc(self.turned, 1)

        def look(g, s, k, back):
            pe.wait_ge(self.markT_ready, g + 1)
            if back:
                pe.wait_ge(self.found, g)
            for j in range(T):
                i = pe.matmul(self.psL[:, j, 0:NG * T], self.markT[:, s, j * P:(j + 1) * P], self.table[:, :],
                              start=True, stop=True)
            i.then_inc(self.looked, 1)
        return (look, 3), (turn_marks, 1)

    def scalar_parts(self, nc, act):
        def turned_marks(g, s, k, back):
            act.wait_ge(self.turned, g + 1)
            if back == R:
                act.wait_ge(self.looked, g - R + 1)
            nc.scalar.activation(self.markT[:, s, :], self.psE[:, :], ACT.Copy).then_inc(self.markT_ready, 1)
        return ((turned_marks, 1),)


def linear_edges(nc, sh, tag, table, acc, w, weight, ends, dst_rows, scale=None, norm=False, bias=None,
                 clear_first=False, clear_next=None,
                 find_share=None, share=False):
    with ExitStack() as ctx:
        ph = Phase(sh, tag, ctx)
        W, B = ph.sb("weight", [P, D]), ph.sb("bias", [P, D])
        end, key = ph.sb("ends", [P, R, T], I32), ph.sb("keys", [P, R, T], I32)
        row = ph.sb("key_row", [P, R, GW], I32)
        factor = ph.sb("factor", [P, R, T])
        x = ph.sb("x", [P, R, T, D])
        hT = ph.sb("hT", [P, GW])
        msg = ph.sb("msg", [P, R, T, w])
        eq = ph.sb("eq", [P, R, block_at(T, T)])
        keyf, count, way = ph.sb("keyf", [P, R, T]), ph.sb("count", [P, T]), ph.sb("way", [P, R, T])
        stats, mv, rstd = ph.sb("stats", [P, T, 6]), ph.sb("mv", [P, T, 2]), ph.sb("rstd", [P, T])
        to = ph.sb("to", [P, R, T], I32)
        sums = ph.sb("sums", [P, R, T, w])
        halves = -(-T * w // GW)
        psT, psM, psS = ph.ps("psT", [P, GW]), ph.ps("psM", [P, GW]), ph.ps("psS", [P, halves, GW])
        if find_share is not None:
            find = Lookup(ph, sh, sh.degree, find_share)

        weights_in = ph.sem("weights_in")
        ends_in = [ph.sem(f"ends_in{s}") for s in range(R)]
        loaded = [ph.sem(f"keys_in{s}") for s in range(R)]
        gathered = [ph.sem(f"rows_gathered{s}") for s in range(R)]
        cleared, next_cleared = ph.sem("acc_cleared"), ph.sem("next_cleared")
        ones_set, own, united, normed = ph.sem("ones_set"), ph.sem("norm_steps"), ph.sem("unite_steps"), ph.sem("rows_normed")
        measured, root_ready = ph.sem("rows_measured"), ph.sem("root_ready")
        turned, hT_ready, product = ph.sem("rows_turned"), ph.sem("hT_ready"), ph.sem("product")
        msg_ready, summed, sums_ready = ph.sem("msg_ready"), ph.sem("summed"), ph.sem("sums_ready")
        landed, shared = ph.sem("scatters_landed"), ph.sem("shared")
        per_load = 16 * (3 if scale is not None else 2)
        n_weights = 16 * (1 if bias is None else 2)
        clears = -(-ROWS * w // P // ZW)

        block = ctx.enter_context(nc.Block())

        @block.sync
        def _(sp):
            sp.dma_start(W[:, :], weight).then_inc(weights_in, 16)
            if find_share is not None:
                find.load(sp)
            if bias is not None:
                sp.dma_start(B[:, :], bias.to_broadcast([P, D])).then_inc(weights_in, 16)

            def load(g, s, k, back):
                if back == R:
                    sp.wait_ge(gathered[s], k * 64)
                sp.dma_start(end[:, s, :], ends[g, :, SRC:SRC + T]).then_inc(ends_in[s], 16)
                if back == R:
                    sp.wait_ge(msg_ready, 2 * (g - R + 1))
                sp.dma_start(key[:, s, :], ends[g, :, DST_KEY:DST_KEY + T]).then_inc(loaded[s], 16)
                sp.dma_start(row[:, s, :], dst_rows[bass.ds(g, 1), :].to_broadcast([P, GW])).then_inc(loaded[s], 16)
                if scale is not None:
                    sp.dma_start(factor[:, s, :], scale[g, :, :]).then_inc(loaded[s], 16)
                if clear_next is not None:
                    part = clear_next[bass.ds(g * (P * ZR), P * ZR), :]
                    sp.dma_start(part.rearrange("(p r) d -> p (r d)", p=P), sh.zeros[:, 0:ZR * part.shape[1]]
                                 ).then_inc(next_cleared, 16)
            over_groups(sp, EG, (load, 0))
            if clear_next is not None:
                sp.wait_ge(next_cleared, 16 * EG)

        @block.gpsimd
        def _(pool):
            passed = ph.sem("pool_waits_passed")
            def gather(s, j):
                at = bass.IndirectOffsetOnAxis(ap=end[:, s, j:j + 1], axis=0)
                pool.indirect_dma_start(x[:, s, j, :], None, table, at).then_inc(gathered[s], 16)

            for s in range(R):
                pool.wait_ge(ends_in[s], 16)
                for j in range(T):
                    gather(s, j)
            if clear_first:
                pool.wait_ge(cleared, 16 * clears)

            def scatter(g, s, k, back):
                ahead = not isinstance(g, int) or g + R < EG
                pool.wait_ge(sums_ready, g + 1)
                wait_apart(pool, msg_ready, 2 * (g + 1), passed)
                if ahead:
                    pool.wait_ge(ends_in[s], (k + 2) * 16)
                    wait_apart(pool, turned, g + 1, passed)
                for j in range(T):
                    at = bass.IndirectOffsetOnAxis(ap=to[:, s, j:j + 1], axis=0)
                    pool.indirect_dma_start(acc, at, sums[:, s, j, :], None, compute_op=ALU.add).then_inc(landed, 16)
                if ahead:
                    for j in range(T):
                        gather(s, j)
                wait_apart(pool, landed, (g + 1) * 64, passed)
            over_groups(pool, EG, (scatter, 0), last=R)

        @block.vector
        def _(dve):
            passed = ph.sem("dve_waits_passed")
            norms = Chain(dve, own, NORM_STEPS, passed)
            unites = Chain(dve, united, UNITE_STEPS, passed)
            nc.vector.memset(msg[:, :, :, :], 1.0).then_inc(ones_set, 1)
            dve.wait_ge(ones_set, 1)
            dve.wait_ge(weights_in, n_weights)

            def norm_rows(g, s, k, back):
                norms.start(g)
                dve.wait_ge(gathered[s], (k + 1) * 64)
                normalise(nc, norms, x[:, s], stats, mv, rstd, measured, root_ready, g).then_inc(normed, 1)

            def unite_edges(g, s, k, back):
                unites.start(g)
                dve.wait_ge(loaded[s], (k + 1) * per_load)
                if back == R:
                    dve.wait_ge(summed, g - R + 1)
                unite(nc, sh, unites, T, eq[:, s], row[:, s], key[:, s], keyf[:, s], count, way[:, s])

            def messages(g, s, k, back):
                dve.wait_ge(product, g + 1)
                if back == R:
                    dve.wait_ge(landed, (g - R + 1) * 64)
                nc.vector.tensor_tensor(to[:, s, :], way[:, s, :], keyf[:, s, :], ALU.add).then_inc(msg_ready, 1)
                if scale is not None:
                    by = factor[:, s, :].unsqueeze(2).to_broadcast([P, T, D])
                    last = nc.vector.tensor_tensor(msg[:, s, :, 0:D], tiled(psM[:, :]), by, ALU.mult)
                else:
                    by = B[:, :].unsqueeze(1).to_broadcast([P, T, D])
                    last = nc.vector.tensor_tensor(msg[:, s, :, 0:D], tiled(psM[:, :]), by, ALU.add)
                last.then_inc(msg_ready, 1)
            if find_share is not None:
                find.place(nc, dve)
            over_groups(dve, EG, *([(norm_rows, 0)] if norm else []), (messages, 1), (unite_edges, -1),
                        *(find.vector_parts(nc, dve) if find_share is not None else []))
            if find_share is not None:
                edge_share = find.result
                dve.wait_ge(find.noted, EG)
                nc.vector.tensor_scalar(edge_share[:, :], edge_share[:, :], 1.0, None, ALU.max).then_inc(shared, 1)
                dve.wait_ge(shared, 1)
                nc.vector.reciprocal(sh.share[:, :], edge_share[:, :]).then_inc(shared, 1)
                dve.wait_ge(shared, 2)

        @block.tensor
        def _(pe):
            pe.wait_ge(weights_in, n_weights)

            def turn(g, s, k, back):
                if norm:
                    pe.wait_ge(normed, g + 1)
                else:
                    pe.wait_ge(gathered[s], (k + 1) * 64)
                if back:
                    pe.wait_ge(hT_ready, g)
                for j in range(T):
                    last = pe.transpose(psT[:, j * P:(j + 1) * P], x[:, s, j, :], sh.ident[:, :])
                last.then_inc(turned, 1)

            def multiply(g, s, k, back):
                pe.wait_ge(hT_ready, g + 1)
                if back:
                    pe.wait_ge(msg_ready, 2 * g)
                for j in range(T):
                    last = pe.matmul(psM[:, j * D:(j + 1) * D], hT[:, j * P:(j + 1) * P], W[:, :],
                                     start=True, stop=True)
                last.then_inc(product, 1)

            def add_up(g, s, k, back):
                pe.wait_ge(msg_ready, 2 * (g + 1))
                if back:
                    pe.wait_ge(sums_ready, g)
                per = T // halves
                batch_sums(pe, T, lambda j: psS[:, j // per, j % per * w:(j % per + 1) * w], eq[:, s], msg[:, s], w
                           ).then_inc(summed, 1)
            over_groups(pe, EG, (turn, 0), (add_up, 1), (multiply, 0),
                        *(find.tensor_parts(pe) if find_share is not None else []))

        @block.scalar
        def _(act):
            if clear_first:
                flat = acc.rearrange("(p r) d -> p (r d)", p=P)
                for c in range(clears):
                    m = min(ZW, flat.shape[1] - c * ZW)
                    act.dma_start(flat[:, c * ZW:c * ZW + m], sh.zeros[:, 0:m]).then_inc(cleared, 16)

            def transposed(g, s, k, back):
                if norm:
                    act.wait_ge(measured, g + 1)
                    nc.scalar.activation(rstd[:, :], mv[:, :, 1], ACT.Sqrt, bias=sh.eps[:, :]).then_inc(root_ready, 1)
                act.wait_ge(turned, g + 1)
                if back:
                    act.wait_ge(product, g)
                nc.scalar.activation(hT[:, :], psT[:, :], ACT.Relu if norm else ACT.Copy).then_inc(hT_ready, 1)

            def sums_out(g, s, k, back):
                act.wait_ge(summed, g + 1)
                if back == R:
                    act.wait_ge(landed, (g - R + 1) * 64)
                if share:
                    for j in range(T):
                        i = nc.scalar.activation(sums[:, s, j, :], psS[:, 0, j * D:(j + 1) * D], ACT.Copy,
                                                 scale=sh.share[:, bass.ds(g * T + j, 1)])
                else:
                    i = nc.scalar.activation(sums[:, s, :, :].rearrange("p (q j) d -> p q (j d)", q=halves),
                                             psS[:, :, 0:T // halves * w], ACT.Copy)
                i.then_inc(sums_ready, 1)
            over_groups(act, EG, (transposed, 0), (sums_out, 1),
                        *(find.scalar_parts(nc, act) if find_share is not None else []))


class Measure:

    def __init__(self, ph, sh, table):
        assert NG == 2 * EG
        self.sh, self.table = sh, table
        self.x, self.stats = ph.sb("all_x", [P, R, 2 * T, D]), ph.sb("all_stats", [P, R, 2 * T, 6])
        self.mv, self.root = ph.sb("all_mv", [P, R, 2 * T, 2]), ph.sb("all_root", [P, R, 2 * T])
        self.loaded = [ph.sem(f"all_rows_in{s}") for s in range(R)]
        self.counted, self.measured, self.rooted, self.kept = (ph.sem(n) for n in (
            "all_counted", "all_measured", "all_rooted", "all_kept"))

    def load(self, sp, g, s, back):
        if back == R:
            sp.wait_ge(self.counted, g - R + 1)
        for half in range(2):
            rows = self.x[:, s, half * T:(half + 1) * T, :].rearrange("p j d -> p (j d)")
            sp.dma_start(rows, rows_of(self.table, g * 2 + half)).then_inc(self.loaded[s], 16)

    def vector_parts(self, nc, dve, passed):
        def count(g, s, k, back):
            dve.wait_ge(self.loaded[s], (k + 1) * 32)
            if back == R:
                dve.wait_ge(self.measured, g - R + 1)
            for j in range(2 * T):
                i = nc.vector.bn_stats(self.stats[:, s, j, :], self.x[:, s, j, :])
            i.then_inc(self.counted, 1)

        def measure(g, s, k, back):
            wait_apart(dve, self.counted, g + 1, passed)
            for j in range(2 * T):
                i = nc.vector.bn_aggr(self.mv[:, s, j, :], self.stats[:, s, j, :])
            i.then_inc(self.measured, 1)

        def keep(g, s, k, back):
            at = bass.ds(g * (2 * T), 2 * T)
            dve.wait_ge(self.measured, g + 1)
            dve.wait_ge(self.rooted, g + 1)
            nc.vector.tensor_copy(self.sh.mean[:, at], self.mv[:, s, :, 0]).then_inc(self.kept, 1)
            nc.vector.reciprocal(self.sh.scale[:, at], self.root[:, s, :]).then_inc(self.kept, 1)
        return count, measure, keep

    def take_root(self, nc, act):
        def take_root(g, s, k, back):
            act.wait_ge(self.measured, g + 1)
            if back == R:
                act.wait_ge(self.kept, 2 * (g - R + 1))
            nc.scalar.activation(self.root[:, s, :], self.mv[:, s, :, 1], ACT.Sqrt, bias=self.sh.eps[:, :]
                                 ).then_inc(self.rooted, 1)
        return take_root


def mlp_edges(nc, sh, tag, table, acc, w1, b1, w2, b2, ends, dst_rows, attrT):
    with ExitStack() as ctx:
        ph = Phase(sh, tag, ctx)
        W1s, W1d, W2, B2 = (ph.sb(n, [P, D]) for n in ("w1_src", "w1_dst", "w2", "b2"))
        W1e, B1 = ph.sb("w1_attr", [T, D]), ph.sb("b1", [P, 1])
        end, key = ph.sb("ends", [P, R, 2 * T], I32), ph.sb("keys", [P, R, T], I32)
        row = ph.sb("key_row", [P, R, GW], I32)
        attr = ph.sb("attr", [4, R, GW])
        x = ph.sb("x", [P, R, 2 * T, D])
        hT, hidden = ph.sb("hT", [P, 2 * GW]), ph.sb("hidden", [P, GW])
        msg = ph.sb("msg", [P, R, T, D])
        eq = ph.sb("eq", [P, R, block_at(T, T)])
        keyf, count, way = ph.sb("keyf", [P, R, T]), ph.sb("count", [P, T]), ph.sb("way", [P, R, T])
        stats, mv, rstd = ph.sb("stats", [P, 2 * T, 6]), ph.sb("mv", [P, 2 * T, 2]), ph.sb("rstd", [P, 2 * T])
        to = ph.sb("to", [P, R, T], I32)
        sums = ph.sb("sums", [P, R, T, D])
        psT, psH, psM, psS = ph.ps("psT", [P, 2 * GW]), ph.ps("psH", [P, GW]), ph.ps("psM", [P, GW]), ph.ps("psS", [P, GW])

        weights_in = ph.sem("weights_in")
        ends_in = [ph.sem(f"ends_in{s}") for s in range(R)]
        loaded = [ph.sem(f"keys_in{s}") for s in range(R)]
        gathered = [ph.sem(f"rows_gathered{s}") for s in range(R)]
        own, united, normed = ph.sem("norm_steps"), ph.sem("unite_steps"), ph.sem("rows_normed")
        measured, root_ready = ph.sem("rows_measured"), ph.sem("root_ready")
        turned, hT_ready, preact = ph.sem("rows_turned"), ph.sem("hT_ready"), ph.sem("preactivation")
        hidden_ready, product, msg_ready = ph.sem("hidden_ready"), ph.sem("product"), ph.sem("msg_ready")
        summed, sums_ready, landed = ph.sem("summed"), ph.sem("sums_ready"), ph.sem("scatters_landed")

        every = Measure(ph, sh, table)

        block = ctx.enter_context(nc.Block())

        @block.sync
        def _(sp):
            for dst, src in ((W1s[:, :], w1[0:D, :]), (W1d[:, :], w1[D:2 * D, :]), (W1e[:, :], w1[2 * D:2 * D + 4, :]),
                             (W2[:, :], w2), (B1[:, :], b1), (B2[:, :], b2.to_broadcast([P, D]))):
                sp.dma_start(dst, src).then_inc(weights_in, 16)

            def load(g, s, k, back):
                if back == R:
                    sp.wait_ge(gathered[s], k * 128)
                sp.dma_start(end[:, s, :], ends[g, :, SRC:SRC + 2 * T]).then_inc(ends_in[s], 16)
                if back == R:
                    sp.wait_ge(msg_ready, 2 * (g - R + 1))
                sp.dma_start(key[:, s, :], ends[g, :, DST_KEY:DST_KEY + T]).then_inc(loaded[s], 16)
                sp.dma_start(row[:, s, :], dst_rows[bass.ds(g, 1), :].to_broadcast([P, GW])).then_inc(loaded[s], 16)
                sp.dma_start(attr[:, s, :], attrT[:, bass.ds(g * GW, GW)]).then_inc(loaded[s], 16)
                every.load(sp, g, s, back)
            over_groups(sp, EG, (load, 0))

        @block.gpsimd
        def _(pool):
            passed = ph.sem("pool_waits_passed")
            def gather(s, j):
                at = bass.IndirectOffsetOnAxis(ap=end[:, s, j:j + 1], axis=0)
                pool.indirect_dma_start(x[:, s, j, :], None, table, at).then_inc(gathered[s], 16)

            for s in range(R):
                pool.wait_ge(ends_in[s], 16)
                for j in range(2 * T):
                    gather(s, j)

            def scatter(g, s, k, back):
                ahead = not isinstance(g, int) or g + R < EG
                pool.wait_ge(sums_ready, g + 1)
                wait_apart(pool, msg_ready, 2 * (g + 1), passed)
                if ahead:
                    pool.wait_ge(ends_in[s], (k + 2) * 16)
                    wait_apart(pool, turned, g + 1, passed)
                for j in range(T):
                    at = bass.IndirectOffsetOnAxis(ap=to[:, s, j:j + 1], axis=0)
                    pool.indirect_dma_start(acc, at, sums[:, s, j, :], None, compute_op=ALU.add).then_inc(landed, 16)
                if ahead:
                    for j in range(2 * T):
                        gather(s, j)
                wait_apart(pool, landed, (g + 1) * 64, passed)
            over_groups(pool, EG, (scatter, 0), last=R)

        @block.vector
        def _(dve):
            passed = ph.sem("dve_waits_passed")
            norms = Chain(dve, own, NORM_STEPS, passed)
            unites = Chain(dve, united, UNITE_STEPS, passed)
            dve.wait_ge(weights_in, 96)

            def norm_rows(g, s, k, back):
                norms.start(g)
                dve.wait_ge(gathered[s], (k + 1) * 128)
                normalise(nc, norms, x[:, s], stats, mv, rstd, measured, root_ready, g).then_inc(normed, 1)

            def unite_edges(g, s, k, back):
                unites.start(g)
                dve.wait_ge(loaded[s], (k + 1) * 48)
                if back == R:
                    dve.wait_ge(summed, g - R + 1)
                unite(nc, sh, unites, T, eq[:, s], row[:, s], key[:, s], keyf[:, s], count, way[:, s])

            def messages(g, s, k, back):
                dve.wait_ge(product, g + 1)
                if back == R:
                    dve.wait_ge(landed, (g - R + 1) * 64)
                nc.vector.tensor_tensor(to[:, s, :], way[:, s, :], keyf[:, s, :], ALU.add).then_inc(msg_ready, 1)
                by = B2[:, :].unsqueeze(1).to_broadcast([P, T, D])
                nc.vector.tensor_tensor(msg[:, s, :, :], tiled(psM[:, :]), by, ALU.add).then_inc(msg_ready, 1)
            count_all, measure_all, keep_all = every.vector_parts(nc, dve, passed)
            over_groups(dve, EG, (norm_rows, 0), (messages, 1), (count_all, 0), (unite_edges, -1), (measure_all, 0), (keep_all, 1))
            dve.wait_ge(every.kept, 2 * EG)

        @block.tensor
        def _(pe):
            pe.wait_ge(weights_in, 96)

            def turn(g, s, k, back):
                pe.wait_ge(normed, g + 1)
                if back:
                    pe.wait_ge(hT_ready, g)
                for j in range(2 * T):
                    last = pe.transpose(psT[:, j * P:(j + 1) * P], x[:, s, j, :], sh.ident[:, :])
                last.then_inc(turned, 1)

            def first_layer(g, s, k, back):
                pe.wait_ge(loaded[s], (k + 1) * 48)
                pe.wait_ge(hT_ready, g + 1)
                if back:
                    pe.wait_ge(hidden_ready, g)
                pe.matmul(psH[:, :], W1s[:, :], hT[:, 0:GW], start=True, stop=False)
                pe.matmul(psH[:, :], W1d[:, :], hT[:, GW:2 * GW], start=False, stop=False)
                pe.matmul(psH[:, :], W1e[:, :], attr[:, s, :], start=False, stop=True).then_inc(preact, 1)

            def second_layer(g, s, k, back):
                pe.wait_ge(hidden_ready, g + 1)
                if back:
                    pe.wait_ge(msg_ready, 2 * g)
                for j in range(T):
                    last = pe.matmul(psM[:, j * D:(j + 1) * D], hidden[:, j * P:(j + 1) * P], W2[:, :],
                                     start=True, stop=True)
                last.then_inc(product, 1)

            def add_up(g, s, k, back):
                pe.wait_ge(msg_ready, 2 * (g + 1))
                if back:
                    pe.wait_ge(sums_ready, g)
                batch_sums(pe, T, lambda j: psS[:, j * D:(j + 1) * D], eq[:, s], msg[:, s], D).then_inc(summed, 1)
            over_groups(pe, EG, (turn, 0), (add_up, 1), (first_layer, 0), (second_layer, 0))

        @block.scalar
        def _(act):
            act.wait_ge(weights_in, 96)

            def transposed(g, s, k, back):
                act.wait_ge(measured, g + 1)
                nc.scalar.activation(rstd[:, :], mv[:, :, 1], ACT.Sqrt, bias=sh.eps[:, :]).then_inc(root_ready, 1)
                act.wait_ge(turned, g + 1)
                if back:
                    act.wait_ge(preact, g)
                nc.scalar.activation(hT[:, :], psT[:, :], ACT.Relu).then_inc(hT_ready, 1)

            def hide(g, s, k, back):
                act.wait_ge(preact, g + 1)
                if back:
                    act.wait_ge(product, g)
                nc.scalar.activation(hidden[:, :], psH[:, :], ACT.Relu, bias=B1[:, :]).then_inc(hidden_ready, 1)

            def sums_out(g, s, k, back):
                act.wait_ge(summed, g + 1)
                if back == R:
                    act.wait_ge(landed, (g - R + 1) * 64)
                nc.scalar.activation(sums[:, s, :, :].rearrange("p j d -> p (j d)"), psS[:, :], ACT.Copy
                                     ).then_inc(sums_ready, 1)
            over_groups(act, EG, (transposed, 0), (sums_out, 1), (hide, 0), (every.take_root(nc, act), 0))


def gcn_nodes(nc, sh, tag, table, acc, w, weights, biases, out, norm=False, last_layer=None, copy=None):
    R, products = (4, 2) if last_layer else (8, 2)
    with ExitStack() as ctx:
        ph = Phase(sh, tag, ctx)
        n_bias = biases.shape[0]
        W, bias_rows, bias = ph.sb("weights", [P, 2 * D]), ph.sb("bias_rows", [P, n_bias, D]), ph.sb("bias", [P, D])
        x, sums = ph.sb("x", [P, R, T * D]), ph.sb("sums", [P, R, T, w])
        hT = ph.sb("hT", [P, R, GW])
        part = ph.sb("part", [P, R, T * D])
        h = ph.sb("h", [P, R, T * D])
        share = ph.sb("share", [P, R, T])
        stats, mv = ph.sb("stats", [P, T, 6]), ph.sb("mv", [P, R, T, 2])
        rstd, minus = ph.sb("rstd", [P, R, T]), ph.sb("minus_mean", [P, R, T])
        psT, psP = ph.ps("psT", [P, GW]), ph.ps("psP", [P, products, T, 2 * D])
        n_load = 2
        if last_layer:
            res_table, wa, ba = last_layer
            WA, BA = ph.sb("w_last", [P, D]), ph.sb("b_last", [P, D])
            res, new = ph.sb("res", [P, R, T * D]), ph.sb("new", [P, R, T * D])
            h2T = ph.sb("h2T", [P, R, GW])
            psT2, psO = ph.ps("psT2", [P, GW]), ph.ps("psO", [P, GW])
            res_in = [ph.sem(f"res_in{s}") for s in range(R)]
        weights_in, spare_cleared = ph.sem("weights_in"), ph.sem("spare_cleared")
        loaded = [ph.sem(f"rows_in{s}") for s in range(R)]
        stored = [ph.sem(f"stored{s}") for s in range(R)]
        degree_set, totalled, share_ready, bias_set = ph.sem("degree_set"), ph.sem("totalled"), ph.sem("share_ready"), ph.sem("bias_set")
        counted, measured, root_ready = ph.sem("counted"), ph.sem("rows_measured"), ph.sem("root_ready")
        inverted, factors_ready, normed = ph.sem("inverted"), ph.sem("factors_ready"), ph.sem("rows_normed")
        neighbours, scaled = ph.sem("neighbours_added"), ph.sem("scaled")
        turned, hT_ready, product = ph.sem("rows_turned"), ph.sem("hT_ready"), ph.sem("product")
        combined, biased, leaked = ph.sem("combined"), ph.sem("biased"), ph.sem("leaked")
        turned2, h2T_ready, product2 = ph.sem("turned2"), ph.sem("h2T_ready"), ph.sem("product2")
        added, finished = ph.sem("added"), ph.sem("finished")
        per_store = 16 if copy is None else 32
        n_weights = 32 + (32 if last_layer else 0)

        block = ctx.enter_context(nc.Block())

        @block.sync
        def _(sp):
            sp.dma_start(W[:, :], weights).then_inc(weights_in, 16)
            rows = biases.rearrange("(o b) d -> o b d", o=1)
            sp.dma_start(bias_rows[:, :, :], rows.to_broadcast([P, n_bias, D])).then_inc(weights_in, 16)
            if last_layer:
                sp.dma_start(WA[:, :], wa).then_inc(weights_in, 16)
                sp.dma_start(BA[:, :], ba.to_broadcast([P, D])).then_inc(weights_in, 16)

            if copy is not None:
                sp.dma_start(copy[N:PAD_ROW, :].rearrange("(p r) d -> p (r d)", p=P), sh.zeros[:, 0:T * D]
                             ).then_inc(spare_cleared, 16)
                sp.dma_start(copy[PAD_ROW:PAD_ROW + 1, :], sh.zeros[0:1, 0:D]).then_inc(spare_cleared, 16)

            def load(g, s, k, back):
                if back == R:
                    sp.wait_ge(turned, g - R + 1)
                    sp.wait_ge(neighbours, g - R + 1)
                    if norm:
                        sp.wait_ge(degree_set, g - R + 1)
                sp.dma_start(x[:, s, :], rows_of(table, g)).then_inc(loaded[s], 16)
                sp.dma_start(sums[:, s, :, :].rearrange("p j d -> p (j d)"), rows_of(acc, g, w)).then_inc(loaded[s], 16)

            def load_res(g, s, k, back):
                if back == R:
                    sp.wait_ge(finished, g - R + 1)
                sp.dma_start(res[:, s, :], rows_of(res_table, g)).then_inc(res_in[s], 16)
            over_groups(sp, NG, (load, 0), *([(load_res, 2)] if last_layer else []), ring=R)
            if copy is not None:
                sp.wait_ge(spare_cleared, 32)

        @block.vector
        def _(dve):
            passed = ph.sem("dve_waits_passed")
            dve.wait_ge(weights_in, n_weights)
            nc.vector.tensor_tensor(bias[:, :], bias_rows[:, 0, :], bias_rows[:, 1, :], ALU.add).then_inc(bias_set, 1)
            for b in range(2, n_bias):
                dve.wait_ge(bias_set, b - 1)
                nc.vector.tensor_tensor(bias[:, :], bias[:, :], bias_rows[:, b, :], ALU.add).then_inc(bias_set, 1)

            def count(g, s, k, back):
                dve.wait_ge(loaded[s], (k + 1) * 32)
                if back:
                    dve.wait_ge(measured, g)
                for j in range(T):
                    i = nc.vector.bn_stats(stats[:, j, :], x[:, s, j * D:(j + 1) * D])
                i.then_inc(counted, 1)

            def measure(g, s, k, back):
                wait_apart(dve, counted, g + 1, passed)
                for j in range(T):
                    i = nc.vector.bn_aggr(mv[:, s, j, :], stats[:, j, :])
                i.then_inc(measured, 1)

            def invert(g, s, k, back):
                dve.wait_ge(root_ready, g + 1)
                nc.vector.reciprocal(rstd[:, s, :], rstd[:, s, :]).then_inc(inverted, 1)

            def centre(g, s, k, back):
                dve.wait_ge(inverted, g + 1)
                nc.vector.scalar_tensor_tensor(minus[:, s, :], mv[:, s, :, 0], -1.0, rstd[:, s, :], ALU.mult, ALU.mult
                                               ).then_inc(factors_ready, 1)

            def degrees(g, s, k, back):
                dve.wait_ge(loaded[s], (k + 1) * 32)
                nc.vector.tensor_copy(sh.degree[:, bass.ds(g * T, T)], sums[:, s, :, D]).then_inc(degree_set, 1)

            def totals(g, s, k, back):
                if norm:
                    dve.wait_ge(degree_set, g + 1)
                if back == R:
                    dve.wait_ge(combined, g - R + 1)
                nc.vector.tensor_scalar(share[:, s, :], sh.degree[:, bass.ds(g * T, T)], 1.0, None, ALU.add
                                        ).then_inc(totalled, 1)

            def shares(g, s, k, back):
                dve.wait_ge(totalled, g + 1)
                nc.vector.reciprocal(share[:, s, :], share[:, s, :]).then_inc(share_ready, 1)

            def add_neighbours(g, s, k, back):
                dve.wait_ge(loaded[s], (k + 1) * 32)
                dve.wait_ge(product, g + 1)
                if back == R:
                    if last_layer:
                        dve.wait_ge(combined, g - R + 1)
                    else:
                        dve.wait_ge(leaked, g - R + 1)
                nc.vector.tensor_tensor(tiled(part[:, s, :]), psP[:, s % products, :, D:2 * D], sums[:, s, :, 0:D], ALU.add
                                        ).then_inc(neighbours, 1)

            def combine(g, s, k, back):
                dve.wait_ge(neighbours, g + 1)
                dve.wait_ge(share_ready, g + 1)
                if back == R:
                    dve.wait_ge(turned2 if last_layer else leaked, g - R + 1)
                    if not last_layer:
                        dve.wait_ge(stored[s], k * per_store)
                for j in range(T):
                    c = slice(j * D, (j + 1) * D)
                    i = nc.vector.scalar_tensor_tensor(h[:, s, c], part[:, s, c], share[:, s, j:j + 1],
                                                       psP[:, s % products, j, 0:D], ALU.mult, ALU.add)
                i.then_inc(combined, 1)

            def add_rest(g, s, k, back):
                dve.wait_ge(product2, g + 1)
                dve.wait_ge(res_in[s], (k + 1) * 16)
                if back == R:
                    dve.wait_ge(stored[s], k * per_store)
                nc.vector.tensor_tensor(new[:, s, :], psO[:, :], res[:, s, :], ALU.add).then_inc(added, 1)

            def leak(g, s, k, back):
                dve.wait_ge(biased, g + 1)
                nc.vector.scalar_tensor_tensor(h[:, s, :], h[:, s, :], SLOPE, h[:, s, :], ALU.mult, ALU.max
                                               ).then_inc(leaked, 1)
            if norm:
                over_groups(dve, NG, (count, 0), (invert, 2), (degrees, 2), (measure, 0), (centre, 2), (totals, 2),
                            (add_neighbours, 5), (shares, 2), (combine, 5), ring=R)
            else:
                over_groups(dve, NG, (totals, 0), (add_neighbours, 1), (shares, 0), (combine, 1), (leak, 2), (add_rest, 4),
                            ring=R)

        @block.gpsimd
        def _(pool):
            passed = ph.sem("pool_waits_passed")
            pool.wait_ge(bias_set, n_bias - 1)

            def add_bias(g, s, k, back):
                pool.wait_ge(combined, g + 1)
                rows = tiled(h[:, s, :])
                nc.gpsimd.tensor_tensor(rows, rows, bias[:, :].unsqueeze(1).to_broadcast([P, T, D]), ALU.add
                                        ).then_inc(biased, 1)

            def finish(g, s, k, back):
                pool.wait_ge(added, g + 1)
                rows = tiled(new[:, s, :])
                nc.gpsimd.tensor_tensor(rows, rows, BA[:, :].unsqueeze(1).to_broadcast([P, T, D]), ALU.add
                                        ).then_inc(finished, 1)


            def leak(g, s, k, back):
                pool.wait_ge(scaled, g + 1)
                nc.gpsimd.tensor_tensor(h[:, s, :], h[:, s, :], part[:, s, :], ALU.add).then_inc(leaked, 1)
            if last_layer:
                over_groups(pool, NG, (add_bias, 1), (finish, 4), ring=R)
            else:
                over_groups(pool, NG, (add_bias, 0), (leak, 1), ring=R)

        @block.tensor
        def _(pe):
            pe.wait_ge(weights_in, n_weights)

            def turn(g, s, k, back):
                if norm:
                    pe.wait_ge(normed, g + 1)
                else:
                    pe.wait_ge(loaded[s], (k + 1) * 32)
                if back:
                    pe.wait_ge(hT_ready, g)
                for j in range(T):
                    i = pe.transpose(psT[:, j * P:(j + 1) * P], x[:, s, j * D:(j + 1) * D], sh.ident[:, :])
                i.then_inc(turned, 1)

            def multiply(g, s, k, back):
                pe.wait_ge(hT_ready, g + 1)
                if back >= products:
                    pe.wait_ge(combined, g - products + 1)
                for j in range(T):
                    i = pe.matmul(psP[:, s % products, j, :], hT[:, s, j * P:(j + 1) * P], W[:, :], start=True, stop=True)
                i.then_inc(product, 1)

            def turn2(g, s, k, back):
                pe.wait_ge(leaked, g + 1)
                if back:
                    pe.wait_ge(h2T_ready, g)
                for j in range(T):
                    i = pe.transpose(psT2[:, j * P:(j + 1) * P], h[:, s, j * D:(j + 1) * D], sh.ident[:, :])
                i.then_inc(turned2, 1)

            def multiply2(g, s, k, back):
                pe.wait_ge(h2T_ready, g + 1)
                if back:
                    pe.wait_ge(added, g)
                for j in range(T):
                    i = pe.matmul(psO[:, j * D:(j + 1) * D], h2T[:, s, j * P:(j + 1) * P], WA[:, :],
                                  start=True, stop=True)
                i.then_inc(product2, 1)
            over_groups(pe, NG, (multiply, 1), (turn, 0),
                        *([(multiply2, 4), (turn2, 3)] if last_layer else []), ring=R)

        @block.scalar
        def _(act):
            def take_root(g, s, k, back):
                act.wait_ge(measured, g + 1)
                nc.scalar.activation(rstd[:, s, :], mv[:, s, :, 1], ACT.Sqrt, bias=sh.eps[:, :]).then_inc(root_ready, 1)

            def normalise(g, s, k, back):
                act.wait_ge(factors_ready, g + 1)
                for j in range(T):
                    c = slice(j * D, (j + 1) * D)
                    i = nc.scalar.activation(x[:, s, c], x[:, s, c], ACT.Relu, scale=rstd[:, s, j:j + 1],
                                             bias=minus[:, s, j:j + 1])
                i.then_inc(normed, 1)

            def transposed(g, s, k, back):
                act.wait_ge(turned, g + 1)
                if back == R:
                    act.wait_ge(product, g - R + 1)
                nc.scalar.activation(hT[:, s, :], psT[:, :], ACT.Copy).then_inc(hT_ready, 1)

            def split_leaky(g, s, k, back):
                act.wait_ge(biased, g + 1)
                nc.scalar.activation(part[:, s, :], h[:, s, :], ACT.Relu, scale=1 - SLOPE)
                nc.scalar.activation(h[:, s, :], h[:, s, :], ACT.Copy, scale=SLOPE).then_inc(scaled, 1)

            def transposed2(g, s, k, back):
                act.wait_ge(turned2, g + 1)
                if back == R:
                    act.wait_ge(product2, g - R + 1)
                nc.scalar.activation(h2T[:, s, :], psT2[:, :], ACT.Copy).then_inc(h2T_ready, 1)

            def store(g, s, k, back):
                await_overlapped(act, stored, g, per_store)
                if last_layer:
                    act.wait_ge(finished, g + 1)
                    act.dma_start(rows_of(out, g), new[:, s, :]).then_inc(stored[s], 16)
                    act.dma_start(rows_of(copy, g), new[:, s, :]).then_inc(stored[s], 16)
                else:
                    act.wait_ge(leaked, g + 1)
                    act.dma_start(rows_of(out, g), h[:, s, :]).then_inc(stored[s], 16)
            if last_layer:
                over_groups(act, NG, (transposed, 0), (transposed2, 3), (store, 5), ring=R)
            else:
                over_groups(act, NG, (take_root, 0), (split_leaky, 6), (transposed, 3), (normalise, 2), (store, 8), ring=R)
            for s in range(R):
                act.wait_ge(stored[s], per_store * -(-(NG - s) // R))


def gated_nodes(nc, sh, tag, table, acc, wz, wr, wh, bz, br, bh, out, wT, a_source):
    R, H = 8, 4
    with ExitStack() as ctx:
        ph = Phase(sh, tag, ctx)
        W = {n: ph.sb("w" + n, [P, 2, D]) for n in "zrh"}
        B = {n: ph.sb("b" + n, [P, 1]) for n in "zrh"}
        x, hT, new = (ph.sb(n, [P, R, T * D]) for n in ("x", "hT", "new"))
        sums, xn, aT, z, r, t = (ph.sb(n, [P, H, GW]) for n in ("sums", "xn", "aT", "z", "r", "t"))
        psH, psA, psZ, psR, psC, psO = (ph.ps(n, [P, GW]) for n in ("psH", "psA", "psZ", "psR", "psC", "psO"))
        WT, A, spread, U = ph.sb("wT", [P, D]), ph.sb("a", [P, 1]), ph.sb("spread", [P, D]), ph.sb("u", [P, D])
        stats, mv = ph.sb("stats", [P, R, T, 6]), ph.sb("mv", [P, R, T, 2])
        minus, dots = ph.sb("minus_mean", [P, R, T]), ph.sb("dots", [P, R, T])
        above, variance = ph.sb("above_mean", [P, H, T * D]), ph.sb("variance", [P, NG * T])
        psU = ph.ps("psU", [P, D])
        spread_set, u_in, u_set, scores_steps = (ph.sem(n) for n in ("spread_set", "u_in", "u_set", "scores_steps"))
        counted, measured, centred = ph.sem("counted"), ph.sem("measured"), ph.sem("centred")
        above_ready, dotted, noted = ph.sem("above_ready"), ph.sem("dotted"), ph.sem("noted")
        weights_in, spare_cleared = ph.sem("weights_in"), ph.sem("spare_cleared")
        loaded = [ph.sem(f"rows_in{s}") for s in range(R)]
        stored = [ph.sem(f"stored{s}") for s in range(R)]
        normed = ph.sem("rows_normed")
        turned, acc_turned, hT_ready, aT_ready = (ph.sem(n) for n in ("turned", "acc_turned", "hT_ready", "aT_ready"))
        z_in, r_in, z_ready, r_ready = (ph.sem(n) for n in ("z_in", "r_in", "z_ready", "r_ready"))
        reset, cand, cand_ready = (ph.sem(n) for n in ("reset", "candidate", "candidate_ready"))
        mixing, back_turned, added = ph.sem("mixing"), ph.sem("back_turned"), ph.sem("added")

        block = ctx.enter_context(nc.Block())

        @block.sync
        def _(sp):
            for n, w, b in (("z", wz, bz), ("r", wr, br), ("h", wh, bh)):
                sp.dma_start(W[n][:, :, :], w.rearrange("(c p) d -> p c d", p=P)).then_inc(weights_in, 16)
                sp.dma_start(B[n][:, :], b).then_inc(weights_in, 16)
            sp.dma_start(WT[:, :], wT).then_inc(weights_in, 16)
            sp.dma_start(A[:, :], a_source).then_inc(weights_in, 16)
            sp.dma_start(out[N:PAD_ROW, :].rearrange("(p r) d -> p (r d)", p=P), sh.zeros[:, 0:T * D]
                         ).then_inc(spare_cleared, 16)
            sp.dma_start(out[PAD_ROW:PAD_ROW + 1, :], sh.zeros[0:1, 0:D]).then_inc(spare_cleared, 16)

            def load(g, s, k, back):
                if back == R:
                    sp.wait_ge(added, g - R + 1)
                sp.dma_start(x[:, s, :], rows_of(table, g)).then_inc(loaded[s], 16)
                if back >= H:
                    sp.wait_ge(acc_turned, g - H + 1)
                sp.dma_start(sums[:, s % H, :], rows_of(acc, g)).then_inc(loaded[s], 16)
            over_groups(sp, NG, (load, 0), ring=R)
            sp.wait_ge(spare_cleared, 32)

        @block.vector
        def _(dve):
            passed = ph.sem("dve_waits_passed")
            dve.wait_ge(weights_in, 128)
            nc.vector.tensor_copy(spread[:, :], A[:, 0:1].to_broadcast([P, D])).then_inc(spread_set, 1)
            dve.wait_ge(u_in, 1)
            nc.vector.tensor_copy(U[:, :], psU[:, :]).then_inc(u_set, 1)
            dve.wait_ge(u_set, 1)
            def norm_rows(g, s, k, back):
                dve.wait_ge(loaded[s], (k + 1) * 32)
                if back >= H:
                    dve.wait_ge(turned, g - H + 1)
                for j in range(T):
                    c, at = slice(j * D, (j + 1) * D), bass.ds(g * T + j, 1)
                    i = nc.vector.tensor_scalar(xn[:, s % H, c], x[:, s, c], sh.mean[:, at], sh.scale[:, at],
                                                ALU.subtract, ALU.mult)
                i.then_inc(normed, 1)

            def reset_h(g, s, k, back):
                dve.wait_ge(r_ready, g + 1)
                nc.vector.tensor_tensor(r[:, s % H, :], r[:, s % H, :], hT[:, s, :], ALU.mult).then_inc(reset, 1)

            def add(g, s, k, back):
                dve.wait_ge(back_turned, g + 1)
                if back == R:
                    dve.wait_ge(stored[s], k * 16)
                    dve.wait_ge(above_ready, g - R + 1)
                nc.vector.tensor_tensor(new[:, s, :], psO[:, :], x[:, s, :], ALU.add).then_inc(added, 1)

            def count(g, s, k, back):
                dve.wait_ge(added, g + 1)
                if back == R:
                    dve.wait_ge(measured, g - R + 1)
                for j in range(T):
                    i = nc.vector.bn_stats(stats[:, s, j, :], new[:, s, j * D:(j + 1) * D])
                i.then_inc(counted, 1)

            def measure(g, s, k, back):
                if back == R:
                    dve.wait_ge(centred, 2 * (g - R + 1))
                wait_apart(dve, counted, g + 1, passed)
                for j in range(T):
                    i = nc.vector.bn_aggr(mv[:, s, j, :], stats[:, s, j, :])
                i.then_inc(measured, 1)

            def centre(g, s, k, back):
                dve.wait_ge(measured, g + 1)
                if back == R:
                    dve.wait_ge(above_ready, g - R + 1)
                nc.vector.tensor_scalar(minus[:, s, :], mv[:, s, :, 0], -1.0, None, ALU.mult).then_inc(centred, 1)
                nc.vector.tensor_copy(variance[:, bass.ds(g * T, T)], mv[:, s, :, 1]).then_inc(centred, 1)

            def dot(g, s, k, back):
                dve.wait_ge(above_ready, g + 1)
                if back == R:
                    dve.wait_ge(noted, g - R + 1)
                for j in range(T):
                    i = nc.vector.scalar_tensor_tensor(sh.junk[:, j, 0:D], above[:, s % H, j * D:(j + 1) * D], 1.0, U[:, :],
                                                       ALU.mult, ALU.mult, accum_out=dots[:, s, j:j + 1])
                i.then_inc(dotted, 1)

            def note(g, s, k, back):
                dve.wait_ge(dotted, g + 1)
                nc.vector.tensor_copy(sh.score[:, bass.ds(g * T, T)], dots[:, s, :]).then_inc(noted, 1)
            over_groups(dve, NG, (norm_rows, 0), (add, 5), (reset_h, 1), (count, 6), (centre, 7), (note, 10), (dot, 9),
                        (measure, 6), ring=R)
            dve.wait_ge(noted, NG)
            dve.wait_ge(scores_steps, 1)
            nc.vector.reciprocal(variance[:, :], variance[:, :]).then_inc(scores_steps, 1)
            dve.wait_ge(scores_steps, 2)
            nc.vector.tensor_tensor(sh.score[:, :], sh.score[:, :], variance[:, :], ALU.mult).then_inc(scores_steps, 1)
            dve.wait_ge(scores_steps, 3)

        @block.gpsimd
        def _(pool):
            passed = ph.sem("pool_waits_passed")
            def mix(g, s, k, back):
                pool.wait_ge(cand_ready, g + 1)
                pool.wait_ge(z_ready, g + 1)
                nc.gpsimd.tensor_tensor(t[:, s % H, :], t[:, s % H, :], hT[:, s, :], ALU.subtract).then_inc(mixing, 1)
                pool.wait_ge(mixing, g * 3 + 1)
                nc.gpsimd.tensor_tensor(t[:, s % H, :], t[:, s % H, :], z[:, s % H, :], ALU.mult).then_inc(mixing, 1)
                pool.wait_ge(mixing, g * 3 + 2)
                nc.gpsimd.tensor_tensor(t[:, s % H, :], t[:, s % H, :], hT[:, s, :], ALU.add).then_inc(mixing, 1)
            over_groups(pool, NG, (mix, 0), ring=R)

        @block.tensor
        def _(pe):
            pe.wait_ge(weights_in, 128)
            pe.wait_ge(spread_set, 1)
            pe.matmul(psU[:, :], spread[:, :], WT[:, :], start=True, stop=True).then_inc(u_in, 1)

            def turn(g, s, k, back):
                pe.wait_ge(loaded[s], (k + 1) * 32)
                if back:
                    pe.wait_ge(aT_ready, g)
                for j in range(T):
                    i = pe.transpose(psA[:, j * P:(j + 1) * P], sums[:, s % H, j * D:(j + 1) * D], sh.ident[:, :])
                i.then_inc(acc_turned, 1)
                pe.wait_ge(normed, g + 1)
                if back:
                    pe.wait_ge(hT_ready, g)
                for j in range(T):
                    i = pe.transpose(psH[:, j * P:(j + 1) * P], xn[:, s % H, j * D:(j + 1) * D], sh.ident[:, :])
                i.then_inc(turned, 1)

            def gates(g, s, k, back):
                pe.wait_ge(hT_ready, g + 1)
                pe.wait_ge(aT_ready, g + 1)
                for n, ps, read, done in (("r", psR, r_ready, r_in), ("z", psZ, z_ready, z_in)):
                    if back:
                        pe.wait_ge(read, g)
                    pe.matmul(ps[:, :], W[n][:, 0, :], hT[:, s, :], start=True, stop=False)
                    pe.matmul(ps[:, :], W[n][:, 1, :], aT[:, s % H, :], start=False, stop=True).then_inc(done, 1)

            def candidate(g, s, k, back):
                pe.wait_ge(reset, g + 1)
                if back:
                    pe.wait_ge(cand_ready, g)
                pe.matmul(psC[:, :], W["h"][:, 1, :], aT[:, s % H, :], start=True, stop=False)
                pe.matmul(psC[:, :], W["h"][:, 0, :], r[:, s % H, :], start=False, stop=True).then_inc(cand, 1)

            def turn_back(g, s, k, back):
                pe.wait_ge(mixing, (g + 1) * 3)
                if back:
                    pe.wait_ge(added, g)
                for j in range(T):
                    i = pe.transpose(psO[:, j * D:(j + 1) * D], t[:, s % H, j * P:(j + 1) * P], sh.ident[:, :])
                i.then_inc(back_turned, 1)
            over_groups(pe, NG, (gates, 1), (turn, 0), (candidate, 2), (turn_back, 4), ring=R)

        @block.scalar
        def _(act):
            act.wait_ge(weights_in, 128)

            def transposed(g, s, k, back):
                act.wait_ge(acc_turned, g + 1)
                if back >= H:
                    act.wait_ge(cand, g - H + 1)
                if back == R:
                    act.wait_ge(mixing, (g - R + 1) * 3)
                nc.scalar.activation(aT[:, s % H, :], psA[:, :], ACT.Copy).then_inc(aT_ready, 1)
                act.wait_ge(turned, g + 1)
                nc.scalar.activation(hT[:, s, :], psH[:, :], ACT.Relu).then_inc(hT_ready, 1)

            def squash(g, s, k, back):
                act.wait_ge(r_in, g + 1)
                if back >= H:
                    act.wait_ge(cand, g - H + 1)
                    act.wait_ge(mixing, (g - H + 1) * 3)
                nc.scalar.activation(r[:, s % H, :], psR[:, :], ACT.Sigmoid, bias=B["r"][:, :]).then_inc(r_ready, 1)
                act.wait_ge(z_in, g + 1)
                nc.scalar.activation(z[:, s % H, :], psZ[:, :], ACT.Sigmoid, bias=B["z"][:, :]).then_inc(z_ready, 1)

            def bend(g, s, k, back):
                act.wait_ge(cand, g + 1)
                if back >= H:
                    act.wait_ge(back_turned, g - H + 1)
                nc.scalar.activation(t[:, s % H, :], psC[:, :], ACT.Tanh, bias=B["h"][:, :]).then_inc(cand_ready, 1)

            def above_mean(g, s, k, back):
                act.wait_ge(centred, 2 * g + 1)
                if back >= H:
                    act.wait_ge(dotted, g - H + 1)
                for j in range(T):
                    c = slice(j * D, (j + 1) * D)
                    i = nc.scalar.activation(above[:, s % H, c], new[:, s, c], ACT.Relu, bias=minus[:, s, j:j + 1])
                i.then_inc(above_ready, 1)

            def store(g, s, k, back):
                await_overlapped(act, stored, g)
                act.wait_ge(added, g + 1)
                act.dma_start(rows_of(out, g), new[:, s, :]).then_inc(stored[s], 16)
            over_groups(act, NG, (transposed, 0), (squash, 1), (bend, 2), (store, 6), (above_mean, 8), ring=R)
            act.wait_ge(centred, 2 * NG)
            nc.scalar.activation(variance[:, :], variance[:, :], ACT.Sqrt, bias=sh.eps[:, :]).then_inc(scores_steps, 1)
            for s in range(R):
                act.wait_ge(stored[s], 16 * -(-(NG - s) // R))


def attend(nc, sh, tag, table, w, wT, a_dst, sources, ends, src_rows, outside):
    with ExitStack() as ctx:
        keep = Phase(sh, tag, ctx)
        values = keep.sb("values", [P, EG, T * D])
        logit = keep.sb("logit", [P, EG * T])
        weight = keep.sb("weight", [P, EG * T])

        with ExitStack() as inner:
            ph = Phase(sh, tag, inner)
            W, WT, A = ph.sb("w", [P, D + 1]), ph.sb("wT", [P, D]), ph.sb("a", [P, 1])
            end = ph.sb("ends", [P, R, T], I32)
            x, hT = ph.sb("x", [P, R, T, D]), ph.sb("hT", [P, 2, GW])
            stats, mv = ph.sb("stats", [P, R, T, 6]), ph.sb("mv", [P, R, T, 2])
            rstd, minus = ph.sb("rstd", [P, R, T]), ph.sb("minus_mean", [P, R, T])
            psT, psM = ph.ps("psT", [P, GW]), ph.ps("psM", [P, 2, GW])
            product_rows = psM[:, :, 0:2 * (D + 1)].rearrange("p q (j d) -> p q j d", j=2)
            find = Lookup(ph, sh, sh.score, sources)
            weights_in, column_in, column_set = ph.sem("weights_in"), ph.sem("column_in"), ph.sem("column_set")
            ends_in = [ph.sem(f"ends_in{s}") for s in range(R)]
            gathered = [ph.sem(f"rows_gathered{s}") for s in range(R)]
            counted, measured, root_ready = ph.sem("counted"), ph.sem("rows_measured"), ph.sem("root_ready")
            inverted, factors_ready, normed = ph.sem("inverted"), ph.sem("factors_ready"), ph.sem("rows_normed")
            turned, hT_ready, product = ph.sem("rows_turned"), ph.sem("hT_ready"), ph.sem("product")
            values_ready, scores_kept, logits_set = ph.sem("values_ready"), ph.sem("scores_kept"), ph.sem("logits_set")

            block = inner.enter_context(nc.Block())

            @block.sync
            def _(sp):
                sp.dma_start(W[:, 0:D], w).then_inc(weights_in, 16)
                sp.dma_start(WT[:, :], wT).then_inc(weights_in, 16)
                sp.dma_start(A[:, :], a_dst).then_inc(weights_in, 16)
                find.load(sp)

                def load(g, s, k, back):
                    if back == R:
                        sp.wait_ge(gathered[s], k * 64)
                    sp.dma_start(end[:, s, :], ends[g, :, DST:DST + T]).then_inc(ends_in[s], 16)
                over_groups(sp, EG, (load, 0))

            @block.gpsimd
            def _(pool):
                passed = ph.sem("pool_waits_passed")

                def gather(g, s, k, back):
                    pool.wait_ge(ends_in[s], (k + 1) * 16)
                    if back == R:
                        wait_apart(pool, turned, g - R + 1, passed)
                    for j in range(T):
                        at = bass.IndirectOffsetOnAxis(ap=end[:, s, j:j + 1], axis=0)
                        pool.indirect_dma_start(x[:, s, j, :], None, table, at).then_inc(gathered[s], 16)
                over_groups(pool, EG, (gather, 0))

            @block.vector
            def _(dve):
                passed = ph.sem("dve_waits_passed")
                dve.wait_ge(weights_in, 48)
                dve.wait_ge(column_in, 1)
                nc.vector.tensor_copy(W[:, D:D + 1], psT[:, 0:1]).then_inc(column_set, 1)
                find.place(nc, dve)

                def count(g, s, k, back):
                    dve.wait_ge(gathered[s], (k + 1) * 64)
                    if back == R:
                        dve.wait_ge(measured, g - R + 1)
                    for j in range(T):
                        i = nc.vector.bn_stats(stats[:, s, j, :], x[:, s, j, :])
                    i.then_inc(counted, 1)

                def measure(g, s, k, back):
                    wait_apart(dve, counted, g + 1, passed)
                    for j in range(T):
                        i = nc.vector.bn_aggr(mv[:, s, j, :], stats[:, s, j, :])
                    i.then_inc(measured, 1)

                def invert(g, s, k, back):
                    dve.wait_ge(root_ready, g + 1)
                    nc.vector.reciprocal(rstd[:, s, :], rstd[:, s, :]).then_inc(inverted, 1)

                def centre(g, s, k, back):
                    dve.wait_ge(inverted, g + 1)
                    nc.vector.scalar_tensor_tensor(minus[:, s, :], mv[:, s, :, 0], -1.0, rstd[:, s, :],
                                                   ALU.mult, ALU.mult).then_inc(factors_ready, 1)
                choose, mark, note = find.vector_parts(nc, dve)
                over_groups(dve, EG, (invert, 1), mark, (centre, 1), choose, (count, 0), note, (measure, 0))
                dve.wait_ge(find.noted, EG)
                dve.wait_ge(scores_kept, EG)
                nc.vector.tensor_tensor(logit[:, :], logit[:, :], find.result[:, :], ALU.add).then_inc(logits_set, 1)
                dve.wait_ge(logits_set, 1)

            @block.tensor
            def _(pe):
                pe.wait_ge(weights_in, 48)
                pe.matmul(psT[:, 0:1], WT[:, :], A[:, :], start=True, stop=True).then_inc(column_in, 1)
                pe.wait_ge(column_set, 1)

                def turn(g, s, k, back):
                    pe.wait_ge(normed, g + 1)
                    if back:
                        pe.wait_ge(hT_ready, g)
                    for j in range(T):
                        i = pe.transpose(psT[:, j * P:(j + 1) * P], x[:, s, j, :], sh.ident[:, :])
                    i.then_inc(turned, 1)

                def multiply(g, s, k, back):
                    pe.wait_ge(hT_ready, g + 1)
                    if back:
                        pe.wait_ge(values_ready, g)
                        pe.wait_ge(scores_kept, g)
                    for j in range(T):
                        i = pe.matmul(product_rows[:, j // 2, j % 2, :], hT[:, s % 2, j * P:(j + 1) * P], W[:, :],
                                      start=True, stop=True)
                    i.then_inc(product, 1)
                look, turn_marks = find.tensor_parts(pe)
                over_groups(pe, EG, look, (multiply, 2), turn_marks, (turn, 1))

            @block.scalar
            def _(act):
                def take_root(g, s, k, back):
                    act.wait_ge(measured, g + 1)
                    nc.scalar.activation(rstd[:, s, :], mv[:, s, :, 1], ACT.Sqrt, bias=sh.eps[:, :]).then_inc(root_ready, 1)

                def normalise(g, s, k, back):
                    act.wait_ge(factors_ready, g + 1)
                    for j in range(T):
                        i = nc.scalar.activation(x[:, s, j, :], x[:, s, j, :], ACT.Relu, scale=rstd[:, s, j:j + 1],
                                                 bias=minus[:, s, j:j + 1])
                    i.then_inc(normed, 1)

                def transposed(g, s, k, back):
                    act.wait_ge(turned, g + 1)
                    if back >= 2:
                        act.wait_ge(product, g - 1)
                    nc.scalar.activation(hT[:, s % 2, :], psT[:, :], ACT.Copy).then_inc(hT_ready, 1)

                def keep_values(g, s, k, back):
                    act.wait_ge(product, g + 1)
                    nc.scalar.activation(logit[:, bass.ds(g * T, T)].rearrange("p (q j) -> p q j", q=2),
                                         product_rows[:, :, :, D], ACT.Copy).then_inc(scores_kept, 1)
                    nc.scalar.activation(values[:, bass.ds(g, 1), :].rearrange("p o (q j d) -> p (o q) j d", q=2, j=2),
                                         product_rows[:, :, :, 0:D], ACT.Copy).then_inc(values_ready, 1)
                over_groups(act, EG, (normalise, 1), (take_root, 0), (keep_values, 3), (transposed, 2),
                            *find.scalar_parts(nc, act))

        with ExitStack() as inner:
            ph = Phase(sh, tag + "softmax_", inner)
            pad = ph.sb("outside", [P, EG * T])
            top, all_top, minus, total, all_total, inverse = (ph.sb(n, [P, 1]) for n in (
                "top", "all_top", "minus_top", "total", "all_total", "inverse"))
            pad_in, steps = ph.sem("outside_in"), ph.sem("steps")
            block = inner.enter_context(nc.Block())

            @block.sync
            def _(sp):
                sp.dma_start(pad[:, :], outside).then_inc(pad_in, 16)

            @block.vector
            def _(dve):
                passed = ph.sem("dve_waits_passed")
                dve.wait_ge(pad_in, 16)
                nc.vector.tensor_tensor(logit[:, :], logit[:, :], pad[:, :], ALU.add).then_inc(steps, 1)
                dve.wait_ge(steps, 1)
                nc.vector.reduce_max(top[:, :], logit[:, :], AX_X).then_inc(steps, 1)
                dve.wait_ge(steps, 5)
                nc.vector.reciprocal(inverse[:, :], all_total[:, :]).then_inc(steps, 1)
                dve.wait_ge(steps, 6)
                nc.vector.tensor_scalar(weight[:, :], weight[:, :], inverse[:, 0:1], None, ALU.mult).then_inc(steps, 1)
                dve.wait_ge(steps, 7)

            @block.gpsimd
            def _(pool):
                passed = ph.sem("pool_waits_passed")
                pool.wait_ge(steps, 2)
                nc.gpsimd.partition_all_reduce(all_top[:, :], top[:, :], P, RMAX).then_inc(steps, 1)
                pool.wait_ge(steps, 4)
                nc.gpsimd.partition_all_reduce(all_total[:, :], total[:, :], P, RADD).then_inc(steps, 1)

            @block.scalar
            def _(act):
                minus_set = ph.sem("minus_set")
                act.wait_ge(steps, 3)
                nc.scalar.mul(minus[:, :], all_top[:, :], -1.0).then_inc(minus_set, 1)
                act.wait_ge(minus_set, 1)
                nc.scalar.activation(weight[:, :], logit[:, :], ACT.Exp, bias=minus[:, :], accum_out=total[:, :]
                                     ).then_inc(steps, 1)

        with ExitStack() as inner:
            ph = Phase(sh, tag + "sum_", inner)
            key, row = ph.sb("keys", [P, R, T], I32), ph.sb("key_row", [P, R, GW], I32)
            msg, sums = ph.sb("msg", [P, R, T, D]), ph.sb("sums", [P, R, T, D])
            eq = ph.sb("eq", [P, 2, block_at(T, T)])
            keyf, count, way = ph.sb("keyf", [P, R, T]), ph.sb("count", [P, T]), ph.sb("way", [P, R, T])
            to = ph.sb("to", [P, R, T], I32)
            psS = ph.ps("psS", [P, 2, GW])
            loaded = [ph.sem(f"keys_in{s}") for s in range(R)]
            united, msg_ready, summed = ph.sem("unite_steps"), ph.sem("msg_ready"), ph.sem("summed")
            sums_ready, landed = ph.sem("sums_ready"), ph.sem("scatters_landed")
            block = inner.enter_context(nc.Block())

            @block.sync
            def _(sp):
                def load(g, s, k, back):
                    if back == R:
                        sp.wait_ge(msg_ready, 2 * (g - R + 1))
                    sp.dma_start(key[:, s, :], ends[g, :, SRC_KEY:SRC_KEY + T]).then_inc(loaded[s], 16)
                    sp.dma_start(row[:, s, :], src_rows[bass.ds(g, 1), :].to_broadcast([P, GW])).then_inc(loaded[s], 16)
                over_groups(sp, EG, (load, 0))

            @block.vector
            def _(dve):
                passed = ph.sem("dve_waits_passed")
                unites = Chain(dve, united, UNITE_STEPS, passed)

                def unite_edges(g, s, k, back):
                    unites.start(g)
                    dve.wait_ge(loaded[s], (k + 1) * 32)
                    if back >= 2:
                        dve.wait_ge(summed, g - 1)
                    unite(nc, sh, unites, T, eq[:, s % 2], row[:, s], key[:, s], keyf[:, s], count, way[:, s])

                def messages(g, s, k, back):
                    if back == R:
                        dve.wait_ge(landed, (g - R + 1) * 64)
                    nc.vector.tensor_tensor(to[:, s, :], way[:, s, :], keyf[:, s, :], ALU.add).then_inc(msg_ready, 1)
                    for j in range(T):
                        i = nc.vector.tensor_scalar(msg[:, s, j, :], values[:, bass.ds(g, 1), j * D:(j + 1) * D].rearrange("p o d -> p (o d)"),
                                                    weight[:, bass.ds(g * T + j, 1)], None, ALU.mult)
                    i.then_inc(msg_ready, 1)
                over_groups(dve, EG, (unite_edges, 0), (messages, 0))

            @block.tensor
            def _(pe):
                def add_up(g, s, k, back):
                    pe.wait_ge(msg_ready, 2 * (g + 1))
                    if back >= 2:
                        pe.wait_ge(sums_ready, g - 1)
                    batch_sums(pe, T, lambda j: psS[:, s % 2, j * D:(j + 1) * D], eq[:, s % 2], msg[:, s], D
                               ).then_inc(summed, 1)
                over_groups(pe, EG, (add_up, 0))

            @block.scalar
            def _(act):
                def sums_out(g, s, k, back):
                    act.wait_ge(summed, g + 1)
                    if back == R:
                        act.wait_ge(landed, (g - R + 1) * 64)
                    nc.scalar.activation(sums[:, s, :, :].rearrange("p j d -> p (j d)"), psS[:, s % 2, :], ACT.Copy
                                         ).then_inc(sums_ready, 1)
                over_groups(act, EG, (sums_out, 0))

            @block.gpsimd
            def _(pool):
                passed = ph.sem("pool_waits_passed")
                def scatter(g, s, k, back):
                    pool.wait_ge(sums_ready, g + 1)
                    wait_apart(pool, msg_ready, 2 * (g + 1), passed)
                    if back:
                        wait_apart(pool, landed, g * 64, passed)
                    for j in range(T):
                        at = bass.IndirectOffsetOnAxis(ap=to[:, s, j:j + 1], axis=0)
                        pool.indirect_dma_start(table, at, sums[:, s, j, :], None, compute_op=ALU.add
                                                ).then_inc(landed, 16)
                over_groups(pool, EG, (scatter, 0))
                pool.wait_ge(landed, EG * 64)


def dram(nc, name, rows, w=D):
    return nc.dram_tensor(name, (rows, w), F32, kind="Internal").ap()


def gnn_stack(nc, a, out):
    h1, x1, x2 = dram(nc, "h1", N), dram(nc, "x1", N), dram(nc, "x2", PAD_ROW + 1)
    acc1 = dram(nc, "acc1", ROWS, CW)
    acc2, acc4 = dram(nc, "acc2", ROWS), dram(nc, "acc4", ROWS)
    x, ends, dst_rows, ew = a["x"], a["ends"], a["dst_rows"], a["edge_factor"]
    with ExitStack() as ctx:
        sh = Shared(nc, ctx)
        load_constants(nc, sh, a["ident"], a["before"], a["spare"], a["counting"])
        linear_edges(nc, sh, "edges1_", x, acc1, CW, a["gcn_w"][0, :, D:2 * D], ends, dst_rows, scale=ew, norm=True,
                     clear_first=True, clear_next=acc2)
        gcn_nodes(nc, sh, "nodes1_", x, acc1, CW, a["gcn_w"][0], a["gcn_b"][0], h1, norm=True)
        linear_edges(nc, sh, "edges2_", h1, acc2, D, a["gcn_w"][1, :, D:2 * D], ends, dst_rows, scale=ew, clear_next=acc4,
                     find_share=a["dst_by_tile"])
        gcn_nodes(nc, sh, "nodes2_", h1, acc2, D, a["gcn_w"][1], a["gcn_b"][1], x1,
                  last_layer=(x, a["agg_wT"], a["agg_b"]), copy=x2)
        linear_edges(nc, sh, "edges3_", x1, x2, D, a["mean_wT"], ends, dst_rows, norm=True, bias=a["mean_b"], share=True)
        mlp_edges(nc, sh, "edges4_", x2, acc4, a["w_msg1"], a["b_msg1"], a["w_msg2"], a["b_msg2"], ends, dst_rows,
                  a["attrT"])
        gated_nodes(nc, sh, "nodes4_", x2, acc4, a["w_z"], a["w_r"], a["w_h"], a["b_z"], a["b_r"], a["b_h"], out,
                    a["att_wT"], a["att_a_src"])
        attend(nc, sh, "attend_", out, a["att_w"], a["att_wT"], a["att_a_dst"], a["src_by_tile"], ends, a["src_rows"], a["outside"])


def kernel(x, src, dst, edge_attr_4, edge_weight, L0_gnn_W_self, L0_gnn_b_self, L0_gnn_W_neigh, L0_gnn_b_neigh,
           L0_gnn_layer_bias, L0_gnn_W_agg, L0_gnn_b_agg, L1_gnn_W, L1_gnn_b, L2_gnn_W_msg1, L2_gnn_b_msg1,
           L2_gnn_W_msg2, L2_gnn_b_msg2, L2_gnn_W_z, L2_gnn_b_z, L2_gnn_W_r, L2_gnn_b_r, L2_gnn_W_h, L2_gnn_b_h,
           L3_gnn_W, L3_gnn_a):
    import numpy as np
    import concourse.bacc as bacc
    from concourse.bass_utils import run_bass_kernel_spmd

    def padded(v, fill):
        return np.concatenate([np.asarray(v), np.full((EG * GW - E,) + v.shape[1:], fill, v.dtype)])

    def by_tile(v):
        return v.reshape(EG, T, P).transpose(0, 2, 1)

    src_key, dst_key = padded(src, PAD_ROW), padded(dst, PAD_ROW)
    position = np.arange(EG * GW).reshape(EG * T, P).T
    arrays = {
        "x": x,
        "ends": np.concatenate([by_tile(v) for v in (padded(src, 0), padded(dst, 0), dst_key, src_key)], 2),
        "dst_rows": dst_key.reshape(EG, GW),
        "src_rows": src_key.reshape(EG, GW),
        "edge_factor": by_tile(padded(edge_weight, 0)),
        "attrT": padded(edge_attr_4, 0).T,
        "ident": np.eye(P, dtype=np.float32),
        "before": np.concatenate([np.ones((P, 3 * P)), np.tril(np.ones((P, P)), -1)], 1).astype(np.float32),
        "spare": (N + np.arange(GW).reshape(T, P).T).astype(np.float32),
        "dst_by_tile": dst_key.reshape(EG * T, P).T, "src_by_tile": src_key.reshape(EG * T, P).T,
        "counting": np.arange(NG * T, dtype=np.float32).reshape(1, NG * T),
        "outside": np.where(position < E, 0.0, OUTSIDE).astype(np.float32),
        "gcn_w": np.concatenate([np.transpose(L0_gnn_W_self, (0, 2, 1)), np.transpose(L0_gnn_W_neigh, (0, 2, 1))], 2),
        "gcn_b": np.stack([L0_gnn_b_self, L0_gnn_b_neigh, L0_gnn_layer_bias], 1),
        "agg_wT": np.transpose(L0_gnn_W_agg), "agg_b": np.reshape(L0_gnn_b_agg, (1, D)),
        "mean_wT": np.transpose(L1_gnn_W), "mean_b": np.reshape(L1_gnn_b, (1, D)),
        "w_msg1": L2_gnn_W_msg1, "b_msg1": np.reshape(L2_gnn_b_msg1, (D, 1)),
        "w_msg2": L2_gnn_W_msg2, "b_msg2": np.reshape(L2_gnn_b_msg2, (1, D)),
        "w_z": L2_gnn_W_z, "b_z": np.reshape(L2_gnn_b_z, (D, 1)),
        "w_r": L2_gnn_W_r, "b_r": np.reshape(L2_gnn_b_r, (D, 1)),
        "w_h": L2_gnn_W_h, "b_h": np.reshape(L2_gnn_b_h, (D, 1)),
        "att_w": L3_gnn_W, "att_wT": np.transpose(L3_gnn_W),
        "att_a_src": np.reshape(L3_gnn_a[:D], (D, 1)), "att_a_dst": np.reshape(L3_gnn_a[D:], (D, 1)),
    }
    nc = bacc.Bacc("TRN2", target_bir_lowering=False, num_devices=1)
    given, aps = {}, {}
    for name, v in arrays.items():
        v = np.ascontiguousarray(v)
        given[f"in_{name}"] = v
        aps[name] = nc.dram_tensor(f"in_{name}", v.shape, mybir.dt.from_np(v.dtype), kind="ExternalInput").ap()
    out = nc.dram_tensor("out", (PAD_ROW + 1, D), F32, kind="ExternalOutput").ap()
    gnn_stack(nc, aps, out)
    result = run_bass_kernel_spmd(nc, [given], core_ids=[0])
    return result.results[0]["out"][0:N]
```
